# Optimizing a Trainium2 kernel written in Bass

```python
import numpy as np
import jax
import jax.numpy as jnp

def _softmax(x, axis=-1):
    return jax.nn.softmax(x, axis=axis)

def _gelu(x):
    return jax.nn.gelu(x, approximate=True)

def _silu(x):
    return jax.nn.silu(x)

def _sigmoid(x):
    return jax.nn.sigmoid(x)

def _layernorm(x, axis=-1, eps=1e-05):
    m = jnp.mean(x, axis=axis, keepdims=True)
    v = jnp.var(x, axis=axis, keepdims=True)
    return (x - m) / jnp.sqrt(v + eps)

def _scatter_add(tgt, idx, src, axis=0):
    return tgt.at[idx].add(src)

def _segment_sum(src, seg, n):
    return jax.ops.segment_sum(src, seg, n)
kernel_name = 'mk_macaron_d2_jaxref_r8_b60e42'

def setup_inputs(seed: int=0):
    np.random.seed(seed)
    _w = jnp.asarray

    def _L0_attn_setup():
        import jax, jax.numpy as jnp
        import numpy as np
        DIM = 128
        DEPTH = 6
        LN_EPS = 1e-05

        def _layernorm(x, gamma, beta):
            mu = jnp.mean(x, axis=-1, keepdims=True)
            var = jnp.mean(jnp.square(x - mu), axis=-1, keepdims=True)
            return (x - mu) * jax.lax.rsqrt(var + LN_EPS) * gamma + beta
        key = jax.random.key(seed)
        ks = jax.random.split(key, 6)
        b, n, d = (4, 256, DIM)
        x = jax.random.normal(ks[0], (b, n, d), dtype=jnp.float32)
        w_qkv = jax.random.normal(ks[1], (DEPTH, d, 3 * d), dtype=jnp.float32) * 0.02
        w_out = jax.random.normal(ks[2], (DEPTH, d, d), dtype=jnp.float32) * 0.02
        b_out = jnp.zeros((DEPTH, d), dtype=jnp.float32)
        gamma = jnp.ones((DEPTH, d), dtype=jnp.float32)
        beta = jnp.zeros((DEPTH, d), dtype=jnp.float32)
        return {'x': x, 'w_qkv': w_qkv, 'w_out': w_out, 'b_out': b_out, 'gamma': gamma, 'beta': beta}
    _L0_attn_in = _L0_attn_setup()

    def _L0_ffn_setup():
        import jax, jax.numpy as jnp
        import numpy as np
        B, S, H, I, E = (2, 512, 128, 64, 8)
        key = jax.random.key(seed)
        ks = jax.random.split(key, 5)
        scale_h = 1.0 / np.sqrt(H)
        scale_i = 1.0 / np.sqrt(I)
        return {'hidden_states': jax.random.normal(ks[0], (B, S, H), dtype=jnp.float32), 'gate_w': jax.random.normal(ks[1], (E, H), dtype=jnp.float32) * scale_h, 'w_gate': jax.random.normal(ks[2], (E, I, H), dtype=jnp.float32) * scale_h, 'w_up': jax.random.normal(ks[3], (E, I, H), dtype=jnp.float32) * scale_h, 'w_down': jax.random.normal(ks[4], (E, H, I), dtype=jnp.float32) * scale_i}
    _L0_ffn_in = _L0_ffn_setup()

    def _L1_attn_setup():
        import jax, jax.numpy as jnp
        import numpy as np
        D_MODEL = 128
        D_STATE = 16
        D_CONV = 4
        EXPAND = 2
        D_INNER = EXPAND * D_MODEL
        DT_RANK = D_INNER // 16
        BATCH = 2
        SEQLEN = 128

        def _silu(x):
            return x * jax.nn.sigmoid(x)
        key = jax.random.key(seed)
        ks = jax.random.split(key, 8)
        s = 0.02
        A_init = jnp.tile(jnp.arange(1, D_STATE + 1, dtype=jnp.float32)[None, :], (D_INNER, 1))
        return {'x': jax.random.normal(ks[0], (BATCH, SEQLEN, D_MODEL), jnp.float32), 'W_in': jax.random.normal(ks[1], (D_MODEL, 2 * D_INNER), jnp.float32) * s, 'conv_k': jax.random.normal(ks[2], (D_CONV, 1, D_INNER), jnp.float32) * s, 'conv_b': jnp.zeros((D_INNER,), jnp.float32), 'W_xproj': jax.random.normal(ks[3], (D_INNER, DT_RANK + 2 * D_STATE), jnp.float32) * s, 'W_dt': jax.random.normal(ks[4], (DT_RANK, D_INNER), jnp.float32) * s, 'b_dt': jnp.zeros((D_INNER,), jnp.float32), 'A_log': jnp.log(A_init), 'D': jnp.ones((D_INNER,), jnp.float32), 'W_out': jax.random.normal(ks[5], (D_INNER, D_MODEL), jnp.float32) * s}
    _L1_attn_in = _L1_attn_setup()

    def _L1_ffn_setup():
        import jax, jax.numpy as jnp
        import numpy as np
        DIM = 128
        DEPTH = 2
        HEADS = 8
        DIM_HEAD = 64
        WINDOW = 64
        INNER = HEADS * DIM_HEAD
        HID = int(DIM * 4 * 2 / 3)
        B, N = (2, 1024)
        QK_SCALE = 8.0

        def shift_token(t):
            t1, t2 = jnp.split(t, 2, axis=-1)
            t2 = jnp.pad(t2, ((0, 0), (1, 0), (0, 0)))[:, :-1]
            return jnp.concatenate([t1, t2], axis=-1)

        def l2norm(t):
            return t / jnp.clip(jnp.linalg.norm(t, axis=-1, keepdims=True), 1e-12)

        def rotate_half(x):
            x1, x2 = jnp.split(x, 2, axis=-1)
            return jnp.concatenate([-x2, x1], axis=-1)

        def rotary_xpos(q, k):
            n = q.shape[-2]
            half_idx = jnp.arange(0, DIM_HEAD, 2, dtype=jnp.float32)
            inv_freq = 1.0 / 10000.0 ** (half_idx / DIM_HEAD)
            t = jnp.arange(n, dtype=jnp.float32)
            freqs = t[:, None] * inv_freq[None, :]
            freqs = jnp.concatenate([freqs, freqs], axis=-1)
            base = (half_idx + 0.4 * DIM_HEAD) / (1.4 * DIM_HEAD)
            power = (t - n // 2) / float(WINDOW // 2)
            scale = base[None, :] ** power[:, None]
            scale = jnp.concatenate([scale, scale], axis=-1)
            cos, sin = (jnp.cos(freqs), jnp.sin(freqs))
            q = q * cos * scale + rotate_half(q) * sin * scale
            k = k * cos / scale + rotate_half(k) * sin / scale
            return (q, k)

        def local_attention(q, k, v):
            b, h, n, d = q.shape
            w = n // WINDOW
            bq = q.reshape(b, h, w, WINDOW, d) * QK_SCALE
            bk = k.reshape(b, h, w, WINDOW, d)
            bv = v.reshape(b, h, w, WINDOW, d)

            def look_around(t):
                p = jnp.pad(t, ((0, 0), (0, 0), (1, 0), (0, 0), (0, 0)))
                return jnp.concatenate([p[:, :, :w], p[:, :, 1:]], axis=3)
            bk, bv = (look_around(bk), look_around(bv))
            bt = jnp.arange(n).reshape(w, WINDOW)
            btp = jnp.pad(bt, ((1, 0), (0, 0)), constant_values=-1)
            btk = jnp.concatenate([btp[:w], btp[1:]], axis=1)
            sim = jnp.einsum('bhwid,bhwjd->bhwij', bq, bk)
            i = bt[:, :, None]
            j = btk[:, None, :]
            mask = (i < j) | (i > j + WINDOW) | (j == -1)
            sim = jnp.where(mask, -jnp.finfo(sim.dtype).max, sim)
            attn = jax.nn.softmax(sim, axis=-1)
            out = jnp.einsum('bhwij,bhwjd->bhwid', attn, bv)
            return out.reshape(b, h, n, d)

        def _layer(x, wqkv, qs, ksc, wo, lg, lb, w1, b1, w2, b2):
            b, n, _ = x.shape
            h = shift_token(x)
            qkv = h @ wqkv
            q, k, v = jnp.split(qkv, 3, axis=-1)
            to_heads = lambda t: t.reshape(b, n, HEADS, DIM_HEAD).transpose(0, 2, 1, 3)
            q, k, v = (to_heads(q), to_heads(k), to_heads(v))
            q = l2norm(q) * qs
            k = l2norm(k) * ksc
            q, k = rotary_xpos(q, k)
            o = local_attention(q, k, v)
            o = o.transpose(0, 2, 1, 3).reshape(b, n, INNER)
            x = x + o @ wo
            h = shift_token(x)
            mu = h.mean(-1, keepdims=True)
            var = h.var(-1, keepdims=True)
            h = (h - mu) / jnp.sqrt(var + 1e-05) * lg + lb
            h = h @ w1 + b1
            a, g = jnp.split(h, 2, axis=-1)
            h = a * jax.nn.gelu(g, approximate=False)
            x = x + h @ w2 + b2
            return x
        key = jax.random.key(seed)
        ks = jax.random.split(key, 6)
        return {'x': jax.random.normal(ks[0], (B, N, DIM), jnp.float32), 'wqkv': jax.random.normal(ks[1], (DEPTH, DIM, 3 * INNER), jnp.float32) * 0.02, 'q_scale': jnp.ones((DEPTH, DIM_HEAD), jnp.float32), 'k_scale': jnp.ones((DEPTH, DIM_HEAD), jnp.float32), 'wo': jax.random.normal(ks[2], (DEPTH, INNER, DIM), jnp.float32) * 0.02, 'ln_g': jnp.ones((DEPTH, DIM), jnp.float32), 'ln_b': jnp.zeros((DEPTH, DIM), jnp.float32), 'w1': jax.random.normal(ks[3], (DEPTH, DIM, 2 * HID), jnp.float32) * 0.02, 'b1': jnp.zeros((DEPTH, 2 * HID), jnp.float32), 'w2': jax.random.normal(ks[4], (DEPTH, HID, DIM), jnp.float32) * 0.02, 'b2': jnp.zeros((DEPTH, DIM), jnp.float32)}
    _L1_ffn_in = _L1_ffn_setup()
    _d = {'L0_attn_x': _L0_attn_in['x'], 'L0_attn_w_qkv': _L0_attn_in['w_qkv'], 'L0_attn_w_out': _L0_attn_in['w_out'], 'L0_attn_b_out': _L0_attn_in['b_out'], 'L0_attn_gamma': _L0_attn_in['gamma'], 'L0_attn_beta': _L0_attn_in['beta'], 'L0_ffn_gate_w': _L0_ffn_in['gate_w'], 'L0_ffn_w_gate': _L0_ffn_in['w_gate'], 'L0_ffn_w_up': _L0_ffn_in['w_up'], 'L0_ffn_w_down': _L0_ffn_in['w_down'], 'L1_attn_W_in': _L1_attn_in['W_in'], 'L1_attn_conv_k': _L1_attn_in['conv_k'], 'L1_attn_conv_b': _L1_attn_in['conv_b'], 'L1_attn_W_xproj': _L1_attn_in['W_xproj'], 'L1_attn_W_dt': _L1_attn_in['W_dt'], 'L1_attn_b_dt': _L1_attn_in['b_dt'], 'L1_attn_A_log': _L1_attn_in['A_log'], 'L1_attn_D': _L1_attn_in['D'], 'L1_attn_W_out': _L1_attn_in['W_out'], 'L1_ffn_wqkv': _L1_ffn_in['wqkv'], 'L1_ffn_q_scale': _L1_ffn_in['q_scale'], 'L1_ffn_k_scale': _L1_ffn_in['k_scale'], 'L1_ffn_wo': _L1_ffn_in['wo'], 'L1_ffn_ln_g': _L1_ffn_in['ln_g'], 'L1_ffn_ln_b': _L1_ffn_in['ln_b'], 'L1_ffn_w1': _L1_ffn_in['w1'], 'L1_ffn_b1': _L1_ffn_in['b1'], 'L1_ffn_w2': _L1_ffn_in['w2'], 'L1_ffn_b2': _L1_ffn_in['b2']}
    _x0 = _d['L0_attn_x']
    _d['L0_attn_x'] = jax.random.normal(jax.random.fold_in(jax.random.key(seed), 1), (16, 256, 128), dtype=_x0.dtype)
    del _x0
    return _d

def reference(L0_attn_x, L0_attn_w_qkv, L0_attn_w_out, L0_attn_b_out, L0_attn_gamma, L0_attn_beta, L0_ffn_gate_w, L0_ffn_w_gate, L0_ffn_w_up, L0_ffn_w_down, L1_attn_W_in, L1_attn_conv_k, L1_attn_conv_b, L1_attn_W_xproj, L1_attn_W_dt, L1_attn_b_dt, L1_attn_A_log, L1_attn_D, L1_attn_W_out, L1_ffn_wqkv, L1_ffn_q_scale, L1_ffn_k_scale, L1_ffn_wo, L1_ffn_ln_g, L1_ffn_ln_b, L1_ffn_w1, L1_ffn_b1, L1_ffn_w2, L1_ffn_b2):

    def _L0_attn_ref(x, w_qkv, w_out, b_out, gamma, beta):
        import jax, jax.numpy as jnp
        import numpy as np
        DIM = 128
        DEPTH = 6
        LN_EPS = 1e-05

        def _layernorm(x, gamma, beta):
            mu = jnp.mean(x, axis=-1, keepdims=True)
            var = jnp.mean(jnp.square(x - mu), axis=-1, keepdims=True)
            return (x - mu) * jax.lax.rsqrt(var + LN_EPS) * gamma + beta
        depth = w_qkv.shape[0]
        for l in range(depth):
            residual = x
            h = _layernorm(x, gamma[l], beta[l])
            qkv = h @ w_qkv[l]
            q, k, v = jnp.split(qkv, 3, axis=-1)
            q = jax.nn.softmax(q, axis=1)
            k = jax.nn.softmax(k, axis=2)
            context = jnp.einsum('bic,bjc->bij', k, v)
            out = jnp.einsum('bic,bij->bjc', q, context)
            out = out @ w_out[l] + b_out[l]
            x = out + residual
        return x

    def _L0_ffn_ref(hidden_states, gate_w, w_gate, w_up, w_down):
        import jax, jax.numpy as jnp
        import numpy as np
        B, S, H, I, E = (2, 512, 128, 64, 8)
        b, s, h = hidden_states.shape
        x = hidden_states.reshape(-1, h)
        logits = x @ gate_w.T
        top_v = jnp.max(logits, axis=-1)
        sel = jnp.argmax(logits, axis=-1)
        rw = jax.nn.sigmoid(top_v)
        out = jnp.zeros_like(x)
        n_exp = gate_w.shape[0]
        for e in range(n_exp):
            mask = (sel == e).astype(x.dtype)
            xs = x * (rw * mask)[:, None]
            g = xs @ w_gate[e].T
            u = xs @ w_up[e].T
            out = out + u * jax.nn.silu(g) @ w_down[e].T
        return out.reshape(b, s, h)

    def _L1_attn_ref(x, W_in, conv_k, conv_b, W_xproj, W_dt, b_dt, A_log, D, W_out):
        import jax, jax.numpy as jnp
        import numpy as np
        D_MODEL = 128
        D_STATE = 16
        D_CONV = 4
        EXPAND = 2
        D_INNER = EXPAND * D_MODEL
        DT_RANK = D_INNER // 16
        BATCH = 2
        SEQLEN = 128

        def _silu(x):
            return x * jax.nn.sigmoid(x)
        xz = x @ W_in
        x_in, z = jnp.split(xz, 2, axis=-1)
        xp = jnp.pad(x_in, ((0, 0), (D_CONV - 1, 0), (0, 0)))
        x_in = jax.lax.conv_general_dilated(xp, conv_k, window_strides=(1,), padding='VALID', dimension_numbers=('NWC', 'WIO', 'NWC'), feature_group_count=D_INNER) + conv_b
        u = _silu(x_in)
        x_dbl = u @ W_xproj
        dt_low, Bm, Cm = jnp.split(x_dbl, [DT_RANK, DT_RANK + D_STATE], axis=-1)
        dt = jax.nn.softplus(dt_low @ W_dt + b_dt)
        A = -jnp.exp(A_log)
        dA = jnp.exp(jnp.einsum('bld,dn->bldn', dt, A))
        dB = jnp.einsum('bld,bln->bldn', dt, Bm)

        def step(h, e):
            a_t, b_t, u_t, c_t = e
            h = a_t * h + b_t * u_t[..., None]
            y_t = jnp.einsum('bdn,bn->bd', h, c_t)
            return (h, y_t)
        h0 = jnp.zeros((x.shape[0], D_INNER, D_STATE), dtype=x.dtype)
        xs = (jnp.swapaxes(dA, 0, 1), jnp.swapaxes(dB, 0, 1), jnp.swapaxes(u, 0, 1), jnp.swapaxes(Cm, 0, 1))
        _, yT = jax.lax.scan(step, h0, xs)
        y = jnp.swapaxes(yT, 0, 1) + u * D
        return y * _silu(z) @ W_out

    def _L1_ffn_ref(x, wqkv, q_scale, k_scale, wo, ln_g, ln_b, w1, b1, w2, b2):
        import jax, jax.numpy as jnp
        import numpy as np
        DIM = 128
        DEPTH = 2
        HEADS = 8
        DIM_HEAD = 64
        WINDOW = 64
        INNER = HEADS * DIM_HEAD
        HID = int(DIM * 4 * 2 / 3)
        B, N = (2, 1024)
        QK_SCALE = 8.0

        def shift_token(t):
            t1, t2 = jnp.split(t, 2, axis=-1)
            t2 = jnp.pad(t2, ((0, 0), (1, 0), (0, 0)))[:, :-1]
            return jnp.concatenate([t1, t2], axis=-1)

        def l2norm(t):
            return t / jnp.clip(jnp.linalg.norm(t, axis=-1, keepdims=True), 1e-12)

        def rotate_half(x):
            x1, x2 = jnp.split(x, 2, axis=-1)
            return jnp.concatenate([-x2, x1], axis=-1)

        def rotary_xpos(q, k):
            n = q.shape[-2]
            half_idx = jnp.arange(0, DIM_HEAD, 2, dtype=jnp.float32)
            inv_freq = 1.0 / 10000.0 ** (half_idx / DIM_HEAD)
            t = jnp.arange(n, dtype=jnp.float32)
            freqs = t[:, None] * inv_freq[None, :]
            freqs = jnp.concatenate([freqs, freqs], axis=-1)
            base = (half_idx + 0.4 * DIM_HEAD) / (1.4 * DIM_HEAD)
            power = (t - n // 2) / float(WINDOW // 2)
            scale = base[None, :] ** power[:, None]
            scale = jnp.concatenate([scale, scale], axis=-1)
            cos, sin = (jnp.cos(freqs), jnp.sin(freqs))
            q = q * cos * scale + rotate_half(q) * sin * scale
            k = k * cos / scale + rotate_half(k) * sin / scale
            return (q, k)

        def local_attention(q, k, v):
            b, h, n, d = q.shape
            w = n // WINDOW
            bq = q.reshape(b, h, w, WINDOW, d) * QK_SCALE
            bk = k.reshape(b, h, w, WINDOW, d)
            bv = v.reshape(b, h, w, WINDOW, d)

            def look_around(t):
                p = jnp.pad(t, ((0, 0), (0, 0), (1, 0), (0, 0), (0, 0)))
                return jnp.concatenate([p[:, :, :w], p[:, :, 1:]], axis=3)
            bk, bv = (look_around(bk), look_around(bv))
            bt = jnp.arange(n).reshape(w, WINDOW)
            btp = jnp.pad(bt, ((1, 0), (0, 0)), constant_values=-1)
            btk = jnp.concatenate([btp[:w], btp[1:]], axis=1)
            sim = jnp.einsum('bhwid,bhwjd->bhwij', bq, bk)
            i = bt[:, :, None]
            j = btk[:, None, :]
            mask = (i < j) | (i > j + WINDOW) | (j == -1)
            sim = jnp.where(mask, -jnp.finfo(sim.dtype).max, sim)
            attn = jax.nn.softmax(sim, axis=-1)
            out = jnp.einsum('bhwij,bhwjd->bhwid', attn, bv)
            return out.reshape(b, h, n, d)

        def _layer(x, wqkv, qs, ksc, wo, lg, lb, w1, b1, w2, b2):
            b, n, _ = x.shape
            h = shift_token(x)
            qkv = h @ wqkv
            q, k, v = jnp.split(qkv, 3, axis=-1)
            to_heads = lambda t: t.reshape(b, n, HEADS, DIM_HEAD).transpose(0, 2, 1, 3)
            q, k, v = (to_heads(q), to_heads(k), to_heads(v))
            q = l2norm(q) * qs
            k = l2norm(k) * ksc
            q, k = rotary_xpos(q, k)
            o = local_attention(q, k, v)
            o = o.transpose(0, 2, 1, 3).reshape(b, n, INNER)
            x = x + o @ wo
            h = shift_token(x)
            mu = h.mean(-1, keepdims=True)
            var = h.var(-1, keepdims=True)
            h = (h - mu) / jnp.sqrt(var + 1e-05) * lg + lb
            h = h @ w1 + b1
            a, g = jnp.split(h, 2, axis=-1)
            h = a * jax.nn.gelu(g, approximate=False)
            x = x + h @ w2 + b2
            return x
        for l in range(DEPTH):
            x = _layer(x, wqkv[l], q_scale[l], k_scale[l], wo[l], ln_g[l], ln_b[l], w1[l], b1[l], w2[l], b2[l])
        return x
    x = L0_attn_x
    x = x + 0.5 * _L0_ffn_ref(_layernorm(x, axis=-1), L0_ffn_gate_w, L0_ffn_w_gate, L0_ffn_w_up, L0_ffn_w_down)
    x = x + _L0_attn_ref(_layernorm(x, axis=-1), L0_attn_w_qkv, L0_attn_w_out, L0_attn_b_out, L0_attn_gamma, L0_attn_beta)
    x = x + 0.5 * _L0_ffn_ref(_layernorm(x, axis=-1), L0_ffn_gate_w, L0_ffn_w_gate, L0_ffn_w_up, L0_ffn_w_down)
    x = x + 0.5 * _L1_ffn_ref(_layernorm(x, axis=-1), L1_ffn_wqkv, L1_ffn_q_scale, L1_ffn_k_scale, L1_ffn_wo, L1_ffn_ln_g, L1_ffn_ln_b, L1_ffn_w1, L1_ffn_b1, L1_ffn_w2, L1_ffn_b2)
    x = x + _L1_attn_ref(_layernorm(x, axis=-1), L1_attn_W_in, L1_attn_conv_k, L1_attn_conv_b, L1_attn_W_xproj, L1_attn_W_dt, L1_attn_b_dt, L1_attn_A_log, L1_attn_D, L1_attn_W_out)
    x = x + 0.5 * _L1_ffn_ref(_layernorm(x, axis=-1), L1_ffn_wqkv, L1_ffn_q_scale, L1_ffn_k_scale, L1_ffn_wo, L1_ffn_ln_g, L1_ffn_ln_b, L1_ffn_w1, L1_ffn_b1, L1_ffn_w2, L1_ffn_b2)
    return x

_drawn_inputs = setup_inputs


def setup_inputs(seed=0):
    import zlib

    import numpy as np

    out = dict(_drawn_inputs(seed))
    spreads = {'L0_attn_b_out': (0.0, 0.1),
     'L0_attn_gamma': (1.0, 0.6),
     'L0_attn_beta': (0.0, 0.8),
     'L1_attn_conv_b': (0.0, 0.8),
     'L1_attn_b_dt': (0.0, 0.8),
     'L1_attn_D': (1.0, 0.6),
     'L1_ffn_q_scale': (1.0, 0.6),
     'L1_ffn_k_scale': (1.0, 0.6),
     'L1_ffn_ln_g': (1.0, 0.6),
     'L1_ffn_ln_b': (0.0, 0.8),
     'L1_ffn_b1': (0.0, 0.8),
     'L1_ffn_b2': (0.0, 0.696)}
    factors = {'L0_attn_w_qkv': 8.0,
     'L0_attn_w_out': 8.0,
     'L1_attn_W_in': 8.0,
     'L1_attn_conv_k': 8.0,
     'L1_attn_W_xproj': 8.0,
     'L1_attn_W_dt': 8.0,
     'L1_attn_A_log': 8.0,
     'L1_attn_W_out': 8.0,
     'L1_ffn_wqkv': 4.288,
     'L1_ffn_wo': 4.14,
     'L1_ffn_w1': 8.0,
     'L1_ffn_w2': 8.0}
    for name, (base, spread) in spreads.items():
        noise = np.random.default_rng([zlib.crc32(name.encode()), seed]).standard_normal(out[name].shape)
        drawn = base * np.exp(spread * noise) if base else spread * noise
        out[name] = jnp.asarray(drawn.astype(out[name].dtype))
    for name, factor in factors.items():
        out[name] = (out[name] * factor).astype(out[name].dtype)
    return out
```

```python
from contextlib import ExitStack

import numpy as np
import concourse.bass as bass
from concourse import mybir

FP32 = mybir.dt.float32
BF16 = mybir.dt.bfloat16
ALU = mybir.AluOpType
ACT = mybir.ActivationFunctionType
AX = mybir.AxisListType

P = 128
SEQS, SEQ_LEN, DIM = 16, 256, 128
TOKENS = SEQS * SEQ_LEN
TILES = TOKENS // P
EPS = 1e-5

EXPERTS, EXPERT_HID = 8, 64
MOE_CHUNKS = EXPERTS * EXPERT_HID // P


class Core:

    def __init__(self, nc, dram, stack):
        self.nc, self.dram, self.stack, self.sems = nc, dram, stack, {}

    def sbuf(self, name, shape, dtype=FP32, stack=None):
        return (stack or self.stack).enter_context(self.nc.sbuf_tensor(f"{name}_sb", shape, dtype))

    def sem(self, name):
        if name not in self.sems:
            self.sems[name] = self.stack.enter_context(self.nc.semaphore(name))
        return self.sems[name]

    def clear(self, kind):
        with self.nc.Block() as block:
            @block.gpsimd
            def _(pool):
                for name, sem in self.sems.items():
                    if name.startswith(f"{kind}_"):
                        pool.sem_clear(sem)


def load_stage(k):
    nc, dram = k.nc, k.dram
    k.psum = k.stack.enter_context(nc.psum_tensor("psum", [P, 8, 512], FP32))
    k.x = k.sbuf("x", [P, TILES, DIM])
    k.y = k.sbuf("y", [P, TILES, DIM])
    k.ident = k.sbuf("ident", [P, P])
    k.neg_half = k.sbuf("neg_half", [P, 32])
    k.loaded = k.sem("loaded")
    k.const = {}
    small = [n for n in dram if n.startswith(("c_", "b_"))]
    landing = ExitStack()
    for n in small:
        k.const[n[2:]] = k.sbuf(n, list(dram[n].shape), FP32 if n.startswith("c_") else BF16)
    landed = {n: k.sbuf(f"{n}_landing", list(dram[n].shape), FP32, landing) if n.startswith("b_") else k.const[n[2:]]
              for n in small}
    consts_done = k.sem("consts_done")
    with nc.Block() as block:
        @block.sync
        def _(sp):
            sp.dma_start(k.x[:], dram["x"]).then_inc(k.loaded, 16)
            for n in small:
                sp.dma_start(landed[n][:], dram[n]).then_inc(k.loaded, 16)
            sp.dma_start(k.ident[:], dram["ident"]).then_inc(k.loaded, 16)
            sp.wait_ge(k.loaded, 16 * (len(small) + 2))

        @block.vector
        def _(dve):
            nc.vector.memset(k.neg_half[:], -0.5).then_inc(consts_done, 1)
            dve.wait_ge(k.loaded, 16 * (len(small) + 2))
            for n in small:
                if n.startswith("b_"):
                    nc.vector.tensor_copy(k.const[n[2:]][:], landed[n][:])
    landing.close()


def settle(eng, sem, value):
    eng.wait_ge(sem, value)
    eng.nop(nofuse=True)


def add_norm_buffers(k, name, kind, tiles, mem):
    b = type("NormBuffers", (), {})()
    b.tiles = tiles
    b.stats = k.sbuf(f"{name}_stats", [P, tiles, 6], FP32, mem)
    b.mv = k.sbuf(f"{name}_mv", [P, tiles, 2], FP32, mem)
    b.var_eps = k.sbuf(f"{name}_var_eps", [P, tiles], FP32, mem)
    b.rstd = k.sbuf(f"{name}_rstd", [P, tiles], FP32, mem)
    b.stats_done = k.sem(f"{kind}_stats_done")
    b.mean_done = k.sem(f"{kind}_mean_done")
    b.var_ready = k.sem(f"{kind}_var_ready")
    b.rstd_ready = k.sem(f"{kind}_rstd_ready")
    return b


def norm_statistics(k, dve, b, t, tile):
    nc = k.nc
    for j in range(b.tiles):
        last = nc.vector.bn_stats(b.stats[:, j, :], tile(j))
    last.then_inc(b.stats_done, 1)
    settle(dve, b.stats_done, t + 1)
    for j in range(b.tiles):
        last = nc.vector.bn_aggr(b.mv[:, j, :], b.stats[:, j, :])
    last.then_inc(b.mean_done, 1)
    dve.wait_ge(b.mean_done, t + 1)
    nc.vector.tensor_scalar(b.var_eps[:], b.mv[:, :, 1], EPS, None, ALU.add).then_inc(b.var_ready, 1)


def norm_rstd(k, pool, b, t):
    pool.wait_ge(b.var_ready, t + 1)
    k.nc.gpsimd.tensor_tensor(b.rstd[:], b.var_eps[:], k.neg_half[:, 0:b.tiles], ALU.pow).then_inc(b.rstd_ready, 1)


def norm_apply(k, dve, b, t, out, tile, done):
    dve.wait_ge(b.rstd_ready, t + 1)
    for j in range(b.tiles):
        last = k.nc.vector.tensor_scalar(out(j), tile(j), b.mv[:, j, 0:1], b.rstd[:, j:j + 1],
                                         ALU.subtract, ALU.mult)
    last.then_inc(*done)


def moe_stage(k, name):
    nc, psum, x = k.nc, k.psum, k.x
    wg, wu, wd = k.const["moe_wg"], k.const["moe_wu"], k.const["moe_wd"]
    gate_w, sel, rank = k.const["moe_gate"], k.const["moe_sel"], k.const["moe_rank"]
    GT = 4
    GROUPS = TILES // GT
    W = GT * P
    C = MOE_CHUNKS

    with ExitStack() as mem:
        def sb(n, shape, dtype=FP32):
            return k.sbuf(f"{name}_{n}", shape, dtype, mem)

        stats = sb("stats", [P, 2, GT, 6])
        mv = sb("mv", [P, 2, GT, 2])
        var_eps = sb("var_eps", [P, 2, GT])
        rstd = sb("rstd", [P, 2, GT])
        h = sb("h", [P, 2, GT, P])
        hT = sb("hT", [P, 2, W])
        top = sb("top", [P, 2, GT])
        is_top = sb("is_top", [P, 2, GT, EXPERTS])
        ranked = sb("ranked", [P, 2, GT, EXPERTS])
        first = sb("first", [P, 2, GT])
        onehot = sb("onehot", [P, 2, GT, EXPERTS])
        tanh = sb("tanh", [P, 2, GT])
        rw = sb("rw", [P, 2, GT])
        hs = sb("hs", [P, 2, GT, P])
        hsT = sb("hsT", [P, 2, W])
        maskT = sb("maskT", [EXPERTS, 2, W], BF16)
        silu = sb("silu", [P, 2, W])
        su = sb("su", [P, 2, W])
        hid = sb("hid", [P, 2, W])

        var_ready = k.sem(f"moe_var_ready")
        rstd_ready = k.sem(f"moe_rstd_ready")
        h_ready = k.sem(f"moe_h_ready")
        hT_in_psum = k.sem(f"moe_hT_in_psum")
        hT_ready = k.sem(f"moe_hT_ready")
        logits_ready = k.sem(f"moe_logits_ready")
        top_ready = k.sem(f"moe_top_ready")
        tanh_ready = k.sem(f"moe_tanh_ready")
        hs_ready = k.sem(f"moe_hs_ready")
        hsT_in_psum = k.sem(f"moe_hsT_in_psum")
        hsT_ready = k.sem(f"moe_hsT_ready")
        up_done = k.sem(f"moe_up_done")
        silu_ready = k.sem(f"moe_silu_ready")
        hid_ready = k.sem(f"moe_hid_ready")
        out_ready = k.sem(f"moe_out_ready")
        front = k.sem(f"moe_front_steps")
        FRONT = 6
        su_ready = k.sem(f"moe_su_ready")

        def bank(u):
            return psum[:, u, :]

        def slot(s, what):
            return psum[:, 2 + 3 * s + what, :]

        mask_bank = slot((C - 1) % 2, 2)

        def tiles(ap, t):
            return ap[:, bass.ts(t, GT), :]

        def run(eng, work):
            work(eng, None, None, 0, 0)
            with eng.Fori(0, GROUPS // 2 - 1) as i:
                work(eng, 2 * i, 0, 2 * i + 1, 1)
                work(eng, 2 * i + 1, 1, 2 * i + 2, 0)
            work(eng, GROUPS - 2, 0, GROUPS - 1, 1)
            work(eng, GROUPS - 1, 1, None, None)

        def transpose_h(pe, t, u):
            pe.wait_ge(h_ready, t + 1)
            for j in range(GT):
                last = nc.tensor.transpose(bank(u)[:, j * P:(j + 1) * P], h[:, u, j, :], k.ident[:])
            last.then_inc(hT_in_psum, 1)

        def gate(pe, t, u):
            pe.wait_ge(hT_ready, t + 1)
            for j in range(GT):
                last = nc.tensor.matmul(bank(u)[:, j * EXPERTS:(j + 1) * EXPERTS],
                                        hT[:, u, j * P:(j + 1) * P], gate_w[:], start=True, stop=True)
            last.then_inc(logits_ready, 1)

        def transpose_scaled(pe, t, u):
            pe.wait_ge(hs_ready, t + 1)
            for j in range(GT):
                nc.tensor.transpose(bank(u)[:, j * P:(j + 1) * P], hs[:, u, j, :], k.ident[:])
            for j in range(GT):
                last = nc.tensor.transpose(mask_bank[0:EXPERTS, j * P:(j + 1) * P],
                                           onehot[:, u, j, :], k.ident[:])
            last.then_inc(hsT_in_psum, 1)

        def up(t, u, c):
            s = c % 2
            nc.tensor.matmul(slot(s, 0), wg[:, c * P:(c + 1) * P], hsT[:, u, :], start=True, stop=True)
            nc.tensor.matmul(slot(s, 1), wu[:, c * P:(c + 1) * P], hsT[:, u, :], start=True, stop=True)
            nc.tensor.matmul(slot(s, 2), sel[:, c, :], maskT[:, u, :], start=True, stop=True).then_inc(up_done, 1)

        def down(pe, t, u, c):
            pe.wait_ge(hid_ready, C * t + c + 1)
            for j in range(GT):
                last = nc.tensor.matmul(bank(u)[:, j * P:(j + 1) * P], hid[:, c % 2, j * P:(j + 1) * P],
                                        wd[:, c, :], start=(c == 0 and j == 0), stop=(c == C - 1),
                                        skip_group_check=True)
            if c == C - 1:
                last.then_inc(out_ready, 1)

        def pe_work(pe, t, u, n, un):
            if t is not None:
                pe.wait_ge(hsT_ready, t + 1)
                up(t, u, 0)
            for c in range(C):
                if t is not None and c + 1 < C:
                    up(t, u, c + 1)
                if n is not None and c == 1:
                    transpose_h(pe, n, un)
                if n is not None and c == 2:
                    gate(pe, n, un)
                if t is not None:
                    down(pe, t, u, c)
            if n is not None:
                transpose_scaled(pe, n, un)

        def row_statistics(dve, t, u):
            for j in range(GT):
                last = nc.vector.bn_stats(stats[:, u, j, :], x[:, bass.ts(GT * t + j, 1), :])
            last.then_inc(front, 1)
            settle(dve, front, FRONT * t + 1)
            for j in range(GT):
                last = nc.vector.bn_aggr(mv[:, u, j, :], stats[:, u, j, :])
            last.then_inc(front, 1)
            dve.wait_ge(front, FRONT * t + 2)
            nc.vector.tensor_scalar(var_eps[:, u, :], mv[:, u, :, 1], EPS, None, ALU.add).then_inc(var_ready, 1)

        def normalize(dve, t, u):
            dve.wait_ge(rstd_ready, t + 1)
            for j in range(GT):
                last = nc.vector.tensor_scalar(h[:, u, j, :], x[:, bass.ts(GT * t + j, 1), :], mv[:, u, j, 0:1],
                                               rstd[:, u, j:j + 1], ALU.subtract, ALU.mult)
            last.then_inc(h_ready, 1)

        def choose(dve, t, u):
            dve.wait_ge(logits_ready, t + 1)
            logits = bank(u)[:, 0:GT * EXPERTS].rearrange("p (j e) -> p j e", e=EXPERTS)
            nc.vector.tensor_reduce(top[:, u, :], logits, AX.X, ALU.max).then_inc(top_ready, 1)
            dve.wait_ge(top_ready, t + 1)
            nc.vector.tensor_tensor(is_top[:, u], logits,
                                    top[:, u, :].unsqueeze(2).broadcast_to([P, GT, EXPERTS]),
                                    ALU.is_equal).then_inc(front, 1)
            dve.wait_ge(front, FRONT * t + 3)
            nc.vector.tensor_tensor(ranked[:, u], is_top[:, u], rank[:], ALU.mult).then_inc(front, 1)
            dve.wait_ge(front, FRONT * t + 4)
            nc.vector.tensor_reduce(first[:, u, :], ranked[:, u], AX.X, ALU.max).then_inc(front, 1)
            dve.wait_ge(front, FRONT * t + 5)
            nc.vector.tensor_tensor(onehot[:, u], ranked[:, u],
                                    first[:, u, :].unsqueeze(2).broadcast_to([P, GT, EXPERTS]), ALU.is_equal)
            dve.wait_ge(tanh_ready, t + 1)
            nc.vector.tensor_scalar(rw[:, u, :], tanh[:, u, :], 0.5, 0.5, ALU.mult, ALU.add).then_inc(front, 1)
            dve.wait_ge(front, FRONT * t + 6)
            for j in range(GT):
                last = nc.vector.tensor_scalar(hs[:, u, j, :], h[:, u, j, :], rw[:, u, j:j + 1], None, ALU.mult)
            last.then_inc(hs_ready, 1)

        def hidden(dve, t, u, c):
            s = c % 2
            dve.wait_ge(silu_ready, C * t + c + 1)
            nc.vector.tensor_tensor(su[:, s, :], silu[:, s, :], slot(s, 1), ALU.mult).then_inc(su_ready, 1)
            dve.wait_ge(su_ready, C * t + c + 1)
            nc.vector.tensor_tensor(hid[:, s, :], su[:, s, :], slot(s, 2), ALU.mult).then_inc(hid_ready, 1)

        def dve_work(dve, t, u, n, un):
            if n is not None:
                row_statistics(dve, n, un)
            for c in range(C):
                if t is not None:
                    hidden(dve, t, u, c)
                if n is not None and c == 0:
                    normalize(dve, n, un)
                if n is not None and c == 2:
                    choose(dve, n, un)
            if t is not None:
                dve.wait_ge(out_ready, t + 1)
                nc.vector.scalar_tensor_tensor(tiles(x, t), bank(u).rearrange("p (j f) -> p j f", f=DIM), 0.5,
                                               tiles(x, t), ALU.mult, ALU.add)

        def act_work(act, t, u, n, un):
            for c in range(C):
                if t is not None:
                    act.wait_ge(up_done, C * t + c + 1)
                    nc.scalar.activation(silu[:, c % 2, :], slot(c % 2, 0), ACT.Silu).then_inc(silu_ready, 1)
                if n is not None and c == 1:
                    act.wait_ge(hT_in_psum, n + 1)
                    nc.scalar.activation(hT[:, un, :], bank(un), ACT.Copy).then_inc(hT_ready, 1)
                if n is not None and c == 2:
                    act.wait_ge(top_ready, n + 1)
                    nc.scalar.activation(tanh[:, un, :], top[:, un, :], ACT.Tanh, scale=0.5).then_inc(tanh_ready, 1)
            if n is not None:
                act.wait_ge(hsT_in_psum, n + 1)
                nc.scalar.activation(hsT[:, un, :], bank(un), ACT.Copy)
                nc.scalar.activation(maskT[:, un, :], mask_bank[0:EXPERTS, :], ACT.Copy).then_inc(hsT_ready, 1)

        def pool_work(pool, t, u, n, un):
            if n is not None:
                pool.wait_ge(var_ready, n + 1)
                nc.gpsimd.tensor_tensor(rstd[:, un, :], var_eps[:, un, :], k.neg_half[:, 0:GT],
                                        ALU.pow).then_inc(rstd_ready, 1)

        with nc.Block() as block:
            @block.tensor
            def _(pe):
                run(pe, pe_work)

            @block.vector
            def _(dve):
                run(dve, dve_work)

            @block.scalar
            def _(act):
                run(act, act_work)

            @block.gpsimd
            def _(pool):
                run(pool, pool_work)


def linear_attention_stage(k, name="lin"):
    nc, psum, x, y = k.nc, k.psum, k.x, k.y
    S = 4
    GROUPS = SEQS // S
    T = SEQ_LEN // P
    gamma, beta, bias = k.const["lin_gamma"], k.const["lin_beta"], k.const["lin_bias"]
    w_dram = k.dram["lin_w"]

    with ExitStack() as mem:
        def sb(n, shape):
            return k.sbuf(f"{name}_{n}", shape, FP32, mem)

        w = sb("w", [P, 2, 4 * P])
        h = sb("h", [P, S * T, P])
        hT = sb("hT", [P, S, SEQ_LEN])
        neg_max = sb("neg_max", [P, S, 1 + T])
        expq_T = sb("expq_T", [P, S, SEQ_LEN])
        expk = sb("expk", [P, S, T, P])
        sums = sb("sums", [P, S, 1 + T])
        inv = sb("inv", [P, S, 1 + T])
        expq = sb("expq", [P, S, T, P])
        MT = sb("MT", [P, S, P])
        G = sb("G", [P, S, P])
        F = sb("F", [P, S, P])
        outer = add_norm_buffers(k, f"{name}_outer", f"{name}_outer", S * T, mem)
        inner = add_norm_buffers(k, f"{name}_inner", f"{name}_inner", S * T, mem)

        w_loaded = [k.sem(f"{name}_w_loaded{p}") for p in range(2)]
        y_ready = k.sem(f"{name}_y_ready")
        h_ready = k.sem(f"{name}_h_ready")
        bias_added = k.sem(f"{name}_bias_added")
        hT_in_psum = k.sem(f"{name}_hT_in_psum")
        hT_ready = k.sem(f"{name}_hT_ready")
        qk_in_psum = k.sem(f"{name}_qk_in_psum")
        max_ready = k.sem(f"{name}_max_ready")
        exp_ready = k.sem(f"{name}_exp_ready")
        inv_ready = k.sem(f"{name}_inv_ready")
        expq_in_psum = k.sem(f"{name}_expq_in_psum")
        expq_ready = k.sem(f"{name}_expq_ready")
        MT_in_psum = k.sem(f"{name}_MT_in_psum")
        MT_ready = k.sem(f"{name}_MT_ready")
        G_in_psum = k.sem(f"{name}_G_in_psum")
        G_ready = k.sem(f"{name}_G_ready")
        F_in_psum = k.sem(f"{name}_F_in_psum")
        F_ready = k.sem(f"{name}_F_ready")
        out_in_psum = k.sem(f"{name}_out_in_psum")

        LAYERS = k.dram["lin_w"].shape[0]

        def Wq(p): return w[:, p, 0:P]
        def Wk(p): return w[:, p, P:2 * P]
        def WvT(p): return w[:, p, 2 * P:3 * P]
        def Wout(p): return w[:, p, 3 * P:4 * P]

        def q_ps(s): return psum[:, s, 0:SEQ_LEN]
        def k_ps(s): return psum[:, s, SEQ_LEN:2 * SEQ_LEN]
        def F_ps(s): return psum[:, s, 0:P]
        def out_ps(s): return psum[:, s, SEQ_LEN:2 * SEQ_LEN]
        def tr_ps(s): return psum[:, 4 + s, 0:SEQ_LEN]
        def MT_ps(s): return psum[:, 4 + s, 2 * P:3 * P]
        def G_ps(s): return psum[:, 4 + s, 3 * P:4 * P]

        def run(eng, work, front):
            def layer(l, p, last):
                with eng.Fori(0, GROUPS - 1) as g:
                    work(eng, l, p, g, (l, g + 1))
                work(eng, l, p, GROUPS - 1, None if last else (l + 1, 0))
            front(eng, 0, 0)
            with eng.Fori(0, LAYERS // 2 - 1) as i:
                layer(2 * i, 0, False)
                layer(2 * i + 1, 1, False)
            layer(LAYERS - 2, 0, False)
            layer(LAYERS - 1, 1, True)

        def unit(l, g, s):
            return SEQS * l + S * g + s

        def pe_front(pe, l, g):
            for s in range(S):
                if s == 0:
                    pe.wait_ge(h_ready, GROUPS * l + g + 1)
                for j in range(T):
                    last = nc.tensor.transpose(tr_ps(s)[:, j * P:(j + 1) * P], h[:, T * s + j, :], k.ident[:])
                last.then_inc(hT_in_psum, 1)

        def pe_work(pe, l, p, g, nxt):
            for s in range(S):
                if s == 0:
                    pe.wait_ge(w_loaded[p], 8 * (l - p) + 16)
                pe.wait_ge(hT_ready, unit(l, g, s) + 1)
                pe.wait_ge(y_ready, unit(l, g, s) + 1 + SEQS - S)
                nc.tensor.matmul(q_ps(s), Wq(p), hT[:, s, :], start=True, stop=True)
                for j in range(T):
                    last = nc.tensor.matmul(k_ps(s)[:, j * P:(j + 1) * P], hT[:, s, j * P:(j + 1) * P], Wk(p),
                                            start=True, stop=True)
                last.then_inc(qk_in_psum, 1)
            for s in range(S):
                pe.wait_ge(exp_ready, unit(l, g, s) + 1)
                for j in range(T):
                    last = nc.tensor.transpose(tr_ps(s)[:, j * P:(j + 1) * P], expq_T[:, s, j * P:(j + 1) * P],
                                               k.ident[:])
                last.then_inc(expq_in_psum, 1)
            for s in range(S):
                pe.wait_ge(expq_ready, unit(l, g, s) + 1)
                for j in range(T):
                    last = nc.tensor.matmul(MT_ps(s), expq[:, s, j, :], expk[:, s, j, :],
                                            start=(j == 0), stop=(j == T - 1))
                last.then_inc(MT_in_psum, 1)
            for s in range(S):
                pe.wait_ge(MT_ready, unit(l, g, s) + 1)
                nc.tensor.matmul(G_ps(s), MT[:, s, :], Wout(p), start=True, stop=True).then_inc(G_in_psum, 1)
            for s in range(S):
                pe.wait_ge(G_ready, unit(l, g, s) + 1)
                nc.tensor.matmul(F_ps(s), WvT(p), G[:, s, :], start=True, stop=True).then_inc(F_in_psum, 1)
            for s in range(S):
                pe.wait_ge(F_ready, unit(l, g, s) + 1)
                for j in range(T):
                    last = nc.tensor.matmul(out_ps(s)[:, j * P:(j + 1) * P], hT[:, s, j * P:(j + 1) * P],
                                            F[:, s, :], start=True, stop=True)
                last.then_inc(out_in_psum, 1)
            if nxt is not None:
                pe_front(pe, *nxt)

        def y_tile(g, j):
            return y[:, bass.ts(S * T * g + j, 1), :]

        def dve_front(dve, l, g):
            dve.wait_ge(y_ready, SEQS * l + S * g + S)
            norm_statistics(k, dve, inner, GROUPS * l + g, lambda j: y_tile(g, j))
            norm_apply(k, dve, inner, GROUPS * l + g, lambda j: h[:, j:j + 1, :], lambda j: y_tile(g, j), (h_ready, 1))

        def dve_work(dve, l, p, g, nxt):
            for s in range(S):
                dve.wait_ge(qk_in_psum, unit(l, g, s) + 1)
                nc.vector.tensor_reduce(neg_max[:, s, 0:1], q_ps(s), AX.X, ALU.max, negate=True)
                nc.vector.tensor_reduce(neg_max[:, s, 1:1 + T], k_ps(s).rearrange("p (j c) -> p j c", c=P),
                                        AX.X, ALU.max, negate=True).then_inc(max_ready, 1)
            for s in range(S):
                dve.wait_ge(exp_ready, unit(l, g, s) + 1)
                nc.vector.reciprocal(inv[:, s, :], sums[:, s, :]).then_inc(inv_ready, 1)
            for s in range(S):
                dve.wait_ge(expq_in_psum, unit(l, g, s) + 1)
                if s == 0:
                    dve.wait_ge(inv_ready, unit(l, g, S - 1) + 1)
                for j in range(T):
                    last = nc.vector.tensor_scalar(expq[:, s, j, :], tr_ps(s)[:, j * P:(j + 1) * P],
                                                   inv[:, s, 1 + j:2 + j], None, ALU.mult)
                last.then_inc(expq_ready, 1)
            for s in range(S):
                dve.wait_ge(MT_in_psum, unit(l, g, s) + 1)
                nc.vector.tensor_scalar(MT[:, s, :], MT_ps(s), inv[:, s, 0:1], None, ALU.mult).then_inc(MT_ready, 1)
            if nxt is not None:
                dve_front(dve, *nxt)
            for s in range(S):
                dve.wait_ge(out_in_psum, unit(l, g, s) + 1)
                dve.wait_ge(bias_added, unit(l, g, s) + 1)
                rows = y[:, bass.ts(S * g + s, T), :]
                nc.vector.tensor_tensor(rows, out_ps(s).rearrange("p (j f) -> p j f", f=DIM), rows,
                                        ALU.add).then_inc(y_ready, 1)

        def act_front(act, l, g):
            for s in range(S):
                settle(act, hT_in_psum, unit(l, g, s) + 1)
                nc.scalar.activation(hT[:, s, :], tr_ps(s), ACT.Identity, bias=beta[:, bass.ts(l, 1)],
                                     scale=gamma[:, bass.ts(l, 1)]).then_inc(hT_ready, 1)

        def act_work(act, l, p, g, nxt):
            for s in range(S):
                act.wait_ge(max_ready, unit(l, g, s) + 1)
                nc.scalar.activation(expq_T[:, s, :], q_ps(s), ACT.Exp, bias=neg_max[:, s, 0:1],
                                     accum_out=sums[:, s, 0:1])
                for j in range(T):
                    last = nc.scalar.activation(expk[:, s, j, :], k_ps(s)[:, j * P:(j + 1) * P], ACT.Exp,
                                                bias=neg_max[:, s, 1 + j:2 + j], accum_out=sums[:, s, 1 + j:2 + j])
                last.then_inc(exp_ready, 1)
            for s in range(S):
                act.wait_ge(G_in_psum, unit(l, g, s) + 1)
                nc.scalar.activation(G[:, s, :], G_ps(s), ACT.Copy).then_inc(G_ready, 1)
            for s in range(S):
                act.wait_ge(F_in_psum, unit(l, g, s) + 1)
                nc.scalar.activation(F[:, s, :], F_ps(s), ACT.Copy).then_inc(F_ready, 1)
            if nxt is not None:
                act_front(act, *nxt)

        def pool_front(pool, l, g):
            norm_rstd(k, pool, inner, GROUPS * l + g)
            pool.wait_ge(h_ready, GROUPS * l + g + 1)
            for s in range(S):
                rows = y[:, bass.ts(S * g + s, T), :]
                nc.gpsimd.tensor_tensor(rows, rows, bias[:, bass.ts(l, 1), :].broadcast_to([P, T, DIM]),
                                        ALU.add).then_inc(bias_added, 1)

        def pool_work(pool, l, p, g, nxt):
            if nxt is not None:
                pool_front(pool, *nxt)

        with nc.Block() as block:
            @block.sync
            def _(sp):
                for p in range(2):
                    sp.dma_start(w[:, p, :], w_dram[p]).then_inc(w_loaded[p], 16)
                with sp.Fori(0, LAYERS // 2 - 1) as i:
                    for p in range(2):
                        sp.wait_ge(out_in_psum, SEQS * (2 * i + p + 1))
                        sp.dma_start(w[:, p, :], w_dram[bass.ts(2 * i + p + 2, 1)].rearrange("a p n -> p (a n)"))\
                          .then_inc(w_loaded[p], 16)

            @block.tensor
            def _(pe):
                run(pe, pe_work, pe_front)

            @block.vector
            def _(dve):
                with dve.Fori(0, GROUPS) as g:
                    norm_statistics(k, dve, outer, g, lambda j: x[:, bass.ts(S * T * g + j, 1), :])
                    norm_apply(k, dve, outer, g, lambda j: y_tile(g, j),
                               lambda j: x[:, bass.ts(S * T * g + j, 1), :], (y_ready, S))
                run(dve, dve_work, dve_front)
                dve.wait_ge(y_ready, SEQS * (LAYERS + 1))
                with dve.Fori(0, GROUPS) as g:
                    rows = bass.ts(g, S * T)
                    nc.vector.tensor_tensor(x[:, rows, :], x[:, rows, :], y[:, rows, :], ALU.add)

            @block.scalar
            def _(act):
                run(act, act_work, act_front)

            @block.gpsimd
            def _(pool):
                with pool.Fori(0, GROUPS) as g:
                    norm_rstd(k, pool, outer, g)
                run(pool, pool_work, pool_front)


SSM_INNER, SSM_STATE, SSM_RANK, SSM_TAPS = 256, 16, 16, 4


def state_space_stage(k, name="ssm"):
    nc, psum, x = k.nc, k.psum, k.x
    GT = 4
    GROUPS = TILES // GT
    W = GT * P
    GS = W // SEQ_LEN
    C = SSM_INNER // P
    N = SSM_STATE
    PAD = SSM_TAPS - 1
    w_in, w_x, w_dt, w_out = k.const["ssm_win"], k.const["ssm_wx"], k.const["ssm_wdt"], k.const["ssm_wout"]
    taps, conv_b, b_dt, skip = k.const["ssm_taps"], k.const["ssm_convb"], k.const["ssm_bdt"], k.const["ssm_d"]
    a_log, pick = k.const["ssm_alog"], k.const["ssm_pick"]

    with ExitStack() as mem:
        def sb(n, shape, dtype=FP32):
            return k.sbuf(f"{name}_{n}", shape, dtype, mem)

        A = sb("A", [P, C, N])
        h = sb("h", [P, GT, P])
        hT = sb("hT", [P, W])
        padded = sb("padded", [P, C, GS, PAD + SEQ_LEN])
        conv = sb("conv", [P, C, GS, SEQ_LEN])
        u_act = sb("u_act", [P, 2, C, W])
        z_act = sb("z_act", [P, 2, C, W])
        bc = sb("bc", [P, 2, W], BF16)
        high = sb("high", [P, W], BF16)
        rest = sb("rest", [P, W])
        dt_low = sb("dt_low", [SSM_RANK, W])
        soft_abs = sb("soft_abs", [P, C, W])
        soft_exp = sb("soft_exp", [P, C, W])
        soft_ln = sb("soft_ln", [P, C, W])
        soft_pos = sb("soft_pos", [P, C, W])
        dt = sb("dt", [P, 2, C, W])
        dtu = sb("dtu", [P, 2, C, W])
        decay = sb("decay", [P, 2, C, W])
        drive = sb("drive", [P, 2, C, W])
        state = sb("state", [P, 2, C, W])
        c_row = sb("c_row", [P, 2, W])
        read = sb("read", [P, 2, C, W])
        gated = sb("gated", [P, C, W])
        norm = add_norm_buffers(k, f"{name}_norm", f"{name}_norm", GT, mem)

        A_exp_ready = k.sem(f"{name}_A_exp_ready")
        A_ready = k.sem(f"{name}_A_ready")
        padding_zero = k.sem(f"{name}_padding_zero")
        h_ready = k.sem(f"{name}_h_ready")
        hT_in_psum = k.sem(f"{name}_hT_in_psum")
        hT_ready = k.sem(f"{name}_hT_ready")
        xin_in_psum = k.sem(f"{name}_xin_in_psum")
        xin_ready = k.sem(f"{name}_xin_ready")
        z_in_psum = k.sem(f"{name}_z_in_psum")
        conv_steps = k.sem(f"{name}_conv_steps")
        u_ready = k.sem(f"{name}_u_ready")
        xdbl_in_psum = k.sem(f"{name}_xdbl_in_psum")
        split_steps = k.sem(f"{name}_split_steps")
        bc_ready = k.sem(f"{name}_bc_ready")
        dt_in_psum = k.sem(f"{name}_dt_in_psum")
        soft_steps = k.sem(f"{name}_soft_steps")
        soft_ready = k.sem(f"{name}_soft_ready")
        dt_ready = k.sem(f"{name}_dt_ready")
        dtu_ready = k.sem(f"{name}_dtu_ready")
        rows_in_psum = k.sem(f"{name}_rows_in_psum")
        decay_ready = k.sem(f"{name}_decay_ready")
        c_ready = k.sem(f"{name}_c_ready")
        drive_ready = k.sem(f"{name}_drive_ready")
        state_ready = k.sem(f"{name}_state_ready")
        read_ready = k.sem(f"{name}_read_ready")
        y_in_psum = k.sem(f"{name}_y_in_psum")
        y_left = k.sem(f"{name}_y_left")
        gated_ready = k.sem(f"{name}_gated_ready")
        out_in_psum = k.sem(f"{name}_out_in_psum")
        x_done = k.sem(f"{name}_x_done")

        def b_bank(n): return psum[:, n % 2, :]
        def c_bank(n): return psum[:, 2 + n % 2, :]
        def y_bank(c): return psum[:, 4 + c, :]
        FA, FB = psum[:, 6, :], psum[:, 7, :]

        def run(eng, work, front, finish):
            for n in range(N):
                front(eng, n, 0, 0)
            work(eng, 0, 0, 1, None)
            work(eng, 1, 1, 2, 0)
            with eng.Fori(1, GROUPS // 2 - 1) as i:
                work(eng, 2 * i, 0, 2 * i + 1, 2 * i - 1)
                work(eng, 2 * i + 1, 1, 2 * i + 2, 2 * i)
            work(eng, GROUPS - 2, 0, GROUPS - 1, GROUPS - 3)
            work(eng, GROUPS - 1, 1, None, GROUPS - 2)
            for n in range(2):
                finish(eng, n, GROUPS - 1, 1)

        def pe_front(pe, n, t, u):
            if n == 3:
                pe.wait_ge(h_ready, t + 1)
                for j in range(GT):
                    last = nc.tensor.transpose(FA[:, j * P:(j + 1) * P], h[:, j, :], k.ident[:])
                last.then_inc(hT_in_psum, 1)
            if n == 4:
                pe.wait_ge(hT_ready, t + 1)
                for c, bank in enumerate((FA, FB)):
                    last = nc.tensor.matmul(bank, w_in[:, c * P:(c + 1) * P], hT[:], start=True, stop=True)
                last.then_inc(xin_in_psum, 1)
            if n == 5:
                pe.wait_ge(xin_ready, t + 1)
                for c, bank in enumerate((FA, FB)):
                    last = nc.tensor.matmul(bank, w_in[:, (C + c) * P:(C + c + 1) * P], hT[:], start=True, stop=True)
                last.then_inc(z_in_psum, 1)
            if n == 9:
                pe.wait_ge(u_ready, t + 1)
                for c in range(C):
                    last = nc.tensor.matmul(FA, w_x[:, c, :], u_act[:, u, c, :], start=(c == 0), stop=(c == C - 1))
                last.then_inc(xdbl_in_psum, 1)
            if n == 11:
                pe.wait_ge(bc_ready, t + 1)
                for c, bank in enumerate((FA, FB)):
                    last = nc.tensor.matmul(bank, w_dt[:, c * P:(c + 1) * P], dt_low[:], start=True, stop=True)
                last.then_inc(dt_in_psum, 1)

        def rows(t, u, n):
            nc.tensor.matmul(b_bank(n), pick[:, n, :], bc[:, u, :], start=True, stop=True)
            nc.tensor.matmul(c_bank(n), pick[:, N + n, :], bc[:, u, :], start=True, stop=True).then_inc(rows_in_psum, 1)

        def pe_finish(pe, n, t, u):
            if n == 1:
                pe.wait_ge(gated_ready, t + 1)
                for j in range(GT):
                    for c in range(C):
                        last = nc.tensor.matmul(FA[:, j * P:(j + 1) * P], gated[:, c, j * P:(j + 1) * P],
                                                w_out[:, c, :], start=(c == 0), stop=(c == C - 1))
                last.then_inc(out_in_psum, 1)

        def pe_work(pe, t, u, nxt, prev):
            pe.wait_ge(bc_ready, t + 1)
            rows(t, u, 0)
            rows(t, u, 1)
            for n in range(N):
                pe.wait_ge(read_ready, N * t + n + 1)
                if n == 0 and prev is not None:
                    pe.wait_ge(y_left, prev + 1)
                for c in range(C):
                    last = nc.tensor.matmul(y_bank(c), k.ident[:], read[:, n % 2, c, :],
                                            start=(n == 0), stop=(n == N - 1))
                if n == N - 1:
                    last.then_inc(y_in_psum, 1)
                if n + 2 < N:
                    rows(t, u, n + 2)
                if prev is not None:
                    pe_finish(pe, n, prev, 1 - u)
                if nxt is not None:
                    pe_front(pe, n, nxt, 1 - u)

        def dve_front(dve, n, t, u):
            def tile(j): return x[:, bass.ts(GT * t + j, 1), :]
            if n == 2:
                norm_statistics(k, dve, norm, t, tile)
            if n == 3:
                norm_apply(k, dve, norm, t, lambda j: h[:, j:j + 1, :], tile, (h_ready, 1))
            if 5 <= n < 5 + SSM_TAPS:
                tap = n - 5
                if tap == 0:
                    dve.wait_ge(xin_ready, t + 1)
                for c in range(C):
                    src = padded[:, c, :, tap:tap + SEQ_LEN]
                    if tap == 0:
                        nc.vector.tensor_scalar(conv[:, c], src, taps[:, c, 0:1], conv_b[:, c:c + 1],
                                                ALU.mult, ALU.add).then_inc(conv_steps, 1)
                    else:
                        dve.wait_ge(conv_steps, C * SSM_TAPS * t + C * (tap - 1) + c + 1)
                        nc.vector.scalar_tensor_tensor(conv[:, c], src, taps[:, c, tap:tap + 1], conv[:, c],
                                                       ALU.mult, ALU.add).then_inc(conv_steps, 1)
            if n == 10:
                dve.wait_ge(xdbl_in_psum, t + 1)
                nc.vector.tensor_copy(high[64:P, :], FA[64:P, :]).then_inc(split_steps, 1)
                nc.vector.tensor_copy(dt_low[:], FA[0:SSM_RANK, :])
                nc.vector.tensor_copy(bc[0:64, u, :], FA[0:64, :])
                dve.wait_ge(split_steps, 3 * t + 1)
                nc.vector.tensor_tensor(rest[64:P, :], FA[64:P, :], high[64:P, :], ALU.subtract).then_inc(split_steps, 1)
                dve.wait_ge(split_steps, 3 * t + 2)
                nc.vector.tensor_copy(high[96:P, :], rest[96:P, :]).then_inc(split_steps, 1)
                nc.vector.tensor_copy(bc[64:96, u, :], rest[64:96, :])
                dve.wait_ge(split_steps, 3 * t + 3)
                nc.vector.tensor_tensor(bc[96:P, u, :], rest[96:P, :], high[96:P, :], ALU.subtract).then_inc(bc_ready, 1)
            if n == 13:
                dve.wait_ge(soft_ready, t + 1)
                nc.vector.tensor_tensor(dt[:, u], soft_ln[:], soft_pos[:], ALU.add).then_inc(dt_ready, 1)
                dve.wait_ge(dt_ready, t + 1)
                nc.vector.tensor_tensor(dtu[:, u], dt[:, u], u_act[:, u], ALU.mult).then_inc(dtu_ready, 1)

        def dve_finish(dve, n, t, u):
            if n == 0:
                dve.wait_ge(y_in_psum, t + 1)
                for c in range(C):
                    last = nc.vector.scalar_tensor_tensor(gated[:, c, :], u_act[:, u, c, :], skip[:, c:c + 1],
                                                          y_bank(c), ALU.mult, ALU.add)
                last.then_inc(y_left, 1)
                dve.wait_ge(y_left, t + 1)
                nc.vector.tensor_tensor(gated[:], gated[:], z_act[:, u], ALU.mult).then_inc(gated_ready, 1)
            if n == 1:
                dve.wait_ge(out_in_psum, t + 1)
                group = x[:, bass.ts(t, GT), :]
                nc.vector.tensor_tensor(group, FA.rearrange("p (j f) -> p j f", f=DIM), group, ALU.add).then_inc(x_done, 1)

        def dve_work(dve, t, u, nxt, prev):
            dve.wait_ge(dtu_ready, t + 1)
            for n in range(N):
                s = n % 2
                dve.wait_ge(rows_in_psum, N * t + n + 1)
                for c in range(C):
                    last = nc.vector.tensor_tensor(drive[:, s, c, :], dtu[:, u, c, :], b_bank(n), ALU.mult)
                last.then_inc(drive_ready, 1)
                dve.wait_ge(drive_ready, N * t + n + 1)
                dve.wait_ge(decay_ready, N * t + n + 1)
                for c in range(C):
                    for q in range(GS):
                        seq = slice(q * SEQ_LEN, (q + 1) * SEQ_LEN)
                        last = nc.vector.tensor_tensor_scan(state[:, s, c, seq], decay[:, s, c, seq],
                                                            drive[:, s, c, seq], 0.0, ALU.mult, ALU.add)
                last.then_inc(state_ready, 1)
                if prev is not None:
                    dve_finish(dve, n, prev, 1 - u)
                if nxt is not None:
                    dve_front(dve, n, nxt, 1 - u)

        def act_front(act, n, t, u):
            if n == 3:
                act.wait_ge(hT_in_psum, t + 1)
                nc.scalar.activation(hT[:], FA, ACT.Copy).then_inc(hT_ready, 1)
            if n == 4:
                act.wait_ge(xin_in_psum, t + 1)
                for c, bank in enumerate((FA, FB)):
                    last = nc.scalar.activation(padded[:, c, :, PAD:PAD + SEQ_LEN],
                                                bank.rearrange("p (q l) -> p q l", l=SEQ_LEN), ACT.Copy)
                last.then_inc(xin_ready, 1)
            if n == 8:
                act.wait_ge(z_in_psum, t + 1)
                for c, bank in enumerate((FA, FB)):
                    nc.scalar.activation(z_act[:, u, c, :], bank, ACT.Silu)
                act.wait_ge(conv_steps, C * SSM_TAPS * (t + 1))
                nc.scalar.activation(u_act[:, u], conv[:].rearrange("p c q l -> p c (q l)"), ACT.Silu).then_inc(u_ready, 1)
            if n == 11:
                act.wait_ge(dt_in_psum, t + 1)
                for c, bank in enumerate((FA, FB)):
                    nc.scalar.activation(soft_pos[:, c, :], bank, ACT.Relu, bias=b_dt[:, c:c + 1])
                    last = nc.scalar.activation(soft_abs[:, c, :], bank, ACT.Abs, bias=b_dt[:, c:c + 1])
                last.then_inc(soft_steps, 1)
            if n == 12:
                act.wait_ge(soft_steps, 2 * t + 1)
                nc.scalar.activation(soft_exp[:], soft_abs[:], ACT.Exp, scale=-1.0).then_inc(soft_steps, 1)
                act.wait_ge(soft_steps, 2 * t + 2)
                nc.scalar.activation(soft_ln[:], soft_exp[:], ACT.Ln, bias=1.0).then_inc(soft_ready, 1)

        def act_work(act, t, u, nxt, prev):
            act.wait_ge(dt_ready, t + 1)
            for n in range(N):
                s = n % 2
                act.wait_ge(rows_in_psum, N * t + n + 1)
                for c in range(C):
                    last = nc.scalar.activation(decay[:, s, c, :], dt[:, u, c, :], ACT.Exp, scale=A[:, c, n:n + 1])
                last.then_inc(decay_ready, 1)
                nc.scalar.activation(c_row[:, s, :], c_bank(n), ACT.Copy).then_inc(c_ready, 1)
                if nxt is not None:
                    act_front(act, n, nxt, 1 - u)

        def pool_front(pool, n, t, u):
            if n == 2:
                norm_rstd(k, pool, norm, t)

        def pool_work(pool, t, u, nxt, prev):
            for n in range(N):
                s = n % 2
                pool.wait_ge(state_ready, N * t + n + 1)
                pool.wait_ge(c_ready, N * t + n + 1)
                nc.gpsimd.tensor_tensor(read[:, s], state[:, s],
                                        c_row[:, s:s + 1, :].broadcast_to([P, C, W]), ALU.mult).then_inc(read_ready, 1)
                if nxt is not None:
                    pool_front(pool, n, nxt, 1 - u)

        def nothing(eng, n, t, u):
            pass

        with nc.Block() as block:
            @block.tensor
            def _(pe):
                run(pe, pe_work, pe_front, pe_finish)

            @block.vector
            def _(dve):
                nc.vector.memset(padded[:], 0.0).then_inc(padding_zero, 1)
                dve.wait_ge(A_exp_ready, 1)
                nc.vector.tensor_scalar(A[:], A[:], -1.0, None, ALU.mult).then_inc(A_ready, 1)
                run(dve, dve_work, dve_front, dve_finish)

            @block.scalar
            def _(act):
                nc.scalar.activation(A[:], a_log[:], ACT.Exp).then_inc(A_exp_ready, 1)
                act.wait_ge(A_ready, 1)
                act.wait_ge(padding_zero, 1)
                run(act, act_work, act_front, nothing)

            @block.gpsimd
            def _(pool):
                run(pool, pool_work, pool_front, nothing)


HEADS, HEAD_DIM, WINDOW = 8, 64, 64
INNER = HEADS * HEAD_DIM
HID_CHUNKS = 3
MASKED = -1e30


def local_attention_stage(k, name):
    nc, psum, x, y = k.nc, k.psum, k.x, k.y
    T = SEQ_LEN // P
    LAYERS = k.dram["loc_wa"].shape[0]
    HP = HEADS // 2
    HALF = HP // 2
    STEPS = 4
    QK = 2 * INNER
    GT = 4
    FGROUPS = TILES // GT
    GS = GT // T
    cos, sin, scale, scale_swapped = (k.const[f"loc_{n}"] for n in ("cos", "sin", "scale", "scale_swapped"))
    mask, ident_bf = k.const["loc_mask"], k.const["loc_ident"]
    ln_g, ln_b, b1, b2 = (k.const[f"loc_{n}"] for n in ("lng", "lnb", "b1", "b2"))

    with ExitStack() as mem:
        def sb(n, shape, dtype=FP32):
            return k.sbuf(f"{name}_{n}", shape, dtype, mem)

        rows_a = sb("rows_a", [P, 2, T, DIM])
        rows_f = sb("rows_f", [P, 2, GT, DIM])
        wa = sb("wa", [P, 3 * INNER + HP * DIM])
        w_qkv, w_o = wa[:, 0:3 * INNER], wa[:, 3 * INNER:].rearrange("p (c n) -> p c n", n=DIM)
        wf = sb("wf", [P, 2 * HID_CHUNKS * P + HID_CHUNKS * DIM])
        w_1 = wf[:, 0:2 * HID_CHUNKS * P].rearrange("p (c n) -> p c n", n=P)
        w_2 = wf[:, 2 * HID_CHUNKS * P:].rearrange("p (c n) -> p c n", n=DIM)
        rot_cos = sb("rot_cos", [P, LAYERS * T, 2, HEAD_DIM])
        rot_sin = sb("rot_sin", [P, LAYERS * T, 2, HEAD_DIM])
        hT = sb("hT", [P, SEQ_LEN])
        square = sb("square", [P, QK])
        ss = sb("ss", [P, 2 * HEADS])
        ss_guard = sb("ss_guard", [P, 2 * HEADS])
        inv_norm = sb("inv_norm", [P, 2 * HEADS])
        unit_qk = sb("unit_qk", [P, QK])
        by_cos = sb("by_cos", [P, QK])
        by_sin = sb("by_sin", [P, QK])
        qk = sb("qk", [P, QK])
        qT = sb("qT", [P, 2, HP, SEQ_LEN])
        kT = sb("kT", [P, 2, HP, SEQ_LEN])
        v = sb("v", [P, 2, T, INNER])
        v_mid = sb("v_mid", [P, 2, INNER])
        top = sb("top", [P, 2, STEPS])
        shifted = sb("shifted", [P, 2, 512])
        prob = sb("prob", [P, 2, 512])
        total = sb("total", [P, 2, STEPS])
        inv_total = sb("inv_total", [P, 2, STEPS])
        prob_n = sb("prob_n", [P, 2, 512])
        prob_T = sb("prob_T", [P, 2, 512])
        oT = sb("oT", [P, HP, SEQ_LEN])
        fh = sb("fh", [P, GT, P])
        fhT = sb("fhT", [P, 2, GT * P])
        gelu = sb("gelu", [P, HID_CHUNKS, GT * P])
        hid = sb("hid", [P, HID_CHUNKS, GT * P])
        outer = add_norm_buffers(k, f"{name}_outer", "loc_outer", 2 * GT, mem)
        inner = add_norm_buffers(k, f"{name}_inner", "loc_inner", GT, mem)

        def sem(n):
            return k.sem(f"loc_{n}")
        tables_steps, wa_loaded, wf_loaded, edge_zero = sem("tables_steps"), sem("wa_loaded"), sem("wf_loaded"), sem("edge_zero")
        y_for_attn, y_for_ffn = sem("y_for_attn"), sem("y_for_ffn")
        sh_for_attn = [sem(f"sh_for_attn{u}") for u in range(2)]
        sh_for_ffn = [sem(f"sh_for_ffn{u}") for u in range(2)]
        hT_in_psum, hT_ready = sem("hT_in_psum"), sem("hT_ready")
        qk_in_psum, v_in_psum = sem("qk_in_psum"), sem("v_in_psum")
        square_ready, v_ready = sem("square_ready"), sem("v_ready")
        ss_ready, guard_ready, inv_norm_ready = sem("ss_ready"), sem("guard_ready"), sem("inv_norm_ready")
        unit_ready, by_cos_ready, by_sin_ready, rot_ready = sem("unit_ready"), sem("by_cos_ready"), sem("by_sin_ready"), sem("rot_ready")
        qkT_in_psum, qkT_ready = sem("qkT_in_psum"), sem("qkT_ready")
        scores_in_psum, top_ready, shifted_ready = sem("scores_in_psum"), sem("top_ready"), sem("shifted_ready")
        prob_ready, total_ready, inv_total_ready = sem("prob_ready"), sem("total_ready"), sem("inv_total_ready")
        prob_n_ready, prob_T_in_psum, prob_T_ready = sem("prob_n_ready"), sem("prob_T_in_psum"), sem("prob_T_ready")
        oT_in_psum, oT_ready, attn_in_psum = sem("oT_in_psum"), sem("oT_ready"), sem("attn_in_psum")
        fh_ready, fhT_in_psum, fhT_ready = sem("fh_ready"), sem("fhT_in_psum"), sem("fhT_ready")
        up_done, gelu_ready, hid_ready = sem("up_done"), sem("gelu_ready"), sem("hid_ready")
        ffn_in_psum, bias_added = sem("ffn_in_psum"), sem("bias_added")

        QK_BANKS = psum[:, 0:2, :]
        V_BANK = psum[:, 2, :]
        HT = psum[:, 3, 0:SEQ_LEN]
        ATTN = psum[:, 3, SEQ_LEN:2 * SEQ_LEN]
        PT_BANK = psum[:, 6, :]
        OT_BANK = psum[:, 7, :]

        def score_bank(e):
            return psum[:, 4 + e, :]

        def run_attention(eng, l, work, front):
            for step in range(FRONT_STEPS):
                front(eng, step, l, 0, 0, None)
            with eng.Fori(0, SEQS // 2 - 1) as i:
                work(eng, l, 2 * i, 0, 2 * i + 1, i)
                work(eng, l, 2 * i + 1, 1, 2 * i + 2, i + 1)
            work(eng, l, SEQS - 2, 0, SEQS - 1, SEQS // 2 - 1)
            work(eng, l, SEQS - 1, 1, None, None)
        FRONT_STEPS = 5

        def seq(l, t):
            return SEQS * l + t


        START = 1
        FREE = 2

        def half_of(a): return a // 2
        def parity_of(a): return a % 2

        def pe_front(pe, step, l, t, u, pair):
            if step == 0:
                pe.wait_ge(sh_for_attn[u], 48 * (SEQS // 2 * l + (0 if pair is None else pair) + 1))
                if pair is not None:
                    pe.wait_ge(y_for_ffn, START + seq(l, t) - 1)
                for j in range(T):
                    last = nc.tensor.transpose(HT[:, j * P:(j + 1) * P], rows_a[:, u, j, :], k.ident[:])
                last.then_inc(hT_in_psum, 1)
            if step in (1, 3):
                j = step // 2
                if j == 0:
                    pe.wait_ge(hT_ready, seq(l, t) + 1)
                pe.wait_ge(qkT_ready, START + T * seq(l, t) + j)
                lhs = hT[:, j * P:(j + 1) * P]
                for b in range(2):
                    last = nc.tensor.matmul(QK_BANKS[:, b, :], lhs, w_qkv[:, b * INNER:(b + 1) * INNER],
                                            start=True, stop=True)
                last.then_inc(qk_in_psum, 1)
                pe.wait_ge(v_ready, START + T * seq(l, t) + j)
                nc.tensor.matmul(V_BANK, lhs, w_qkv[:, QK:QK + INNER], start=True, stop=True).then_inc(v_in_psum, 1)
            if step in (2, 4):
                j = step // 2 - 1
                pe.wait_ge(rot_ready, T * seq(l, t) + j + 1)
                for b in range(2):
                    for c in range(HP):
                        last = nc.tensor.transpose(QK_BANKS[:, b, c * P:(c + 1) * P],
                                                   qk[:, b * INNER + c * P:b * INNER + (c + 1) * P], k.ident[:])
                last.then_inc(qkT_in_psum, 1)

        def scores(u, half):
            for e in range(2):
                last = nc.tensor.matmul(score_bank(e), ident_bf[:], mask[:], start=True, stop=False,
                                        skip_group_check=True)
            for c in range(HALF):
                for w in range(SEQ_LEN // WINDOW):
                    rows = slice(WINDOW * (w % 2), WINDOW * (w % 2) + WINDOW)
                    col = (c * 2 + w // 2) * P
                    if w == 2:
                        parts = [(col, w * WINDOW, WINDOW), (col + WINDOW, (w - 1) * WINDOW, WINDOW)]
                    else:
                        parts = [(col, (w // 2) * P, P)]
                    for at, key, n in parts:
                        for e in range(2):
                            d = slice(HEAD_DIM * e, HEAD_DIM * (e + 1))
                            last = nc.tensor.matmul(score_bank(e)[rows, at:at + n],
                                                    qT[d, u, HALF * half + c, w * WINDOW:(w + 1) * WINDOW],
                                                    kT[d, u, HALF * half + c, key:key + n],
                                                    start=False, stop=True, skip_group_check=True)
            last.then_inc(scores_in_psum, 1)

        def weighted(pe, l, t, u, a):
            half, e = half_of(a), parity_of(a)
            idx = STEPS * seq(l, t) + a
            pe.wait_ge(prob_n_ready, idx + 1)
            for i in range(4):
                last = nc.tensor.transpose(PT_BANK[:, i * P:(i + 1) * P], prob_n[:, a % 2, i * P:(i + 1) * P], k.ident[:])
            last.then_inc(prob_T_in_psum, 1)
            if e == 0:
                pe.wait_ge(oT_ready, START + 2 * seq(l, t) + half)
            pe.wait_ge(prob_T_ready, idx + 1)
            for c in range(HALF):
                head = 2 * (HALF * half + c) + e
                d = slice(HEAD_DIM * head, HEAD_DIM * (head + 1))
                out = OT_BANK[HEAD_DIM * e:HEAD_DIM * (e + 1), c * SEQ_LEN:(c + 1) * SEQ_LEN]
                p0 = prob_T[:, a % 2, 2 * c * P:(2 * c + 1) * P]
                p1 = prob_T[:, a % 2, (2 * c + 1) * P:(2 * c + 2) * P]
                nc.tensor.matmul(out[:, 0:P], v[:, u, 0, d], p0, start=True, stop=True)
                nc.tensor.matmul(out[:, P:P + WINDOW], v_mid[:, u, d], p1[:, 0:WINDOW], start=True, stop=True)
                last = nc.tensor.matmul(out[:, P + WINDOW:2 * P], v[:, u, 1, d], p1[:, WINDOW:P], start=True, stop=True)
            last.then_inc(oT_in_psum, 1)

        def attention_out(pe, l, t):
            pe.wait_ge(oT_ready, START + 2 * seq(l, t) + 2)
            for j in range(T):
                for c in range(HP):
                    last = nc.tensor.matmul(ATTN[:, j * P:(j + 1) * P], oT[:, c, j * P:(j + 1) * P], w_o[:, c, :],
                                            start=(c == 0), stop=(c == HP - 1))
            last.then_inc(attn_in_psum, 1)

        def pe_attention(pe, l, t, u, nxt, pair):
            def front(step):
                if nxt is not None:
                    pe_front(pe, step, l, nxt, 1 - u, pair)
            pe.wait_ge(qkT_ready, START + T * (seq(l, t) + 1))
            scores(u, 0)
            front(0)
            front(1)
            pe.wait_ge(v_ready, START + T * (seq(l, t) + 1))
            weighted(pe, l, t, u, 0)
            weighted(pe, l, t, u, 1)
            scores(u, 1)
            front(2)
            front(3)
            weighted(pe, l, t, u, 2)
            weighted(pe, l, t, u, 3)
            attention_out(pe, l, t)
            front(4)

        def heads(ap):
            return ap.rearrange("p (s h d) -> p s h d", s=2, d=HEAD_DIM)

        def table(tab, l, j, cols=slice(0, HEAD_DIM)):
            one = tab[:, bass.ts(T * l + j, 1), :, cols].rearrange("p a s d -> p (a s) d")
            return one.unsqueeze(2).broadcast_to([P, 2, HEADS, cols.stop - cols.start])

        def dve_front(dve, step, l, t, u, pair):
            if step in (2, 4):
                j = step // 2 - 1
                i = T * seq(l, t) + j
                dve.wait_ge(square_ready, i + 1)
                nc.vector.tensor_reduce(ss[:], square[:].rearrange("p (h d) -> p h d", d=HEAD_DIM), AX.X,
                                        ALU.add).then_inc(ss_ready, 1)
                dve.wait_ge(ss_ready, i + 1)
                nc.vector.tensor_scalar(ss_guard[:], ss[:], 1e-24, None, ALU.max).then_inc(guard_ready, 1)
                dve.wait_ge(inv_norm_ready, i + 1)
                nc.vector.tensor_tensor(unit_qk[:].rearrange("p (h d) -> p h d", d=HEAD_DIM),
                                        QK_BANKS.rearrange("p b (h d) -> p (b h) d", d=HEAD_DIM),
                                        inv_norm[:].unsqueeze(2).broadcast_to([P, 2 * HEADS, HEAD_DIM]),
                                        ALU.mult).then_inc(unit_ready, 1)
                dve.wait_ge(unit_ready, i + 1)
                nc.vector.tensor_tensor(heads(by_cos[:]), heads(unit_qk[:]), table(rot_cos, l, j),
                                        ALU.mult).then_inc(by_cos_ready, 1)
                dve.wait_ge(by_cos_ready, i + 1)
                dve.wait_ge(by_sin_ready, i + 1)
                nc.vector.tensor_tensor(qk[:], by_cos[:], by_sin[:], ALU.add).then_inc(rot_ready, 1)

        def dve_shift(dve, l, t, a):
            idx = STEPS * seq(l, t) + a
            bank = score_bank(a % 2).rearrange("p (g c) -> p g c", c=P)
            dve.wait_ge(scores_in_psum, 2 * seq(l, t) + a // 2 + 1)
            nc.vector.tensor_reduce(top[:, a % 2, :], bank, AX.X, ALU.max).then_inc(top_ready, 1)
            dve.wait_ge(top_ready, idx + 1)
            nc.vector.tensor_tensor(shifted[:, a % 2, :].rearrange("p (g c) -> p g c", c=P), bank,
                                    top[:, a % 2, :].unsqueeze(2).broadcast_to([P, STEPS, P]),
                                    ALU.subtract).then_inc(shifted_ready, 1)

        def dve_total(dve, l, t, a):
            idx = STEPS * seq(l, t) + a
            dve.wait_ge(prob_ready, idx + 1)
            nc.vector.tensor_reduce(total[:, a % 2, :], prob[:, a % 2, :].rearrange("p (g c) -> p g c", c=P), AX.X,
                                    ALU.add).then_inc(total_ready, 1)
            dve.wait_ge(total_ready, idx + 1)
            nc.vector.reciprocal(inv_total[:, a % 2, :], total[:, a % 2, :]).then_inc(inv_total_ready, 1)

        def dve_attention(dve, l, t, u, nxt, pair):
            for half in range(2):
                for a in (2 * half, 2 * half + 1):
                    dve_shift(dve, l, t, a)
                for a in (2 * half, 2 * half + 1):
                    dve_total(dve, l, t, a)
                if nxt is not None:
                    dve_front(dve, 2 * half + 2, l, nxt, 1 - u, pair)
            dve.wait_ge(attn_in_psum, START + seq(l, t) + 1)
            rows = y[:, bass.ts(t, T), :]
            nc.vector.tensor_tensor(rows, ATTN.rearrange("p (j f) -> p j f", f=DIM), rows,
                                    ALU.add).then_inc(y_for_ffn, 1)

        def act_front(act, step, l, t, u, pair):
            if step == 0:
                act.wait_ge(hT_in_psum, seq(l, t) + 1 + FREE)
                nc.scalar.activation(hT[:], HT, ACT.Copy).then_inc(hT_ready, 1)
            if step in (1, 3):
                i = T * seq(l, t) + step // 2
                act.wait_ge(qk_in_psum, i + 1)
                nc.scalar.activation(square[:], QK_BANKS.rearrange("p b n -> p (b n)"), ACT.Square).then_inc(square_ready, 1)
                act.wait_ge(v_in_psum, i + 1)
                half = slice(64, P) if step == 1 else slice(0, 64)
                nc.scalar.activation(v_mid[half, u, :], V_BANK[half, :], ACT.Copy)
                nc.scalar.activation(v[:, u, step // 2, :], V_BANK, ACT.Copy).then_inc(v_ready, 1)
            if step in (2, 4):
                j = step // 2 - 1
                act.wait_ge(qkT_in_psum, T * seq(l, t) + j + 1)
                for b, dst in enumerate((qT, kT)):
                    last = nc.scalar.activation(dst[:, u, :, j * P:(j + 1) * P],
                                                QK_BANKS[:, b, :].rearrange("p (c n) -> p c n", n=P), ACT.Copy)
                last.then_inc(qkT_ready, 1)

        def act_exp(act, l, t, a):
            act.wait_ge(shifted_ready, STEPS * seq(l, t) + a + 1)
            nc.scalar.activation(prob[:, a % 2, :], shifted[:, a % 2, :], ACT.Exp).then_inc(prob_ready, 1)

        def act_prob_T(act, l, t, a):
            act.wait_ge(prob_T_in_psum, STEPS * seq(l, t) + a + 1)
            nc.scalar.activation(prob_T[:, a % 2, :], PT_BANK, ACT.Copy).then_inc(prob_T_ready, 1)

        def act_oT(act, l, t, half):
            act.wait_ge(oT_in_psum, STEPS * seq(l, t) + 2 * half + 2)
            nc.scalar.activation(oT[:, HALF * half:HALF * (half + 1), :],
                                 OT_BANK.rearrange("p (c n) -> p c n", n=SEQ_LEN), ACT.Copy).then_inc(oT_ready, 1)

        def act_attention(act, l, t, u, nxt, pair):
            def front(step):
                if nxt is not None:
                    act_front(act, step, l, nxt, 1 - u, pair)
            act_exp(act, l, t, 0)
            act_exp(act, l, t, 1)
            front(0)
            front(1)
            act_prob_T(act, l, t, 0)
            act_prob_T(act, l, t, 1)
            act_oT(act, l, t, 0)
            front(2)
            front(3)
            act_exp(act, l, t, 2)
            act_exp(act, l, t, 3)
            act_prob_T(act, l, t, 2)
            act_prob_T(act, l, t, 3)
            act_oT(act, l, t, 1)
            front(4)

        def pool_front(pool, step, l, t, u, pair):
            if step in (2, 4):
                j = step // 2 - 1
                i = T * seq(l, t) + j
                pool.wait_ge(guard_ready, i + 1)
                nc.gpsimd.tensor_tensor(inv_norm[:], ss_guard[:], k.neg_half[:, 0:2 * HEADS], ALU.pow)\
                  .then_inc(inv_norm_ready, 1)
                settle(pool, unit_ready, i + 1)
                H = HEAD_DIM // 2
                lo, hi = slice(0, H), slice(H, HEAD_DIM)
                nc.gpsimd.tensor_tensor(heads(by_sin[:])[:, :, :, lo], heads(unit_qk[:])[:, :, :, hi],
                                        table(rot_sin, l, j, lo), ALU.mult)
                nc.gpsimd.tensor_tensor(heads(by_sin[:])[:, :, :, hi], heads(unit_qk[:])[:, :, :, lo],
                                        table(rot_sin, l, j, hi), ALU.mult).then_inc(by_sin_ready, 1)

        def pool_attention(pool, l, t, u, nxt, pair):
            for half in range(2):
                for a in (2 * half, 2 * half + 1):
                    idx = STEPS * seq(l, t) + a
                    pool.wait_ge(inv_total_ready, idx + 1)
                    nc.gpsimd.tensor_tensor(prob_n[:, a % 2, :].rearrange("p (g c) -> p g c", c=P),
                                            prob[:, a % 2, :].rearrange("p (g c) -> p g c", c=P),
                                            inv_total[:, a % 2, :].unsqueeze(2).broadcast_to([P, STEPS, P]),
                                            ALU.mult).then_inc(prob_n_ready, 1)
                if nxt is not None:
                    pool_front(pool, 2 * half + 2, l, nxt, 1 - u, pair)

        def a_bank(c): return psum[:, 2 * c, :]
        def g_bank(c): return psum[:, 2 * c + 1, :]
        F_OUT, F_HT = psum[:, 6, :], psum[:, 7, :]
        C = HID_CHUNKS

        def group(l, g):
            return FGROUPS * l + g

        def run_ffn(eng, l, work):
            work(eng, l, None, None, 0, 0, 0)
            with eng.Fori(0, FGROUPS // 2 - 1) as i:
                work(eng, l, 2 * i, 0, 2 * i + 1, 1, i)
                work(eng, l, 2 * i + 1, 1, 2 * i + 2, 0, i + 1)
            work(eng, l, FGROUPS - 2, 0, FGROUPS - 1, 1, FGROUPS // 2 - 1)
            work(eng, l, FGROUPS - 1, 1, None, None, None)

        def pe_ffn(pe, l, g, u, n, un, pair):
            def up(c):
                nc.tensor.matmul(a_bank(c), w_1[:, c, :], fhT[:, u, :], start=True, stop=True)
                nc.tensor.matmul(g_bank(c), w_1[:, C + c, :], fhT[:, u, :], start=True, stop=True).then_inc(up_done, 1)

            def down(c):
                pe.wait_ge(hid_ready, C * group(l, g) + c + 1)
                if c == 0:
                    pe.wait_ge(y_for_attn, SEQS + GS * group(l, g))
                for j in range(GT):
                    last = nc.tensor.matmul(F_OUT[:, j * P:(j + 1) * P], hid[:, c, j * P:(j + 1) * P], w_2[:, c, :],
                                            start=(c == 0 and j == 0), stop=(c == C - 1), skip_group_check=True)
                if c == C - 1:
                    last.then_inc(ffn_in_psum, 1)
            if g is not None:
                pe.wait_ge(fhT_ready, group(l, g) + 1)
                up(0)
                up(1)
                down(0)
                up(2)
                down(1)
            if n is not None:
                pe.wait_ge(fh_ready, group(l, n) + 1 + FREE)
                for j in range(GT):
                    last = nc.tensor.transpose(F_HT[:, j * P:(j + 1) * P], fh[:, j, :], k.ident[:])
                last.then_inc(fhT_in_psum, 1)
            if g is not None:
                down(2)

        def dve_ffn(dve, l, g, u, n, un, pair):
            def hidden(c):
                idx = C * group(l, g) + c
                dve.wait_ge(gelu_ready, idx + 1)
                nc.vector.scalar_tensor_tensor(hid[:, c, :], a_bank(c), b1[:, bass.ts(2 * C * l + c, 1)],
                                               gelu[:, c, :], ALU.add, ALU.mult).then_inc(hid_ready, 1)
            if n is not None:
                dve.wait_ge(sh_for_ffn[un], 48 * (FGROUPS // 2 * l + pair + 1))
                norm_statistics(k, dve, inner, group(l, n), lambda j: rows_f[:, un, j, :])
            if g is not None:
                hidden(0)
            if n is not None:
                norm_apply(k, dve, inner, group(l, n), lambda j: fh[:, j, :], lambda j: rows_f[:, un, j, :],
                           (fh_ready, 1))
            if g is not None:
                hidden(1)
                hidden(2)
                dve.wait_ge(ffn_in_psum, START + group(l, g) + 1)
                dve.wait_ge(bias_added, group(l, g) + 1)
                rows = y[:, bass.ts(g, GT), :]
                nc.vector.tensor_tensor(rows, F_OUT.rearrange("p (j f) -> p j f", f=DIM), rows,
                                        ALU.add).then_inc(y_for_attn, GS)

        def act_ffn(act, l, g, u, n, un, pair):
            def gate(c):
                settle(act, up_done, C * group(l, g) + c + 1)
                nc.scalar.activation(gelu[:, c, :], g_bank(c), ACT.Gelu,
                                     bias=b1[:, bass.ts(2 * C * l + C + c, 1)]).then_inc(gelu_ready, 1)
            if g is not None:
                gate(0)
                gate(1)
            if n is not None:
                settle(act, fhT_in_psum, group(l, n) + 1)
                nc.scalar.activation(fhT[:, un, :], F_HT, ACT.Identity, bias=ln_b[:, bass.ts(l, 1)],
                                     scale=ln_g[:, bass.ts(l, 1)]).then_inc(fhT_ready, 1)
            if g is not None:
                gate(2)

        def pool_ffn(pool, l, g, u, n, un, pair):
            if n is not None:
                norm_rstd(k, pool, inner, group(l, n))
                settle(pool, sh_for_ffn[un], 48 * (FGROUPS // 2 * l + pair + 1))
                rows = y[:, bass.ts(n, GT), :]
                nc.gpsimd.tensor_tensor(rows, rows, b2[:, bass.ts(l, 1), :].broadcast_to([P, GT, DIM]),
                                        ALU.add).then_inc(bias_added, 1)

        def shift_rows(sp, dst, tile, n, done):
            src = y[:, bass.ts(tile, n), :]
            H = DIM // 2
            sp.dma_start(dst[:, :, 0:H], src[:, :, 0:H]).then_inc(done, 16)
            sp.dma_start(dst[1:P, :, H:DIM], src[0:P - 1, :, H:DIM]).then_inc(done, 16)
            sp.dma_start(dst[0:1, 1::2, H:DIM], src[P - 1:P, 0::2, H:DIM]).then_inc(done, 16)

        with nc.Block() as block:
            @block.sync
            def _(sp):
                sp.wait_ge(edge_zero, 2)
                with sp.Fori(0, LAYERS) as l:
                    sp.wait_ge(attn_in_psum, START + SEQS * l)
                    sp.dma_start(wa[:], k.dram["loc_wa"][bass.ts(l, 1)].rearrange("a p n -> p (a n)"))\
                      .then_inc(wa_loaded, 16)
                    sp.wait_ge(ffn_in_psum, START + FGROUPS * l)
                    sp.dma_start(wf[:], k.dram["loc_wf"][bass.ts(l, 1)].rearrange("a p n -> p (a n)"))\
                      .then_inc(wf_loaded, 16)
                    with sp.Fori(0, SEQS // 2) as i:
                        for u in range(2):
                            t = 2 * i + u
                            sp.wait_ge(hT_in_psum, seq(l, t) + 1)
                            sp.wait_ge(y_for_attn, seq(l, t) + 1)
                            shift_rows(sp, rows_a[:, u], t, T, sh_for_attn[u])
                    with sp.Fori(0, FGROUPS // 2) as i:
                        for u in range(2):
                            g = 2 * i + u
                            sp.wait_ge(fh_ready, group(l, g) + 1)
                            sp.wait_ge(y_for_ffn, START + SEQS * l + GS * (g + 1))
                            shift_rows(sp, rows_f[:, u], g, GT, sh_for_ffn[u])

            @block.tensor
            def _(pe):
                pe.sem_inc(hT_in_psum, FREE)
                pe.sem_inc(attn_in_psum, START)
                pe.sem_inc(ffn_in_psum, START)
                with pe.Fori(0, LAYERS) as l:
                    pe.wait_ge(y_for_attn, SEQS * (l + 1))
                    pe.wait_ge(wa_loaded, 16 * (l + 1))
                    run_attention(pe, l, pe_attention, pe_front)
                    pe.wait_ge(y_for_ffn, START + SEQS * (l + 1))
                    pe.wait_ge(wf_loaded, 16 * (l + 1))
                    run_ffn(pe, l, pe_ffn)

            @block.vector
            def _(dve):
                nc.vector.memset(rows_a[0:1, :, 0, DIM // 2:DIM], 0.0).then_inc(edge_zero, 1)
                nc.vector.memset(rows_f[0:1, :, 0::2, DIM // 2:DIM], 0.0).then_inc(edge_zero, 1)
                dve.sem_inc(fh_ready, FREE)
                dve.sem_inc(y_for_ffn, START)
                for l in range(LAYERS):
                    for tab, const, by in ((rot_cos, cos, scale), (rot_sin, sin, scale_swapped)):
                        nc.vector.tensor_tensor(tab[:, T * l:T * (l + 1)], const[:],
                                                by[:, l:l + 1].broadcast_to([P, T, 2, HEAD_DIM]),
                                                ALU.mult).then_inc(tables_steps, 1)
                dve.wait_ge(tables_steps, 2 * LAYERS)
                with dve.Fori(0, TILES // (2 * GT)) as g:
                    def tile(j, of=x): return of[:, bass.ts(2 * GT * g + j, 1), :]
                    norm_statistics(k, dve, outer, g, tile)
                    norm_apply(k, dve, outer, g, lambda j: tile(j, y), tile, (y_for_attn, 2 * GT // T))
                with dve.Fori(0, LAYERS) as l:
                    run_attention(dve, l, dve_attention, dve_front)
                    run_ffn(dve, l, dve_ffn)
                dve.wait_ge(y_for_attn, SEQS * (LAYERS + 1))
                with dve.Fori(0, TILES // (2 * GT)) as g:
                    rows = bass.ts(g, 2 * GT)
                    nc.vector.scalar_tensor_tensor(x[:, rows, :], y[:, rows, :], 0.5, x[:, rows, :],
                                                   ALU.mult, ALU.add)

            @block.scalar
            def _(act):
                for started in (qkT_ready, v_ready, oT_ready):
                    act.sem_inc(started, START)
                with act.Fori(0, LAYERS) as l:
                    run_attention(act, l, act_attention, act_front)
                    run_ffn(act, l, act_ffn)

            @block.gpsimd
            def _(pool):
                with pool.Fori(0, TILES // (2 * GT)) as g:
                    norm_rstd(k, pool, outer, g)
                pool.wait_ge(tables_steps, 2 * LAYERS)
                with pool.Fori(0, LAYERS) as l:
                    run_attention(pool, l, pool_attention, pool_front)
                    run_ffn(pool, l, pool_ffn)


def store_stage(k):
    nc = k.nc
    stored = k.sem("stored")
    with nc.Block() as block:
        @block.sync
        def _(sp):
            sp.dma_start(k.dram["out"], k.x[:]).then_inc(stored, 16)
            sp.wait_ge(stored, 16)


STAGES = {
    "moe1": (moe_stage, "moe", "moe1"),
    "l0": (linear_attention_stage, "lin", "lin"),
    "moe2": (moe_stage, "moe", "moe2"),
    "l1a": (local_attention_stage, "loc", "loc1"),
    "mamba": (state_space_stage, "ssm", "ssm"),
    "l1b": (local_attention_stage, "loc", "loc2"),
}


def build(nc, dram, stages):
    with ExitStack() as stack:
        k = Core(nc, dram, stack)
        load_stage(k)
        done = set()
        for s in stages:
            stage, kind, name = STAGES[s]
            if kind in done:
                k.clear(kind)
            done.add(kind)
            stage(k, name)
        store_stage(k)


def shape_constants():
    c = {"ident": np.eye(P, dtype=np.float32)}
    expert_of = 2 * np.arange(MOE_CHUNKS)[:, None] + np.arange(P)[None, :] // EXPERT_HID
    c["b_moe_sel"] = (np.arange(EXPERTS)[:, None, None] == expert_of[None]).astype(np.float32)
    c["c_moe_rank"] = np.broadcast_to(EXPERTS - np.arange(EXPERTS, dtype=np.float32), (P, 4, EXPERTS))
    pick = np.zeros((P, 2 * SSM_STATE, P), np.float32)
    for n in range(2 * SSM_STATE):
        pick[32 + n::32, n, :] = 1.0
    c["b_ssm_pick"] = pick.astype(np.float32)
    f = np.float32
    half = np.arange(0, HEAD_DIM, 2, dtype=f)
    inv_freq = f(1.0) / f(10000.0) ** (half / f(HEAD_DIM))
    pos = np.arange(SEQ_LEN, dtype=f)
    angle = pos[:, None] * inv_freq[None, :]
    base = (half + f(0.4 * HEAD_DIM)) / f(1.4 * HEAD_DIM)
    stretch = base[None, :] ** ((pos - SEQ_LEN // 2) / f(WINDOW // 2))[:, None]
    both = np.stack([8 * stretch, 1 / stretch], axis=1)
    cos, sin = np.cos(angle)[:, None] * both, np.sin(angle)[:, None] * both

    def by_tile(v):
        return v.reshape(SEQ_LEN // P, P, 2, HEAD_DIM).swapaxes(0, 1).astype(f)
    c["c_loc_cos"] = by_tile(np.concatenate([cos, cos], axis=-1))
    c["c_loc_sin"] = by_tile(np.concatenate([-sin, sin], axis=-1))
    i, j = np.arange(WINDOW)[:, None], np.arange(WINDOW)[None, :]
    own, before, never = j <= i, j >= i, np.zeros((WINDOW, WINDOW), bool)
    rows = [np.concatenate([own, never], 1), np.concatenate([before, own], 1),
            np.concatenate([own, before], 1), np.concatenate([before, own], 1)]
    pairs = np.concatenate([np.concatenate(rows[0:2]), np.concatenate(rows[2:4])], axis=1)
    c["b_loc_mask"] = np.where(np.tile(pairs, (1, 2)), 0, MASKED).astype(np.float32)
    c["b_loc_ident"] = np.eye(P).astype(np.float32)
    return c


def layouts(i):
    a = {}
    a["x"] = i["L0_attn_x"].reshape(TILES, P, DIM).transpose(1, 0, 2)
    a["c_moe_gate"] = i["L0_ffn_gate_w"].T
    a["c_moe_wg"] = i["L0_ffn_w_gate"].reshape(EXPERTS * EXPERT_HID, DIM).T
    a["c_moe_wu"] = i["L0_ffn_w_up"].reshape(EXPERTS * EXPERT_HID, DIM).T
    a["c_moe_wd"] = i["L0_ffn_w_down"].transpose(0, 2, 1).reshape(MOE_CHUNKS, P, DIM).transpose(1, 0, 2)
    qkv = i["L0_attn_w_qkv"]
    a["lin_w"] = np.concatenate([qkv[:, :, 0:DIM], qkv[:, :, DIM:2 * DIM],
                                 qkv[:, :, 2 * DIM:3 * DIM].transpose(0, 2, 1), i["L0_attn_w_out"]], axis=2)
    a["c_lin_gamma"] = i["L0_attn_gamma"].T
    a["c_lin_beta"] = i["L0_attn_beta"].T
    a["c_lin_bias"] = np.broadcast_to(i["L0_attn_b_out"], (P,) + i["L0_attn_b_out"].shape)
    chunks = SSM_INNER // P

    def by_chunk(v):
        return v.reshape((chunks, P) + v.shape[1:]).swapaxes(0, 1)
    a["c_ssm_win"] = i["L1_attn_W_in"]
    wx = i["L1_attn_W_xproj"]
    low, rows = wx[:, :SSM_RANK], wx[:, SSM_RANK:]
    a["c_ssm_wx"] = by_chunk(np.concatenate([low, np.zeros_like(low), rows, rows, rows], axis=1))
    a["c_ssm_wdt"] = i["L1_attn_W_dt"]
    a["c_ssm_wout"] = by_chunk(i["L1_attn_W_out"])
    a["c_ssm_taps"] = by_chunk(i["L1_attn_conv_k"][:, 0, :].T)
    a["c_ssm_convb"] = by_chunk(i["L1_attn_conv_b"])
    a["c_ssm_bdt"] = by_chunk(i["L1_attn_b_dt"])
    a["c_ssm_d"] = by_chunk(i["L1_attn_D"])
    a["c_ssm_alog"] = by_chunk(i["L1_attn_A_log"])
    layers = i["L1_ffn_wo"].shape[0]
    w_o = i["L1_ffn_wo"].reshape(layers, INNER // P, P, DIM).transpose(0, 2, 1, 3).reshape(layers, P, -1)
    a["loc_wa"] = np.concatenate([i["L1_ffn_wqkv"], w_o], axis=2)
    hid = i["L1_ffn_w2"].shape[1]

    def pad(v, axis):
        width = [(0, 0)] * v.ndim
        width[axis] = (0, HID_CHUNKS * P - hid)
        return np.pad(v, width)
    w1, b1 = i["L1_ffn_w1"], i["L1_ffn_b1"]
    w2 = pad(i["L1_ffn_w2"], 1).reshape(layers, HID_CHUNKS, P, DIM).transpose(0, 2, 1, 3).reshape(layers, P, -1)
    a["loc_wf"] = np.concatenate([pad(w1[..., :hid], 2), pad(w1[..., hid:], 2), w2], axis=2)
    b1 = np.stack([pad(b1[:, :hid], 1), pad(b1[:, hid:], 1)], axis=1)
    a["c_loc_b1"] = b1.reshape(layers * 2 * HID_CHUNKS, P).T
    a["c_loc_b2"] = np.broadcast_to(i["L1_ffn_b2"], (P,) + i["L1_ffn_b2"].shape)
    a["c_loc_lng"] = i["L1_ffn_ln_g"].T
    a["c_loc_lnb"] = i["L1_ffn_ln_b"].T
    scale = np.stack([i["L1_ffn_q_scale"], i["L1_ffn_k_scale"]], axis=1)
    a["c_loc_scale"] = np.broadcast_to(scale, (P,) + scale.shape)
    a["c_loc_scale_swapped"] = np.broadcast_to(np.roll(scale, HEAD_DIM // 2, axis=-1), (P,) + scale.shape)
    return a


ALL = ("moe1", "l0", "moe2", "l1a", "mamba", "l1b")


def program(nc, inputs, stages=ALL):
    arrays = {n: np.ascontiguousarray(a) for n, a in
              (layouts({n: np.asarray(v) for n, v in inputs.items()}) | shape_constants()).items()}
    dram = {n: nc.dram_tensor(n, a.shape, mybir.dt.from_np(a.dtype), kind="ExternalInput").ap()
            for n, a in arrays.items()}
    dram["out"] = nc.dram_tensor("out", (P, TILES, DIM), FP32, kind="ExternalOutput").ap()
    build(nc, dram, stages)
    return arrays


def kernel(**inputs):
    import concourse.bacc as _bacc
    from concourse.bass_utils import run_bass_kernel_spmd as _run

    nc = _bacc.Bacc("TRN2", target_bir_lowering=False, num_devices=1)
    arrays = program(nc, inputs)
    out = _run(nc, [arrays], core_ids=[0]).results[0]["out"]
    return out.transpose(1, 0, 2).reshape(SEQS, SEQ_LEN, DIM)
```

```python
from contextlib import ExitStack

import numpy as np
import concourse.bass as bass
from concourse import mybir

FP32 = mybir.dt.float32
BF16 = mybir.dt.bfloat16
ALU = mybir.AluOpType
ACT = mybir.ActivationFunctionType
AX = mybir.AxisListType

P = 128
SEQS, SEQ_LEN, DIM = 16, 256, 128
TOKENS = SEQS * SEQ_LEN
TILES = TOKENS // P
EPS = 1e-5

EXPERTS, EXPERT_HID = 8, 64
MOE_CHUNKS = EXPERTS * EXPERT_HID // P


class Core:

    def __init__(self, nc, dram, stack):
        self.nc, self.dram, self.stack, self.sems = nc, dram, stack, {}

    def sbuf(self, name, shape, dtype=FP32, stack=None):
        return (stack or self.stack).enter_context(self.nc.sbuf_tensor(f"{name}_sb", shape, dtype))

    def sem(self, name):
        if name not in self.sems:
            self.sems[name] = self.stack.enter_context(self.nc.semaphore(name))
        return self.sems[name]

    def clear(self, kind):
        with self.nc.Block() as block:
            @block.gpsimd
            def _(pool):
                for name, sem in self.sems.items():
                    if name.startswith(f"{kind}_"):
                        pool.sem_clear(sem)


def load_stage(k):
    nc, dram = k.nc, k.dram
    k.psum = k.stack.enter_context(nc.psum_tensor("psum", [P, 8, 512], FP32))
    k.x = k.sbuf("x", [P, TILES, DIM])
    k.y = k.sbuf("y", [P, TILES, DIM])
    k.ident = k.sbuf("ident", [P, P])
    k.neg_half = k.sbuf("neg_half", [P, 32])
    k.loaded = k.sem("loaded")
    k.const = {}
    small = [n for n in dram if n.startswith(("c_", "b_"))]
    landing = ExitStack()
    for n in small:
        k.const[n[2:]] = k.sbuf(n, list(dram[n].shape), FP32 if n.startswith("c_") else BF16)
    landed = {n: k.sbuf(f"{n}_landing", list(dram[n].shape), FP32, landing) if n.startswith("b_") else k.const[n[2:]]
              for n in small}
    consts_done = k.sem("consts_done")
    with nc.Block() as block:
        @block.sync
        def _(sp):
            sp.dma_start(k.x[:], dram["x"]).then_inc(k.loaded, 16)
            for n in small:
                sp.dma_start(landed[n][:], dram[n]).then_inc(k.loaded, 16)
            sp.dma_start(k.ident[:], dram["ident"]).then_inc(k.loaded, 16)
            sp.wait_ge(k.loaded, 16 * (len(small) + 2))

        @block.vector
        def _(dve):
            nc.vector.memset(k.neg_half[:], -0.5).then_inc(consts_done, 1)
            dve.wait_ge(k.loaded, 16 * (len(small) + 2))
            for n in small:
                if n.startswith("b_"):
                    nc.vector.tensor_copy(k.const[n[2:]][:], landed[n][:])
    landing.close()


def settle(eng, sem, value):
    eng.wait_ge(sem, value)
    eng.nop(nofuse=True)


def add_norm_buffers(k, name, kind, tiles, mem):
    b = type("NormBuffers", (), {})()
    b.tiles = tiles
    b.stats = k.sbuf(f"{name}_stats", [P, tiles, 6], FP32, mem)
    b.mv = k.sbuf(f"{name}_mv", [P, tiles, 2], FP32, mem)
    b.var_eps = k.sbuf(f"{name}_var_eps", [P, tiles], FP32, mem)
    b.rstd = k.sbuf(f"{name}_rstd", [P, tiles], FP32, mem)
    b.stats_done = k.sem(f"{kind}_stats_done")
    b.mean_done = k.sem(f"{kind}_mean_done")
    b.var_ready = k.sem(f"{kind}_var_ready")
    b.rstd_ready = k.sem(f"{kind}_rstd_ready")
    return b


def norm_statistics(k, dve, b, t, tile):
    nc = k.nc
    for j in range(b.tiles):
        last = nc.vector.bn_stats(b.stats[:, j, :], tile(j))
    last.then_inc(b.stats_done, 1)
    settle(dve, b.stats_done, t + 1)
    for j in range(b.tiles):
        last = nc.vector.bn_aggr(b.mv[:, j, :], b.stats[:, j, :])
    last.then_inc(b.mean_done, 1)
    dve.wait_ge(b.mean_done, t + 1)
    nc.vector.tensor_scalar(b.var_eps[:], b.mv[:, :, 1], EPS, None, ALU.add).then_inc(b.var_ready, 1)


def norm_rstd(k, pool, b, t):
    pool.wait_ge(b.var_ready, t + 1)
    k.nc.gpsimd.tensor_tensor(b.rstd[:], b.var_eps[:], k.neg_half[:, 0:b.tiles], ALU.pow).then_inc(b.rstd_ready, 1)


def norm_apply(k, dve, b, t, out, tile, done):
    dve.wait_ge(b.rstd_ready, t + 1)
    for j in range(b.tiles):
        last = k.nc.vector.tensor_scalar(out(j), tile(j), b.mv[:, j, 0:1], b.rstd[:, j:j + 1],
                                         ALU.subtract, ALU.mult)
    last.then_inc(*done)


def moe_stage(k, name):
    nc, psum, x = k.nc, k.psum, k.x
    wg, wu, wd = k.const["moe_wg"], k.const["moe_wu"], k.const["moe_wd"]
    gate_w, sel, rank = k.const["moe_gate"], k.const["moe_sel"], k.const["moe_rank"]
    GT = 4
    GROUPS = TILES // GT
    W = GT * P
    C = MOE_CHUNKS

    with ExitStack() as mem:
        def sb(n, shape, dtype=FP32):
            return k.sbuf(f"{name}_{n}", shape, dtype, mem)

        stats = sb("stats", [P, 2, GT, 6])
        mv = sb("mv", [P, 2, GT, 2])
        var_eps = sb("var_eps", [P, 2, GT])
        rstd = sb("rstd", [P, 2, GT])
        h = sb("h", [P, 2, GT, P])
        hT = sb("hT", [P, 2, W])
        top = sb("top", [P, 2, GT])
        is_top = sb("is_top", [P, 2, GT, EXPERTS])
        ranked = sb("ranked", [P, 2, GT, EXPERTS])
        first = sb("first", [P, 2, GT])
        onehot = sb("onehot", [P, 2, GT, EXPERTS])
        tanh = sb("tanh", [P, 2, GT])
        rw = sb("rw", [P, 2, GT])
        hs = sb("hs", [P, 2, GT, P])
        hsT = sb("hsT", [P, 2, W])
        maskT = sb("maskT", [EXPERTS, 2, W], BF16)
        silu = sb("silu", [P, 2, W])
        su = sb("su", [P, 2, W])
        hid = sb("hid", [P, 2, W])

        var_ready = k.sem(f"moe_var_ready")
        rstd_ready = k.sem(f"moe_rstd_ready")
        h_ready = k.sem(f"moe_h_ready")
        hT_in_psum = k.sem(f"moe_hT_in_psum")
        hT_ready = k.sem(f"moe_hT_ready")
        logits_ready = k.sem(f"moe_logits_ready")
        top_ready = k.sem(f"moe_top_ready")
        tanh_ready = k.sem(f"moe_tanh_ready")
        hs_ready = k.sem(f"moe_hs_ready")
        hsT_in_psum = k.sem(f"moe_hsT_in_psum")
        hsT_ready = k.sem(f"moe_hsT_ready")
        up_done = k.sem(f"moe_up_done")
        silu_ready = k.sem(f"moe_silu_ready")
        hid_ready = k.sem(f"moe_hid_ready")
        out_ready = k.sem(f"moe_out_ready")
        front = k.sem(f"moe_front_steps")
        FRONT = 6
        su_ready = k.sem(f"moe_su_ready")

        def bank(u):
            return psum[:, u, :]

        def slot(s, what):
            return psum[:, 2 + 3 * s + what, :]

        mask_bank = slot((C - 1) % 2, 2)

        def tiles(ap, t):
            return ap[:, bass.ts(t, GT), :]

        def run(eng, work):
            work(eng, None, None, 0, 0)
            with eng.Fori(0, GROUPS // 2 - 1) as i:
                work(eng, 2 * i, 0, 2 * i + 1, 1)
                work(eng, 2 * i + 1, 1, 2 * i + 2, 0)
            work(eng, GROUPS - 2, 0, GROUPS - 1, 1)
            work(eng, GROUPS - 1, 1, None, None)

        def transpose_h(pe, t, u):
            pe.wait_ge(h_ready, t + 1)
            for j in range(GT):
                last = nc.tensor.transpose(bank(u)[:, j * P:(j + 1) * P], h[:, u, j, :], k.ident[:])
            last.then_inc(hT_in_psum, 1)

        def gate(pe, t, u):
            pe.wait_ge(hT_ready, t + 1)
            for j in range(GT):
                last = nc.tensor.matmul(bank(u)[:, j * EXPERTS:(j + 1) * EXPERTS],
                                        hT[:, u, j * P:(j + 1) * P], gate_w[:], start=True, stop=True)
            last.then_inc(logits_ready, 1)

        def transpose_scaled(pe, t, u):
            pe.wait_ge(hs_ready, t + 1)
            for j in range(GT):
                nc.tensor.transpose(bank(u)[:, j * P:(j + 1) * P], hs[:, u, j, :], k.ident[:])
            for j in range(GT):
                last = nc.tensor.transpose(mask_bank[0:EXPERTS, j * P:(j + 1) * P],
                                           onehot[:, u, j, :], k.ident[:])
            last.then_inc(hsT_in_psum, 1)

        def up(t, u, c):
            s = c % 2
            nc.tensor.matmul(slot(s, 0), wg[:, c * P:(c + 1) * P], hsT[:, u, :], start=True, stop=True)
            nc.tensor.matmul(slot(s, 1), wu[:, c * P:(c + 1) * P], hsT[:, u, :], start=True, stop=True)
            nc.tensor.matmul(slot(s, 2), sel[:, c, :], maskT[:, u, :], start=True, stop=True).then_inc(up_done, 1)

        def down(pe, t, u, c):
            pe.wait_ge(hid_ready, C * t + c + 1)
            for j in range(GT):
                last = nc.tensor.matmul(bank(u)[:, j * P:(j + 1) * P], hid[:, c % 2, j * P:(j + 1) * P],
                                        wd[:, c, :], start=(c == 0 and j == 0), stop=(c == C - 1),
                                        skip_group_check=True)
            if c == C - 1:
                last.then_inc(out_ready, 1)

        def pe_work(pe, t, u, n, un):
            if t is not None:
                pe.wait_ge(hsT_ready, t + 1)
                up(t, u, 0)
            for c in range(C):
                if t is not None and c + 1 < C:
                    up(t, u, c + 1)
                if n is not None and c == 1:
                    transpose_h(pe, n, un)
                if n is not None and c == 2:
                    gate(pe, n, un)
                if t is not None:
                    down(pe, t, u, c)
            if n is not None:
                transpose_scaled(pe, n, un)

        def row_statistics(dve, t, u):
            for j in range(GT):
                last = nc.vector.bn_stats(stats[:, u, j, :], x[:, bass.ts(GT * t + j, 1), :])
            last.then_inc(front, 1)
            settle(dve, front, FRONT * t + 1)
            for j in range(GT):
                last = nc.vector.bn_aggr(mv[:, u, j, :], stats[:, u, j, :])
            last.then_inc(front, 1)
            dve.wait_ge(front, FRONT * t + 2)
            nc.vector.tensor_scalar(var_eps[:, u, :], mv[:, u, :, 1], EPS, None, ALU.add).then_inc(var_ready, 1)

        def normalize(dve, t, u):
            dve.wait_ge(rstd_ready, t + 1)
            for j in range(GT):
                last = nc.vector.tensor_scalar(h[:, u, j, :], x[:, bass.ts(GT * t + j, 1), :], mv[:, u, j, 0:1],
                                               rstd[:, u, j:j + 1], ALU.subtract, ALU.mult)
            last.then_inc(h_ready, 1)

        def choose(dve, t, u):
            dve.wait_ge(logits_ready, t + 1)
            logits = bank(u)[:, 0:GT * EXPERTS].rearrange("p (j e) -> p j e", e=EXPERTS)
            nc.vector.tensor_reduce(top[:, u, :], logits, AX.X, ALU.max).then_inc(top_ready, 1)
            dve.wait_ge(top_ready, t + 1)
            nc.vector.tensor_tensor(is_top[:, u], logits,
                                    top[:, u, :].unsqueeze(2).broadcast_to([P, GT, EXPERTS]),
                                    ALU.is_equal).then_inc(front, 1)
            dve.wait_ge(front, FRONT * t + 3)
            nc.vector.tensor_tensor(ranked[:, u], is_top[:, u], rank[:], ALU.mult).then_inc(front, 1)
            dve.wait_ge(front, FRONT * t + 4)
            nc.vector.tensor_reduce(first[:, u, :], ranked[:, u], AX.X, ALU.max).then_inc(front, 1)
            dve.wait_ge(front, FRONT * t + 5)
            nc.vector.tensor_tensor(onehot[:, u], ranked[:, u],
                                    first[:, u, :].unsqueeze(2).broadcast_to([P, GT, EXPERTS]), ALU.is_equal)
            dve.wait_ge(tanh_ready, t + 1)
            nc.vector.tensor_scalar(rw[:, u, :], tanh[:, u, :], 0.5, 0.5, ALU.mult, ALU.add).then_inc(front, 1)
            dve.wait_ge(front, FRONT * t + 6)
            for j in range(GT):
                last = nc.vector.tensor_scalar(hs[:, u, j, :], h[:, u, j, :], rw[:, u, j:j + 1], None, ALU.mult)
            last.then_inc(hs_ready, 1)

        def hidden(dve, t, u, c):
            s = c % 2
            dve.wait_ge(silu_ready, C * t + c + 1)
            nc.vector.tensor_tensor(su[:, s, :], silu[:, s, :], slot(s, 1), ALU.mult).then_inc(su_ready, 1)
            dve.wait_ge(su_ready, C * t + c + 1)
            nc.vector.tensor_tensor(hid[:, s, :], su[:, s, :], slot(s, 2), ALU.mult).then_inc(hid_ready, 1)

        def dve_work(dve, t, u, n, un):
            if n is not None:
                row_statistics(dve, n, un)
            for c in range(C):
                if t is not None:
                    hidden(dve, t, u, c)
                if n is not None and c == 0:
                    normalize(dve, n, un)
                if n is not None and c == 2:
                    choose(dve, n, un)
            if t is not None:
                dve.wait_ge(out_ready, t + 1)
                nc.vector.scalar_tensor_tensor(tiles(x, t), bank(u).rearrange("p (j f) -> p j f", f=DIM), 0.5,
                                               tiles(x, t), ALU.mult, ALU.add)

        def act_work(act, t, u, n, un):
            for c in range(C):
                if t is not None:
                    act.wait_ge(up_done, C * t + c + 1)
                    nc.scalar.activation(silu[:, c % 2, :], slot(c % 2, 0), ACT.Silu).then_inc(silu_ready, 1)
                if n is not None and c == 1:
                    act.wait_ge(hT_in_psum, n + 1)
                    nc.scalar.activation(hT[:, un, :], bank(un), ACT.Copy).then_inc(hT_ready, 1)
                if n is not None and c == 2:
                    act.wait_ge(top_ready, n + 1)
                    nc.scalar.activation(tanh[:, un, :], top[:, un, :], ACT.Tanh, scale=0.5).then_inc(tanh_ready, 1)
            if n is not None:
                act.wait_ge(hsT_in_psum, n + 1)
                nc.scalar.activation(hsT[:, un, :], bank(un), ACT.Copy)
                nc.scalar.activation(maskT[:, un, :], mask_bank[0:EXPERTS, :], ACT.Copy).then_inc(hsT_ready, 1)

        def pool_work(pool, t, u, n, un):
            if n is not None:
                pool.wait_ge(var_ready, n + 1)
                nc.gpsimd.tensor_tensor(rstd[:, un, :], var_eps[:, un, :], k.neg_half[:, 0:GT],
                                        ALU.pow).then_inc(rstd_ready, 1)

        with nc.Block() as block:
            @block.tensor
            def _(pe):
                run(pe, pe_work)

            @block.vector
            def _(dve):
                run(dve, dve_work)

            @block.scalar
            def _(act):
                run(act, act_work)

            @block.gpsimd
            def _(pool):
                run(pool, pool_work)


def linear_attention_stage(k, name="lin"):
    nc, psum, x, y = k.nc, k.psum, k.x, k.y
    S = 4
    GROUPS = SEQS // S
    T = SEQ_LEN // P
    gamma, beta, bias = k.const["lin_gamma"], k.const["lin_beta"], k.const["lin_bias"]
    w_dram = k.dram["lin_w"]

    with ExitStack() as mem:
        def sb(n, shape):
            return k.sbuf(f"{name}_{n}", shape, FP32, mem)

        w = sb("w", [P, 2, 4 * P])
        h = sb("h", [P, S * T, P])
        hT = sb("hT", [P, S, SEQ_LEN])
        neg_max = sb("neg_max", [P, S, 1 + T])
        expq_T = sb("expq_T", [P, S, SEQ_LEN])
        expk = sb("expk", [P, S, T, P])
        sums = sb("sums", [P, S, 1 + T])
        inv = sb("inv", [P, S, 1 + T])
        expq = sb("expq", [P, S, T, P])
        MT = sb("MT", [P, S, P])
        G = sb("G", [P, S, P])
        F = sb("F", [P, S, P])
        outer = add_norm_buffers(k, f"{name}_outer", f"{name}_outer", S * T, mem)
        inner = add_norm_buffers(k, f"{name}_inner", f"{name}_inner", S * T, mem)

        w_loaded = [k.sem(f"{name}_w_loaded{p}") for p in range(2)]
        y_ready = k.sem(f"{name}_y_ready")
        h_ready = k.sem(f"{name}_h_ready")
        bias_added = k.sem(f"{name}_bias_added")
        hT_in_psum = k.sem(f"{name}_hT_in_psum")
        hT_ready = k.sem(f"{name}_hT_ready")
        qk_in_psum = k.sem(f"{name}_qk_in_psum")
        max_ready = k.sem(f"{name}_max_ready")
        exp_ready = k.sem(f"{name}_exp_ready")
        inv_ready = k.sem(f"{name}_inv_ready")
        expq_in_psum = k.sem(f"{name}_expq_in_psum")
        expq_ready = k.sem(f"{name}_expq_ready")
        MT_in_psum = k.sem(f"{name}_MT_in_psum")
        MT_ready = k.sem(f"{name}_MT_ready")
        G_in_psum = k.sem(f"{name}_G_in_psum")
        G_ready = k.sem(f"{name}_G_ready")
        F_in_psum = k.sem(f"{name}_F_in_psum")
        F_ready = k.sem(f"{name}_F_ready")
        out_in_psum = k.sem(f"{name}_out_in_psum")

        LAYERS = k.dram["lin_w"].shape[0]

        def Wq(p): return w[:, p, 0:P]
        def Wk(p): return w[:, p, P:2 * P]
        def WvT(p): return w[:, p, 2 * P:3 * P]
        def Wout(p): return w[:, p, 3 * P:4 * P]

        def q_ps(s): return psum[:, s, 0:SEQ_LEN]
        def k_ps(s): return psum[:, s, SEQ_LEN:2 * SEQ_LEN]
        def F_ps(s): return psum[:, s, 0:P]
        def out_ps(s): return psum[:, s, SEQ_LEN:2 * SEQ_LEN]
        def tr_ps(s): return psum[:, 4 + s, 0:SEQ_LEN]
        def MT_ps(s): return psum[:, 4 + s, 2 * P:3 * P]
        def G_ps(s): return psum[:, 4 + s, 3 * P:4 * P]

        def run(eng, work, front):
            def layer(l, p, last):
                with eng.Fori(0, GROUPS - 1) as g:
                    work(eng, l, p, g, (l, g + 1))
                work(eng, l, p, GROUPS - 1, None if last else (l + 1, 0))
            front(eng, 0, 0)
            with eng.Fori(0, LAYERS // 2 - 1) as i:
                layer(2 * i, 0, False)
                layer(2 * i + 1, 1, False)
            layer(LAYERS - 2, 0, False)
            layer(LAYERS - 1, 1, True)

        def unit(l, g, s):
            return SEQS * l + S * g + s

        def pe_front(pe, l, g):
            for s in range(S):
                if s == 0:
                    pe.wait_ge(h_ready, GROUPS * l + g + 1)
                for j in range(T):
                    last = nc.tensor.transpose(tr_ps(s)[:, j * P:(j + 1) * P], h[:, T * s + j, :], k.ident[:])
                last.then_inc(hT_in_psum, 1)

        def pe_work(pe, l, p, g, nxt):
            for s in range(S):
                if s == 0:
                    pe.wait_ge(w_loaded[p], 8 * (l - p) + 16)
                pe.wait_ge(hT_ready, unit(l, g, s) + 1)
                pe.wait_ge(y_ready, unit(l, g, s) + 1 + SEQS - S)
                nc.tensor.matmul(q_ps(s), Wq(p), hT[:, s, :], start=True, stop=True)
                for j in range(T):
                    last = nc.tensor.matmul(k_ps(s)[:, j * P:(j + 1) * P], hT[:, s, j * P:(j + 1) * P], Wk(p),
                                            start=True, stop=True)
                last.then_inc(qk_in_psum, 1)
            for s in range(S):
                pe.wait_ge(exp_ready, unit(l, g, s) + 1)
                for j in range(T):
                    last = nc.tensor.transpose(tr_ps(s)[:, j * P:(j + 1) * P], expq_T[:, s, j * P:(j + 1) * P],
                                               k.ident[:])
                last.then_inc(expq_in_psum, 1)
            for s in range(S):
                pe.wait_ge(expq_ready, unit(l, g, s) + 1)
                for j in range(T):
                    last = nc.tensor.matmul(MT_ps(s), expq[:, s, j, :], expk[:, s, j, :],
                                            start=(j == 0), stop=(j == T - 1))
                last.then_inc(MT_in_psum, 1)
            for s in range(S):
                pe.wait_ge(MT_ready, unit(l, g, s) + 1)
                nc.tensor.matmul(G_ps(s), MT[:, s, :], Wout(p), start=True, stop=True).then_inc(G_in_psum, 1)
            for s in range(S):
                pe.wait_ge(G_ready, unit(l, g, s) + 1)
                nc.tensor.matmul(F_ps(s), WvT(p), G[:, s, :], start=True, stop=True).then_inc(F_in_psum, 1)
            for s in range(S):
                pe.wait_ge(F_ready, unit(l, g, s) + 1)
                for j in range(T):
                    last = nc.tensor.matmul(out_ps(s)[:, j * P:(j + 1) * P], hT[:, s, j * P:(j + 1) * P],
                                            F[:, s, :], start=True, stop=True)
                last.then_inc(out_in_psum, 1)
            if nxt is not None:
                pe_front(pe, *nxt)

        def y_tile(g, j):
            return y[:, bass.ts(S * T * g + j, 1), :]

        def dve_front(dve, l, g):
            dve.wait_ge(y_ready, SEQS * l + S * g + S)
            norm_statistics(k, dve, inner, GROUPS * l + g, lambda j: y_tile(g, j))
            norm_apply(k, dve, inner, GROUPS * l + g, lambda j: h[:, j:j + 1, :], lambda j: y_tile(g, j), (h_ready, 1))

        def dve_work(dve, l, p, g, nxt):
            for s in range(S):
                dve.wait_ge(qk_in_psum, unit(l, g, s) + 1)
                nc.vector.tensor_reduce(neg_max[:, s, 0:1], q_ps(s), AX.X, ALU.max, negate=True)
                nc.vector.tensor_reduce(neg_max[:, s, 1:1 + T], k_ps(s).rearrange("p (j c) -> p j c", c=P),
                                        AX.X, ALU.max, negate=True).then_inc(max_ready, 1)
            for s in range(S):
                dve.wait_ge(exp_ready, unit(l, g, s) + 1)
                nc.vector.reciprocal(inv[:, s, :], sums[:, s, :]).then_inc(inv_ready, 1)
            for s in range(S):
                dve.wait_ge(expq_in_psum, unit(l, g, s) + 1)
                if s == 0:
                    dve.wait_ge(inv_ready, unit(l, g, S - 1) + 1)
                for j in range(T):
                    last = nc.vector.tensor_scalar(expq[:, s, j, :], tr_ps(s)[:, j * P:(j + 1) * P],
                                                   inv[:, s, 1 + j:2 + j], None, ALU.mult)
                last.then_inc(expq_ready, 1)
            for s in range(S):
                dve.wait_ge(MT_in_psum, unit(l, g, s) + 1)
                nc.vector.tensor_scalar(MT[:, s, :], MT_ps(s), inv[:, s, 0:1], None, ALU.mult).then_inc(MT_ready, 1)
            if nxt is not None:
                dve_front(dve, *nxt)
            for s in range(S):
                dve.wait_ge(out_in_psum, unit(l, g, s) + 1)
                dve.wait_ge(bias_added, unit(l, g, s) + 1)
                rows = y[:, bass.ts(S * g + s, T), :]
                nc.vector.tensor_tensor(rows, out_ps(s).rearrange("p (j f) -> p j f", f=DIM), rows,
                                        ALU.add).then_inc(y_ready, 1)

        def act_front(act, l, g):
            for s in range(S):
                settle(act, hT_in_psum, unit(l, g, s) + 1)
                nc.scalar.activation(hT[:, s, :], tr_ps(s), ACT.Identity, bias=beta[:, bass.ts(l, 1)],
                                     scale=gamma[:, bass.ts(l, 1)]).then_inc(hT_ready, 1)

        def act_work(act, l, p, g, nxt):
            for s in range(S):
                act.wait_ge(max_ready, unit(l, g, s) + 1)
                nc.scalar.activation(expq_T[:, s, :], q_ps(s), ACT.Exp, bias=neg_max[:, s, 0:1],
                                     accum_out=sums[:, s, 0:1])
                for j in range(T):
                    last = nc.scalar.activation(expk[:, s, j, :], k_ps(s)[:, j * P:(j + 1) * P], ACT.Exp,
                                                bias=neg_max[:, s, 1 + j:2 + j], accum_out=sums[:, s, 1 + j:2 + j])
                last.then_inc(exp_ready, 1)
            for s in range(S):
                act.wait_ge(G_in_psum, unit(l, g, s) + 1)
                nc.scalar.activation(G[:, s, :], G_ps(s), ACT.Copy).then_inc(G_ready, 1)
            for s in range(S):
                act.wait_ge(F_in_psum, unit(l, g, s) + 1)
                nc.scalar.activation(F[:, s, :], F_ps(s), ACT.Copy).then_inc(F_ready, 1)
            if nxt is not None:
                act_front(act, *nxt)

        def pool_front(pool, l, g):
            norm_rstd(k, pool, inner, GROUPS * l + g)
            pool.wait_ge(h_ready, GROUPS * l + g + 1)
            for s in range(S):
                rows = y[:, bass.ts(S * g + s, T), :]
                nc.gpsimd.tensor_tensor(rows, rows, bias[:, bass.ts(l, 1), :].broadcast_to([P, T, DIM]),
                                        ALU.add).then_inc(bias_added, 1)

        def pool_work(pool, l, p, g, nxt):
            if nxt is not None:
                pool_front(pool, *nxt)

        with nc.Block() as block:
            @block.sync
            def _(sp):
                for p in range(2):
                    sp.dma_start(w[:, p, :], w_dram[p]).then_inc(w_loaded[p], 16)
                with sp.Fori(0, LAYERS // 2 - 1) as i:
                    for p in range(2):
                        sp.wait_ge(out_in_psum, SEQS * (2 * i + p + 1))
                        sp.dma_start(w[:, p, :], w_dram[bass.ts(2 * i + p + 2, 1)].rearrange("a p n -> p (a n)"))\
                          .then_inc(w_loaded[p], 16)

            @block.tensor
            def _(pe):
                run(pe, pe_work, pe_front)

            @block.vector
            def _(dve):
                with dve.Fori(0, GROUPS) as g:
                    norm_statistics(k, dve, outer, g, lambda j: x[:, bass.ts(S * T * g + j, 1), :])
                    norm_apply(k, dve, outer, g, lambda j: y_tile(g, j),
                               lambda j: x[:, bass.ts(S * T * g + j, 1), :], (y_ready, S))
                run(dve, dve_work, dve_front)
                dve.wait_ge(y_ready, SEQS * (LAYERS + 1))
                with dve.Fori(0, GROUPS) as g:
                    rows = bass.ts(g, S * T)
                    nc.vector.tensor_tensor(x[:, rows, :], x[:, rows, :], y[:, rows, :], ALU.add)

            @block.scalar
            def _(act):
                run(act, act_work, act_front)

            @block.gpsimd
            def _(pool):
                with pool.Fori(0, GROUPS) as g:
                    norm_rstd(k, pool, outer, g)
                run(pool, pool_work, pool_front)


SSM_INNER, SSM_STATE, SSM_RANK, SSM_TAPS = 256, 16, 16, 4


def state_space_stage(k, name="ssm"):
    nc, psum, x = k.nc, k.psum, k.x
    GT = 4
    GROUPS = TILES // GT
    W = GT * P
    GS = W // SEQ_LEN
    C = SSM_INNER // P
    N = SSM_STATE
    PAD = SSM_TAPS - 1
    w_in, w_x, w_dt, w_out = k.const["ssm_win"], k.const["ssm_wx"], k.const["ssm_wdt"], k.const["ssm_wout"]
    taps, conv_b, b_dt, skip = k.const["ssm_taps"], k.const["ssm_convb"], k.const["ssm_bdt"], k.const["ssm_d"]
    a_log, pick = k.const["ssm_alog"], k.const["ssm_pick"]

    with ExitStack() as mem:
        def sb(n, shape, dtype=FP32):
            return k.sbuf(f"{name}_{n}", shape, dtype, mem)

        A = sb("A", [P, C, N])
        h = sb("h", [P, GT, P])
        hT = sb("hT", [P, W])
        padded = sb("padded", [P, C, GS, PAD + SEQ_LEN])
        conv = sb("conv", [P, C, GS, SEQ_LEN])
        u_act = sb("u_act", [P, 2, C, W])
        z_act = sb("z_act", [P, 2, C, W])
        bc = sb("bc", [P, 2, W], BF16)
        high = sb("high", [P, W], BF16)
        rest = sb("rest", [P, W])
        dt_low = sb("dt_low", [SSM_RANK, W])
        soft_abs = sb("soft_abs", [P, C, W])
        soft_exp = sb("soft_exp", [P, C, W])
        soft_ln = sb("soft_ln", [P, C, W])
        soft_pos = sb("soft_pos", [P, C, W])
        dt = sb("dt", [P, 2, C, W])
        dtu = sb("dtu", [P, 2, C, W])
        decay = sb("decay", [P, 2, C, W])
        drive = sb("drive", [P, 2, C, W])
        state = sb("state", [P, 2, C, W])
        c_row = sb("c_row", [P, 2, W])
        read = sb("read", [P, 2, C, W])
        gated = sb("gated", [P, C, W])
        norm = add_norm_buffers(k, f"{name}_norm", f"{name}_norm", GT, mem)

        A_exp_ready = k.sem(f"{name}_A_exp_ready")
        A_ready = k.sem(f"{name}_A_ready")
        padding_zero = k.sem(f"{name}_padding_zero")
        h_ready = k.sem(f"{name}_h_ready")
        hT_in_psum = k.sem(f"{name}_hT_in_psum")
        hT_ready = k.sem(f"{name}_hT_ready")
        xin_in_psum = k.sem(f"{name}_xin_in_psum")
        xin_ready = k.sem(f"{name}_xin_ready")
        z_in_psum = k.sem(f"{name}_z_in_psum")
        conv_steps = k.sem(f"{name}_conv_steps")
        u_ready = k.sem(f"{name}_u_ready")
        xdbl_in_psum = k.sem(f"{name}_xdbl_in_psum")
        split_steps = k.sem(f"{name}_split_steps")
        bc_ready = k.sem(f"{name}_bc_ready")
        dt_in_psum = k.sem(f"{name}_dt_in_psum")
        soft_steps = k.sem(f"{name}_soft_steps")
        soft_ready = k.sem(f"{name}_soft_ready")
        dt_ready = k.sem(f"{name}_dt_ready")
        dtu_ready = k.sem(f"{name}_dtu_ready")
        rows_in_psum = k.sem(f"{name}_rows_in_psum")
        decay_ready = k.sem(f"{name}_decay_ready")
        c_ready = k.sem(f"{name}_c_ready")
        drive_ready = k.sem(f"{name}_drive_ready")
        state_ready = k.sem(f"{name}_state_ready")
        read_ready = k.sem(f"{name}_read_ready")
        y_in_psum = k.sem(f"{name}_y_in_psum")
        y_left = k.sem(f"{name}_y_left")
        gated_ready = k.sem(f"{name}_gated_ready")
        out_in_psum = k.sem(f"{name}_out_in_psum")
        x_done = k.sem(f"{name}_x_done")

        def b_bank(n): return psum[:, n % 2, :]
        def c_bank(n): return psum[:, 2 + n % 2, :]
        def y_bank(c): return psum[:, 4 + c, :]
        FA, FB = psum[:, 6, :], psum[:, 7, :]

        def run(eng, work, front, finish):
            for n in range(N):
                front(eng, n, 0, 0)
            work(eng, 0, 0, 1, None)
            work(eng, 1, 1, 2, 0)
            with eng.Fori(1, GROUPS // 2 - 1) as i:
                work(eng, 2 * i, 0, 2 * i + 1, 2 * i - 1)
                work(eng, 2 * i + 1, 1, 2 * i + 2, 2 * i)
            work(eng, GROUPS - 2, 0, GROUPS - 1, GROUPS - 3)
            work(eng, GROUPS - 1, 1, None, GROUPS - 2)
            for n in range(2):
                finish(eng, n, GROUPS - 1, 1)

        def pe_front(pe, n, t, u):
            if n == 3:
                pe.wait_ge(h_ready, t + 1)
                for j in range(GT):
                    last = nc.tensor.transpose(FA[:, j * P:(j + 1) * P], h[:, j, :], k.ident[:])
                last.then_inc(hT_in_psum, 1)
            if n == 4:
                pe.wait_ge(hT_ready, t + 1)
                for c, bank in enumerate((FA, FB)):
                    last = nc.tensor.matmul(bank, w_in[:, c * P:(c + 1) * P], hT[:], start=True, stop=True)
                last.then_inc(xin_in_psum, 1)
            if n == 5:
                pe.wait_ge(xin_ready, t + 1)
                for c, bank in enumerate((FA, FB)):
                    last = nc.tensor.matmul(bank, w_in[:, (C + c) * P:(C + c + 1) * P], hT[:], start=True, stop=True)
                last.then_inc(z_in_psum, 1)
            if n == 9:
                pe.wait_ge(u_ready, t + 1)
                for c in range(C):
                    last = nc.tensor.matmul(FA, w_x[:, c, :], u_act[:, u, c, :], start=(c == 0), stop=(c == C - 1))
                last.then_inc(xdbl_in_psum, 1)
            if n == 11:
                pe.wait_ge(bc_ready, t + 1)
                for c, bank in enumerate((FA, FB)):
                    last = nc.tensor.matmul(bank, w_dt[:, c * P:(c + 1) * P], dt_low[:], start=True, stop=True)
                last.then_inc(dt_in_psum, 1)

        def rows(t, u, n):
            nc.tensor.matmul(b_bank(n), pick[:, n, :], bc[:, u, :], start=True, stop=True)
            nc.tensor.matmul(c_bank(n), pick[:, N + n, :], bc[:, u, :], start=True, stop=True).then_inc(rows_in_psum, 1)

        def pe_finish(pe, n, t, u):
            if n == 1:
                pe.wait_ge(gated_ready, t + 1)
                for j in range(GT):
                    for c in range(C):
                        last = nc.tensor.matmul(FA[:, j * P:(j + 1) * P], gated[:, c, j * P:(j + 1) * P],
                                                w_out[:, c, :], start=(c == 0), stop=(c == C - 1))
                last.then_inc(out_in_psum, 1)

        def pe_work(pe, t, u, nxt, prev):
            pe.wait_ge(bc_ready, t + 1)
            rows(t, u, 0)
            rows(t, u, 1)
            for n in range(N):
                pe.wait_ge(read_ready, N * t + n + 1)
                if n == 0 and prev is not None:
                    pe.wait_ge(y_left, prev + 1)
                for c in range(C):
                    last = nc.tensor.matmul(y_bank(c), k.ident[:], read[:, n % 2, c, :],
                                            start=(n == 0), stop=(n == N - 1))
                if n == N - 1:
                    last.then_inc(y_in_psum, 1)
                if n + 2 < N:
                    rows(t, u, n + 2)
                if prev is not None:
                    pe_finish(pe, n, prev, 1 - u)
                if nxt is not None:
                    pe_front(pe, n, nxt, 1 - u)

        def dve_front(dve, n, t, u):
            def tile(j): return x[:, bass.ts(GT * t + j, 1), :]
            if n == 2:
                norm_statistics(k, dve, norm, t, tile)
            if n == 3:
                norm_apply(k, dve, norm, t, lambda j: h[:, j:j + 1, :], tile, (h_ready, 1))
            if 5 <= n < 5 + SSM_TAPS:
                tap = n - 5
                if tap == 0:
                    dve.wait_ge(xin_ready, t + 1)
                for c in range(C):
                    src = padded[:, c, :, tap:tap + SEQ_LEN]
                    if tap == 0:
                        nc.vector.tensor_scalar(conv[:, c], src, taps[:, c, 0:1], conv_b[:, c:c + 1],
                                                ALU.mult, ALU.add).then_inc(conv_steps, 1)
                    else:
                        dve.wait_ge(conv_steps, C * SSM_TAPS * t + C * (tap - 1) + c + 1)
                        nc.vector.scalar_tensor_tensor(conv[:, c], src, taps[:, c, tap:tap + 1], conv[:, c],
                                                       ALU.mult, ALU.add).then_inc(conv_steps, 1)
            if n == 10:
                dve.wait_ge(xdbl_in_psum, t + 1)
                nc.vector.tensor_copy(high[64:P, :], FA[64:P, :]).then_inc(split_steps, 1)
                nc.vector.tensor_copy(dt_low[:], FA[0:SSM_RANK, :])
                nc.vector.tensor_copy(bc[0:64, u, :], FA[0:64, :])
                dve.wait_ge(split_steps, 3 * t + 1)
                nc.vector.tensor_tensor(rest[64:P, :], FA[64:P, :], high[64:P, :], ALU.subtract).then_inc(split_steps, 1)
                dve.wait_ge(split_steps, 3 * t + 2)
                nc.vector.tensor_copy(high[96:P, :], rest[96:P, :]).then_inc(split_steps, 1)
                nc.vector.tensor_copy(bc[64:96, u, :], rest[64:96, :])
                dve.wait_ge(split_steps, 3 * t + 3)
                nc.vector.tensor_tensor(bc[96:P, u, :], rest[96:P, :], high[96:P, :], ALU.subtract).then_inc(bc_ready, 1)
            if n == 13:
                dve.wait_ge(soft_ready, t + 1)
                nc.vector.tensor_tensor(dt[:, u], soft_ln[:], soft_pos[:], ALU.add).then_inc(dt_ready, 1)
                dve.wait_ge(dt_ready, t + 1)
                nc.vector.tensor_tensor(dtu[:, u], dt[:, u], u_act[:, u], ALU.mult).then_inc(dtu_ready, 1)

        def dve_finish(dve, n, t, u):
            if n == 0:
                dve.wait_ge(y_in_psum, t + 1)
                for c in range(C):
                    last = nc.vector.scalar_tensor_tensor(gated[:, c, :], u_act[:, u, c, :], skip[:, c:c + 1],
                                                          y_bank(c), ALU.mult, ALU.add)
                last.then_inc(y_left, 1)
                dve.wait_ge(y_left, t + 1)
                nc.vector.tensor_tensor(gated[:], gated[:], z_act[:, u], ALU.mult).then_inc(gated_ready, 1)
            if n == 1:
                dve.wait_ge(out_in_psum, t + 1)
                group = x[:, bass.ts(t, GT), :]
                nc.vector.tensor_tensor(group, FA.rearrange("p (j f) -> p j f", f=DIM), group, ALU.add).then_inc(x_done, 1)

        def dve_work(dve, t, u, nxt, prev):
            dve.wait_ge(dtu_ready, t + 1)
            for n in range(N):
                s = n % 2
                dve.wait_ge(rows_in_psum, N * t + n + 1)
                for c in range(C):
                    last = nc.vector.tensor_tensor(drive[:, s, c, :], dtu[:, u, c, :], b_bank(n), ALU.mult)
                last.then_inc(drive_ready, 1)
                dve.wait_ge(drive_ready, N * t + n + 1)
                dve.wait_ge(decay_ready, N * t + n + 1)
                for c in range(C):
                    for q in range(GS):
                        seq = slice(q * SEQ_LEN, (q + 1) * SEQ_LEN)
                        last = nc.vector.tensor_tensor_scan(state[:, s, c, seq], decay[:, s, c, seq],
                                                            drive[:, s, c, seq], 0.0, ALU.mult, ALU.add)
                last.then_inc(state_ready, 1)
                if prev is not None:
                    dve_finish(dve, n, prev, 1 - u)
                if nxt is not None:
                    dve_front(dve, n, nxt, 1 - u)

        def act_front(act, n, t, u):
            if n == 3:
                act.wait_ge(hT_in_psum, t + 1)
                nc.scalar.activation(hT[:], FA, ACT.Copy).then_inc(hT_ready, 1)
            if n == 4:
                act.wait_ge(xin_in_psum, t + 1)
                for c, bank in enumerate((FA, FB)):
                    last = nc.scalar.activation(padded[:, c, :, PAD:PAD + SEQ_LEN],
                                                bank.rearrange("p (q l) -> p q l", l=SEQ_LEN), ACT.Copy)
                last.then_inc(xin_ready, 1)
            if n == 8:
                act.wait_ge(z_in_psum, t + 1)
                for c, bank in enumerate((FA, FB)):
                    nc.scalar.activation(z_act[:, u, c, :], bank, ACT.Silu)
                act.wait_ge(conv_steps, C * SSM_TAPS * (t + 1))
                nc.scalar.activation(u_act[:, u], conv[:].rearrange("p c q l -> p c (q l)"), ACT.Silu).then_inc(u_ready, 1)
            if n == 11:
                act.wait_ge(dt_in_psum, t + 1)
                for c, bank in enumerate((FA, FB)):
                    nc.scalar.activation(soft_pos[:, c, :], bank, ACT.Relu, bias=b_dt[:, c:c + 1])
                    last = nc.scalar.activation(soft_abs[:, c, :], bank, ACT.Abs, bias=b_dt[:, c:c + 1])
                last.then_inc(soft_steps, 1)
            if n == 12:
                act.wait_ge(soft_steps, 2 * t + 1)
                nc.scalar.activation(soft_exp[:], soft_abs[:], ACT.Exp, scale=-1.0).then_inc(soft_steps, 1)
                act.wait_ge(soft_steps, 2 * t + 2)
                nc.scalar.activation(soft_ln[:], soft_exp[:], ACT.Ln, bias=1.0).then_inc(soft_ready, 1)

        def act_work(act, t, u, nxt, prev):
            act.wait_ge(dt_ready, t + 1)
            for n in range(N):
                s = n % 2
                act.wait_ge(rows_in_psum, N * t + n + 1)
                for c in range(C):
                    last = nc.scalar.activation(decay[:, s, c, :], dt[:, u, c, :], ACT.Exp, scale=A[:, c, n:n + 1])
                last.then_inc(decay_ready, 1)
                nc.scalar.activation(c_row[:, s, :], c_bank(n), ACT.Copy).then_inc(c_ready, 1)
                if nxt is not None:
                    act_front(act, n, nxt, 1 - u)

        def pool_front(pool, n, t, u):
            if n == 2:
                norm_rstd(k, pool, norm, t)

        def pool_work(pool, t, u, nxt, prev):
            for n in range(N):
                s = n % 2
                pool.wait_ge(state_ready, N * t + n + 1)
                pool.wait_ge(c_ready, N * t + n + 1)
                nc.gpsimd.tensor_tensor(read[:, s], state[:, s],
                                        c_row[:, s:s + 1, :].broadcast_to([P, C, W]), ALU.mult).then_inc(read_ready, 1)
                if nxt is not None:
                    pool_front(pool, n, nxt, 1 - u)

        def nothing(eng, n, t, u):
            pass

        with nc.Block() as block:
            @block.tensor
            def _(pe):
                run(pe, pe_work, pe_front, pe_finish)

            @block.vector
            def _(dve):
                nc.vector.memset(padded[:], 0.0).then_inc(padding_zero, 1)
                dve.wait_ge(A_exp_ready, 1)
                nc.vector.tensor_scalar(A[:], A[:], -1.0, None, ALU.mult).then_inc(A_ready, 1)
                run(dve, dve_work, dve_front, dve_finish)

            @block.scalar
            def _(act):
                nc.scalar.activation(A[:], a_log[:], ACT.Exp).then_inc(A_exp_ready, 1)
                act.wait_ge(A_ready, 1)
                act.wait_ge(padding_zero, 1)
                run(act, act_work, act_front, nothing)

            @block.gpsimd
            def _(pool):
                run(pool, pool_work, pool_front, nothing)


HEADS, HEAD_DIM, WINDOW = 8, 64, 64
INNER = HEADS * HEAD_DIM
HID_CHUNKS = 3
MASKED = -1e30


def local_attention_stage(k, name):
    nc, psum, x, y = k.nc, k.psum, k.x, k.y
    T = SEQ_LEN // P
    LAYERS = k.dram["loc_wa"].shape[0]
    HP = HEADS // 2
    HALF = HP // 2
    STEPS = 4
    QK = 2 * INNER
    GT = 4
    FGROUPS = TILES // GT
    GS = GT // T
    cos, sin, scale, scale_swapped = (k.const[f"loc_{n}"] for n in ("cos", "sin", "scale", "scale_swapped"))
    mask, ident_bf = k.const["loc_mask"], k.const["loc_ident"]
    ln_g, ln_b, b1, b2 = (k.const[f"loc_{n}"] for n in ("lng", "lnb", "b1", "b2"))

    with ExitStack() as mem:
        def sb(n, shape, dtype=FP32):
            return k.sbuf(f"{name}_{n}", shape, dtype, mem)

        rows_a = sb("rows_a", [P, 2, T, DIM])
        rows_f = sb("rows_f", [P, 2, GT, DIM])
        wa = sb("wa", [P, 3 * INNER + HP * DIM])
        w_qkv, w_o = wa[:, 0:3 * INNER], wa[:, 3 * INNER:].rearrange("p (c n) -> p c n", n=DIM)
        wf = sb("wf", [P, 2 * HID_CHUNKS * P + HID_CHUNKS * DIM])
        w_1 = wf[:, 0:2 * HID_CHUNKS * P].rearrange("p (c n) -> p c n", n=P)
        w_2 = wf[:, 2 * HID_CHUNKS * P:].rearrange("p (c n) -> p c n", n=DIM)
        rot_cos = sb("rot_cos", [P, LAYERS * T, 2, HEAD_DIM])
        rot_sin = sb("rot_sin", [P, LAYERS * T, 2, HEAD_DIM])
        hT = sb("hT", [P, SEQ_LEN])
        raw = sb("raw", [P, T, QK])
        square = sb("square", [P, T, QK])
        ss = sb("ss", [P, T, 2 * HEADS])
        ss_guard = sb("ss_guard", [P, T, 2 * HEADS])
        inv_norm = sb("inv_norm", [P, T, 2 * HEADS])
        by_sin = sb("by_sin", [P, T, QK])
        qk = sb("qk", [P, T, QK])
        qT = sb("qT", [P, 2, HP, SEQ_LEN])
        kT = sb("kT", [P, 2, HP, SEQ_LEN])
        v = sb("v", [P, 2, T, INNER])
        v_mid = sb("v_mid", [P, 2, INNER])
        top = sb("top", [P, STEPS, STEPS])
        total = sb("total", [P, STEPS, STEPS])
        inv_total = sb("inv_total", [P, STEPS, STEPS])
        prob = sb("prob", [P, STEPS, 512])
        prob_T = sb("prob_T", [P, 2, 512])
        oT = sb("oT", [P, HP, SEQ_LEN])
        fh = sb("fh", [P, GT, P])
        fhT = sb("fhT", [P, 2, GT * P])
        gelu = sb("gelu", [P, HID_CHUNKS, GT * P])
        hid = sb("hid", [P, HID_CHUNKS, GT * P])
        outer = add_norm_buffers(k, f"{name}_outer", "loc_outer", 2 * GT, mem)
        inner = add_norm_buffers(k, f"{name}_inner", "loc_inner", GT, mem)

        def sem(n):
            return k.sem(f"loc_{n}")
        tables_steps, wa_loaded, wf_loaded, edge_zero = sem("tables_steps"), sem("wa_loaded"), sem("wf_loaded"), sem("edge_zero")
        y_for_attn, y_for_ffn = sem("y_for_attn"), sem("y_for_ffn")
        sh_for_attn = [sem(f"sh_for_attn{u}") for u in range(2)]
        sh_for_ffn = [sem(f"sh_for_ffn{u}") for u in range(2)]
        hT_in_psum, hT_ready = sem("hT_in_psum"), sem("hT_ready")
        qk_in_psum, v_in_psum = sem("qk_in_psum"), sem("v_in_psum")
        raw_ready, square_ready, v_ready = sem("raw_ready"), sem("square_ready"), sem("v_ready")
        ss_ready, guard_ready, inv_norm_ready = sem("ss_ready"), sem("guard_ready"), sem("inv_norm_ready")
        by_cos_ready, by_sin_ready, sum_ready, rot_ready = sem("by_cos_ready"), sem("by_sin_ready"), sem("sum_ready"), sem("rot_ready")
        qkT_in_psum, qkT_ready = sem("qkT_in_psum"), sem("qkT_ready")
        scores_in_psum, top_ready, shifted_ready = sem("scores_in_psum"), sem("top_ready"), sem("shifted_ready")
        exp_ready, total_ready, inv_total_ready = sem("exp_ready"), sem("total_ready"), sem("inv_total_ready")
        prob_ready, prob_T_in_psum, prob_T_ready = sem("prob_ready"), sem("prob_T_in_psum"), sem("prob_T_ready")
        oT_in_psum, oT_ready, attn_in_psum = sem("oT_in_psum"), sem("oT_ready"), sem("attn_in_psum")
        fh_ready, fhT_in_psum, fhT_ready = sem("fh_ready"), sem("fhT_in_psum"), sem("fhT_ready")
        up_done, gelu_ready, hid_ready = sem("up_done"), sem("gelu_ready"), sem("hid_ready")
        ffn_in_psum, bias_added = sem("ffn_in_psum"), sem("bias_added")

        QK_BANKS = psum[:, 0:2, :]
        V_BANK = psum[:, 2, :]
        HT = psum[:, 3, 0:SEQ_LEN]
        ATTN = psum[:, 3, SEQ_LEN:2 * SEQ_LEN]
        PT_BANK = psum[:, 6, :]
        OT_BANK = psum[:, 7, :]

        def score_bank(e):
            return psum[:, 4 + e, :]

        def run_attention(eng, l, work, first):
            first(eng, l)
            with eng.Fori(0, SEQS // 2 - 1) as i:
                work(eng, l, 2 * i, 0, 2 * i + 1, 2 * i + 2, i + 1)
                work(eng, l, 2 * i + 1, 1, 2 * i + 2, 2 * i + 3, i + 1)
            work(eng, l, SEQS - 2, 0, SEQS - 1, None, None)
            work(eng, l, SEQS - 1, 1, None, None, None)

        def seq(l, t):
            return SEQS * l + t

        START = 1
        FREE = 2

        def transpose_rows(pe, l, t, u, pair):
            pe.wait_ge(sh_for_attn[u], 48 * (SEQS // 2 * l + pair + 1))
            for j in range(T):
                last = nc.tensor.transpose(HT[:, j * P:(j + 1) * P], rows_a[:, u, j, :], k.ident[:])
            last.then_inc(hT_in_psum, 1)

        def project_qk(pe, l, t, j):
            i = T * seq(l, t) + j
            if j == 0:
                pe.wait_ge(hT_ready, seq(l, t) + 1)
                pe.wait_ge(qkT_ready, START + 2 * i)
            else:
                pe.wait_ge(raw_ready, START + i)
            for b in range(2):
                last = nc.tensor.matmul(QK_BANKS[:, b, :], hT[:, j * P:(j + 1) * P],
                                        w_qkv[:, b * INNER:(b + 1) * INNER], start=True, stop=True)
            last.then_inc(qk_in_psum, 1)

        def project_v(pe, l, t, j):
            pe.wait_ge(v_ready, START + T * seq(l, t) + j)
            nc.tensor.matmul(V_BANK, hT[:, j * P:(j + 1) * P], w_qkv[:, QK:QK + INNER], start=True, stop=True)\
              .then_inc(v_in_psum, 1)

        def transpose_qk(pe, l, t, j, b):
            i = T * seq(l, t) + j
            if b == 0:
                pe.wait_ge(rot_ready, i + 1)
            if j == 0:
                pe.wait_ge(raw_ready, START + i + T)
            else:
                pe.wait_ge(qkT_ready, START + 2 * i + b - 1)
            for c in range(HP):
                last = nc.tensor.transpose(QK_BANKS[:, b, c * P:(c + 1) * P],
                                           qk[:, j, b * INNER + c * P:b * INNER + (c + 1) * P], k.ident[:])
            last.then_inc(qkT_in_psum, 1)

        def scores(pe, l, t, u, half):
            if half == 0:
                pe.wait_ge(qkT_ready, START + 2 * T * (seq(l, t) + 1))
            else:
                pe.wait_ge(shifted_ready, STEPS * seq(l, t) + 2)
            for e in range(2):
                last = nc.tensor.matmul(score_bank(e), ident_bf[:], mask[:], start=True, stop=False,
                                        skip_group_check=True)
            for c in range(HALF):
                for w in range(SEQ_LEN // WINDOW):
                    rows = slice(WINDOW * (w % 2), WINDOW * (w % 2) + WINDOW)
                    col = (c * 2 + w // 2) * P
                    if w == 2:
                        parts = [(col, w * WINDOW, WINDOW), (col + WINDOW, (w - 1) * WINDOW, WINDOW)]
                    else:
                        parts = [(col, (w // 2) * P, P)]
                    for at, key, n in parts:
                        for e in range(2):
                            d = slice(HEAD_DIM * e, HEAD_DIM * (e + 1))
                            last = nc.tensor.matmul(score_bank(e)[rows, at:at + n],
                                                    qT[d, u, HALF * half + c, w * WINDOW:(w + 1) * WINDOW],
                                                    kT[d, u, HALF * half + c, key:key + n],
                                                    start=False, stop=True, skip_group_check=True)
            last.then_inc(scores_in_psum, 1)

        def transpose_prob(pe, l, t, a):
            pe.wait_ge(prob_ready, STEPS * seq(l, t) + a + 1)
            for i in range(4):
                last = nc.tensor.transpose(PT_BANK[:, i * P:(i + 1) * P], prob[:, a, i * P:(i + 1) * P], k.ident[:])
            last.then_inc(prob_T_in_psum, 1)

        def weighted(pe, l, t, u, a):
            half, e = a // 2, a % 2
            if a == 0:
                pe.wait_ge(v_ready, START + T * (seq(l, t) + 1))
            if e == 0:
                pe.wait_ge(oT_ready, START + 2 * seq(l, t) + half)
            pe.wait_ge(prob_T_ready, STEPS * seq(l, t) + a + 1)
            for c in range(HALF):
                head = 2 * (HALF * half + c) + e
                d = slice(HEAD_DIM * head, HEAD_DIM * (head + 1))
                out = OT_BANK[HEAD_DIM * e:HEAD_DIM * (e + 1), c * SEQ_LEN:(c + 1) * SEQ_LEN]
                p0 = prob_T[:, a % 2, 2 * c * P:(2 * c + 1) * P]
                p1 = prob_T[:, a % 2, (2 * c + 1) * P:(2 * c + 2) * P]
                nc.tensor.matmul(out[:, 0:P], v[:, u, 0, d], p0, start=True, stop=True)
                nc.tensor.matmul(out[:, P:P + WINDOW], v_mid[:, u, d], p1[:, 0:WINDOW], start=True, stop=True)
                last = nc.tensor.matmul(out[:, P + WINDOW:2 * P], v[:, u, 1, d], p1[:, WINDOW:P], start=True, stop=True)
            last.then_inc(oT_in_psum, 1)

        def attention_out(pe, l, t, after):
            pe.wait_ge(oT_ready, START + 2 * seq(l, t) + 2)
            if after is not None:
                pe.wait_ge(hT_ready, seq(l, after) + 1)
            for j in range(T):
                for c in range(HP):
                    last = nc.tensor.matmul(ATTN[:, j * P:(j + 1) * P], oT[:, c, j * P:(j + 1) * P], w_o[:, c, :],
                                            start=(c == 0), stop=(c == HP - 1))
            last.then_inc(attn_in_psum, 1)

        def pe_first(pe, l):
            transpose_rows(pe, l, 0, 0, 0)
            for j in range(T):
                project_qk(pe, l, 0, j)
                project_v(pe, l, 0, j)
            transpose_rows(pe, l, 1, 1, 0)
            for j in range(T):
                for b in range(2):
                    transpose_qk(pe, l, 0, j, b)

        def pe_attention(pe, l, t, u, nxt, after, pair):
            scores(pe, l, t, u, 0)
            if nxt is not None:
                project_qk(pe, l, nxt, 0)
                project_v(pe, l, nxt, 0)
                project_qk(pe, l, nxt, 1)
            scores(pe, l, t, u, 1)
            transpose_prob(pe, l, t, 0)
            if nxt is not None:
                project_v(pe, l, nxt, 1)
            weighted(pe, l, t, u, 0)
            transpose_prob(pe, l, t, 1)
            if after is not None:
                pe.wait_ge(y_for_ffn, START + seq(l, t))
                transpose_rows(pe, l, after, u, pair)
            weighted(pe, l, t, u, 1)
            transpose_prob(pe, l, t, 2)
            if nxt is not None:
                transpose_qk(pe, l, nxt, 0, 0)
                transpose_qk(pe, l, nxt, 0, 1)
            weighted(pe, l, t, u, 2)
            transpose_prob(pe, l, t, 3)
            if nxt is not None:
                transpose_qk(pe, l, nxt, 1, 0)
            weighted(pe, l, t, u, 3)
            if nxt is not None:
                transpose_qk(pe, l, nxt, 1, 1)
            attention_out(pe, l, t, after)

        def heads(ap):
            return ap.rearrange("p (s h d) -> p s h d", s=2, d=HEAD_DIM)

        def by_head(ap):
            return ap.rearrange("p (h d) -> p h d", d=HEAD_DIM)

        def table(tab, l, j, cols=slice(0, HEAD_DIM)):
            one = tab[:, bass.ts(T * l + j, 1), :, cols].rearrange("p a s d -> p (a s) d")
            return one.unsqueeze(2).broadcast_to([P, 2, HEADS, cols.stop - cols.start])

        def head_squares(dve, l, t, j):
            i = T * seq(l, t) + j
            dve.wait_ge(square_ready, i + 1)
            nc.vector.tensor_reduce(ss[:, j], by_head(square[:, j]), AX.X, ALU.add).then_inc(ss_ready, 1)
            dve.wait_ge(ss_ready, i + 1)
            nc.vector.tensor_scalar(ss_guard[:, j], ss[:, j], 1e-24, None, ALU.max).then_inc(guard_ready, 1)

        def times_cos(dve, l, t, j):
            dve.wait_ge(raw_ready, START + T * seq(l, t) + j + 1)
            nc.vector.tensor_tensor(heads(qk[:, j]), heads(raw[:, j]), table(rot_cos, l, j), ALU.mult)\
              .then_inc(by_cos_ready, 1)

        def rotated(dve, l, t, j):
            i = T * seq(l, t) + j
            dve.wait_ge(by_cos_ready, i + 1)
            dve.wait_ge(by_sin_ready, i + 1)
            nc.vector.tensor_tensor(qk[:, j], qk[:, j], by_sin[:, j], ALU.add).then_inc(sum_ready, 1)

        def unit_norm(dve, l, t, j):
            i = T * seq(l, t) + j
            dve.wait_ge(sum_ready, i + 1)
            dve.wait_ge(inv_norm_ready, i + 1)
            nc.vector.tensor_tensor(by_head(qk[:, j]), by_head(qk[:, j]),
                                    inv_norm[:, j].unsqueeze(2).broadcast_to([P, 2 * HEADS, HEAD_DIM]),
                                    ALU.mult).then_inc(rot_ready, 1)

        def by_row(ap):
            return ap.rearrange("p (g c) -> p g c", c=P)

        def minus_top(dve, l, t, a):
            bank = by_row(score_bank(a % 2))
            dve.wait_ge(scores_in_psum, 2 * seq(l, t) + a // 2 + 1)
            nc.vector.tensor_reduce(top[:, a, :], bank, AX.X, ALU.max).then_inc(top_ready, 1)
            dve.wait_ge(top_ready, STEPS * seq(l, t) + a + 1)
            nc.vector.tensor_tensor(by_row(prob[:, a]), bank, top[:, a, :].unsqueeze(2).broadcast_to([P, STEPS, P]),
                                    ALU.subtract).then_inc(shifted_ready, 1)

        def row_totals(dve, l, t, a):
            idx = STEPS * seq(l, t) + a
            dve.wait_ge(exp_ready, idx + 1)
            nc.vector.tensor_reduce(total[:, a, :], by_row(prob[:, a]), AX.X, ALU.add).then_inc(total_ready, 1)
            dve.wait_ge(total_ready, idx + 1)
            nc.vector.reciprocal(inv_total[:, a, :], total[:, a, :]).then_inc(inv_total_ready, 1)

        def dve_first(dve, l):
            for j in range(T):
                times_cos(dve, l, 0, j)
                head_squares(dve, l, 0, j)
            for j in range(T):
                rotated(dve, l, 0, j)
                unit_norm(dve, l, 0, j)

        def dve_attention(dve, l, t, u, nxt, after, pair):
            minus_top(dve, l, t, 0)
            minus_top(dve, l, t, 1)
            row_totals(dve, l, t, 0)
            row_totals(dve, l, t, 1)
            if nxt is not None:
                for j in range(T):
                    times_cos(dve, l, nxt, j)
                    head_squares(dve, l, nxt, j)
            minus_top(dve, l, t, 2)
            minus_top(dve, l, t, 3)
            row_totals(dve, l, t, 2)
            row_totals(dve, l, t, 3)
            if nxt is not None:
                for j in range(T):
                    rotated(dve, l, nxt, j)
                    unit_norm(dve, l, nxt, j)
            dve.wait_ge(attn_in_psum, START + seq(l, t) + 1)
            rows = y[:, bass.ts(t, T), :]
            nc.vector.tensor_tensor(rows, ATTN.rearrange("p (j f) -> p j f", f=DIM), rows,
                                    ALU.add).then_inc(y_for_ffn, 1)

        def copy_hT(act, l, t):
            act.wait_ge(hT_in_psum, seq(l, t) + 1 + FREE)
            nc.scalar.activation(hT[:], HT, ACT.Copy).then_inc(hT_ready, 1)

        def copy_qk(act, l, t, j):
            i = T * seq(l, t) + j
            act.wait_ge(qk_in_psum, i + 1)
            nc.scalar.activation(raw[:, j], QK_BANKS.rearrange("p b n -> p (b n)"), ACT.Copy).then_inc(raw_ready, 1)

        def square_qk(act, l, t, j):
            act.wait_ge(raw_ready, START + T * seq(l, t) + j + 1)
            nc.scalar.activation(square[:, j], raw[:, j], ACT.Square).then_inc(square_ready, 1)

        def copy_v(act, l, t, u, j):
            act.wait_ge(v_in_psum, T * seq(l, t) + j + 1)
            half = slice(64, P) if j == 0 else slice(0, 64)
            nc.scalar.activation(v_mid[half, u, :], V_BANK[half, :], ACT.Copy)
            nc.scalar.activation(v[:, u, j, :], V_BANK, ACT.Copy).then_inc(v_ready, 1)

        def copy_qkT(act, l, t, u, j, b):
            act.wait_ge(qkT_in_psum, 2 * (T * seq(l, t) + j) + b + 1)
            dst = (qT, kT)[b]
            nc.scalar.activation(dst[:, u, :, j * P:(j + 1) * P],
                                 QK_BANKS[:, b, :].rearrange("p (c n) -> p c n", n=P), ACT.Copy).then_inc(qkT_ready, 1)

        def exponential(act, l, t, a):
            act.wait_ge(shifted_ready, STEPS * seq(l, t) + a + 1)
            nc.scalar.activation(prob[:, a], prob[:, a], ACT.Exp).then_inc(exp_ready, 1)

        def copy_prob_T(act, l, t, a):
            act.wait_ge(prob_T_in_psum, STEPS * seq(l, t) + a + 1)
            nc.scalar.activation(prob_T[:, a % 2, :], PT_BANK, ACT.Copy).then_inc(prob_T_ready, 1)

        def copy_oT(act, l, t, half):
            act.wait_ge(oT_in_psum, STEPS * seq(l, t) + 2 * half + 2)
            nc.scalar.activation(oT[:, HALF * half:HALF * (half + 1), :],
                                 OT_BANK.rearrange("p (c n) -> p c n", n=SEQ_LEN), ACT.Copy).then_inc(oT_ready, 1)

        def act_first(act, l):
            copy_hT(act, l, 0)
            for j in range(T):
                copy_qk(act, l, 0, j)
                square_qk(act, l, 0, j)
                copy_v(act, l, 0, 0, j)
            copy_hT(act, l, 1)
            for j in range(T):
                for b in range(2):
                    copy_qkT(act, l, 0, 0, j, b)

        def act_attention(act, l, t, u, nxt, after, pair):
            exponential(act, l, t, 0)
            exponential(act, l, t, 1)
            if nxt is not None:
                copy_qk(act, l, nxt, 0)
                square_qk(act, l, nxt, 0)
                copy_v(act, l, nxt, 1 - u, 0)
                copy_qk(act, l, nxt, 1)
                square_qk(act, l, nxt, 1)
            copy_prob_T(act, l, t, 0)
            if nxt is not None:
                copy_v(act, l, nxt, 1 - u, 1)
            exponential(act, l, t, 2)
            copy_prob_T(act, l, t, 1)
            exponential(act, l, t, 3)
            if after is not None:
                copy_hT(act, l, after)
            copy_oT(act, l, t, 0)
            copy_prob_T(act, l, t, 2)
            if nxt is not None:
                copy_qkT(act, l, nxt, 1 - u, 0, 0)
                copy_qkT(act, l, nxt, 1 - u, 0, 1)
            copy_prob_T(act, l, t, 3)
            if nxt is not None:
                copy_qkT(act, l, nxt, 1 - u, 1, 0)
            copy_oT(act, l, t, 1)
            if nxt is not None:
                copy_qkT(act, l, nxt, 1 - u, 1, 1)

        def inverse_norms(pool, l, t, j):
            i = T * seq(l, t) + j
            pool.wait_ge(guard_ready, i + 1)
            nc.gpsimd.tensor_tensor(inv_norm[:, j], ss_guard[:, j], k.neg_half[:, 0:2 * HEADS], ALU.pow)\
              .then_inc(inv_norm_ready, 1)

        def times_sin(pool, l, t, j):
            settle(pool, raw_ready, START + T * seq(l, t) + j + 1)
            H = HEAD_DIM // 2
            lo, hi = slice(0, H), slice(H, HEAD_DIM)
            nc.gpsimd.tensor_tensor(heads(by_sin[:, j])[:, :, :, lo], heads(raw[:, j])[:, :, :, hi],
                                    table(rot_sin, l, j, lo), ALU.mult)
            nc.gpsimd.tensor_tensor(heads(by_sin[:, j])[:, :, :, hi], heads(raw[:, j])[:, :, :, lo],
                                    table(rot_sin, l, j, hi), ALU.mult).then_inc(by_sin_ready, 1)

        def divide(pool, l, t, a):
            pool.wait_ge(inv_total_ready, STEPS * seq(l, t) + a + 1)
            nc.gpsimd.tensor_tensor(by_row(prob[:, a]), by_row(prob[:, a]),
                                    inv_total[:, a, :].unsqueeze(2).broadcast_to([P, STEPS, P]),
                                    ALU.mult).then_inc(prob_ready, 1)

        def pool_first(pool, l):
            for j in range(T):
                times_sin(pool, l, 0, j)
                inverse_norms(pool, l, 0, j)

        def pool_attention(pool, l, t, u, nxt, after, pair):
            divide(pool, l, t, 0)
            divide(pool, l, t, 1)
            if nxt is not None:
                times_sin(pool, l, nxt, 0)
                inverse_norms(pool, l, nxt, 0)
                times_sin(pool, l, nxt, 1)
            divide(pool, l, t, 2)
            divide(pool, l, t, 3)
            if nxt is not None:
                inverse_norms(pool, l, nxt, 1)

        def a_bank(c): return psum[:, 2 * c, :]
        def g_bank(c): return psum[:, 2 * c + 1, :]
        F_OUT, F_HT = psum[:, 6, :], psum[:, 7, :]
        C = HID_CHUNKS

        def group(l, g):
            return FGROUPS * l + g

        def run_ffn(eng, l, work):
            work(eng, l, None, None, 0, 0, 0)
            with eng.Fori(0, FGROUPS // 2 - 1) as i:
                work(eng, l, 2 * i, 0, 2 * i + 1, 1, i)
                work(eng, l, 2 * i + 1, 1, 2 * i + 2, 0, i + 1)
            work(eng, l, FGROUPS - 2, 0, FGROUPS - 1, 1, FGROUPS // 2 - 1)
            work(eng, l, FGROUPS - 1, 1, None, None, None)

        def pe_ffn(pe, l, g, u, n, un, pair):
            def up(c):
                nc.tensor.matmul(a_bank(c), w_1[:, c, :], fhT[:, u, :], start=True, stop=True)
                nc.tensor.matmul(g_bank(c), w_1[:, C + c, :], fhT[:, u, :], start=True, stop=True).then_inc(up_done, 1)

            def down(c):
                pe.wait_ge(hid_ready, C * group(l, g) + c + 1)
                if c == 0:
                    pe.wait_ge(y_for_attn, SEQS + GS * group(l, g))
                for j in range(GT):
                    last = nc.tensor.matmul(F_OUT[:, j * P:(j + 1) * P], hid[:, c, j * P:(j + 1) * P], w_2[:, c, :],
                                            start=(c == 0 and j == 0), stop=(c == C - 1), skip_group_check=True)
                if c == C - 1:
                    last.then_inc(ffn_in_psum, 1)
            if g is not None:
                pe.wait_ge(fhT_ready, group(l, g) + 1)
                up(0)
                up(1)
                down(0)
                up(2)
                down(1)
            if n is not None:
                pe.wait_ge(fh_ready, group(l, n) + 1 + FREE)
                for j in range(GT):
                    last = nc.tensor.transpose(F_HT[:, j * P:(j + 1) * P], fh[:, j, :], k.ident[:])
                last.then_inc(fhT_in_psum, 1)
            if g is not None:
                down(2)

        def dve_ffn(dve, l, g, u, n, un, pair):
            def hidden(c):
                idx = C * group(l, g) + c
                dve.wait_ge(gelu_ready, idx + 1)
                nc.vector.scalar_tensor_tensor(hid[:, c, :], a_bank(c), b1[:, bass.ts(2 * C * l + c, 1)],
                                               gelu[:, c, :], ALU.add, ALU.mult).then_inc(hid_ready, 1)
            if n is not None:
                dve.wait_ge(sh_for_ffn[un], 48 * (FGROUPS // 2 * l + pair + 1))
                norm_statistics(k, dve, inner, group(l, n), lambda j: rows_f[:, un, j, :])
            if g is not None:
                hidden(0)
            if n is not None:
                norm_apply(k, dve, inner, group(l, n), lambda j: fh[:, j, :], lambda j: rows_f[:, un, j, :],
                           (fh_ready, 1))
            if g is not None:
                hidden(1)
                hidden(2)
                dve.wait_ge(ffn_in_psum, START + group(l, g) + 1)
                dve.wait_ge(bias_added, group(l, g) + 1)
                rows = y[:, bass.ts(g, GT), :]
                nc.vector.tensor_tensor(rows, F_OUT.rearrange("p (j f) -> p j f", f=DIM), rows,
                                        ALU.add).then_inc(y_for_attn, GS)

        def act_ffn(act, l, g, u, n, un, pair):
            def gate(c):
                settle(act, up_done, C * group(l, g) + c + 1)
                nc.scalar.activation(gelu[:, c, :], g_bank(c), ACT.Gelu,
                                     bias=b1[:, bass.ts(2 * C * l + C + c, 1)]).then_inc(gelu_ready, 1)
            if g is not None:
                gate(0)
                gate(1)
            if n is not None:
                settle(act, fhT_in_psum, group(l, n) + 1)
                nc.scalar.activation(fhT[:, un, :], F_HT, ACT.Identity, bias=ln_b[:, bass.ts(l, 1)],
                                     scale=ln_g[:, bass.ts(l, 1)]).then_inc(fhT_ready, 1)
            if g is not None:
                gate(2)

        def pool_ffn(pool, l, g, u, n, un, pair):
            if n is not None:
                norm_rstd(k, pool, inner, group(l, n))
                settle(pool, sh_for_ffn[un], 48 * (FGROUPS // 2 * l + pair + 1))
                rows = y[:, bass.ts(n, GT), :]
                nc.gpsimd.tensor_tensor(rows, rows, b2[:, bass.ts(l, 1), :].broadcast_to([P, GT, DIM]),
                                        ALU.add).then_inc(bias_added, 1)

        def shift_rows(sp, dst, tile, n, done):
            src = y[:, bass.ts(tile, n), :]
            H = DIM // 2
            sp.dma_start(dst[:, :, 0:H], src[:, :, 0:H]).then_inc(done, 16)
            sp.dma_start(dst[1:P, :, H:DIM], src[0:P - 1, :, H:DIM]).then_inc(done, 16)
            sp.dma_start(dst[0:1, 1::2, H:DIM], src[P - 1:P, 0::2, H:DIM]).then_inc(done, 16)

        with nc.Block() as block:
            @block.sync
            def _(sp):
                sp.wait_ge(edge_zero, 2)
                with sp.Fori(0, LAYERS) as l:
                    sp.wait_ge(attn_in_psum, START + SEQS * l)
                    sp.dma_start(wa[:], k.dram["loc_wa"][bass.ts(l, 1)].rearrange("a p n -> p (a n)"))\
                      .then_inc(wa_loaded, 16)
                    sp.wait_ge(ffn_in_psum, START + FGROUPS * l)
                    sp.dma_start(wf[:], k.dram["loc_wf"][bass.ts(l, 1)].rearrange("a p n -> p (a n)"))\
                      .then_inc(wf_loaded, 16)
                    with sp.Fori(0, SEQS // 2) as i:
                        for u in range(2):
                            t = 2 * i + u
                            sp.wait_ge(hT_in_psum, seq(l, t) + 1)
                            sp.wait_ge(y_for_attn, seq(l, t) + 1)
                            shift_rows(sp, rows_a[:, u], t, T, sh_for_attn[u])
                    with sp.Fori(0, FGROUPS // 2) as i:
                        for u in range(2):
                            g = 2 * i + u
                            sp.wait_ge(fh_ready, group(l, g) + 1)
                            sp.wait_ge(y_for_ffn, START + SEQS * l + GS * (g + 1))
                            shift_rows(sp, rows_f[:, u], g, GT, sh_for_ffn[u])

            @block.tensor
            def _(pe):
                pe.sem_inc(hT_in_psum, FREE)
                pe.sem_inc(attn_in_psum, START)
                pe.sem_inc(ffn_in_psum, START)
                with pe.Fori(0, LAYERS) as l:
                    pe.wait_ge(y_for_attn, SEQS * (l + 1))
                    pe.wait_ge(wa_loaded, 16 * (l + 1))
                    run_attention(pe, l, pe_attention, pe_first)
                    pe.wait_ge(y_for_ffn, START + SEQS * (l + 1))
                    pe.wait_ge(wf_loaded, 16 * (l + 1))
                    run_ffn(pe, l, pe_ffn)

            @block.vector
            def _(dve):
                nc.vector.memset(rows_a[0:1, :, 0, DIM // 2:DIM], 0.0).then_inc(edge_zero, 1)
                nc.vector.memset(rows_f[0:1, :, 0::2, DIM // 2:DIM], 0.0).then_inc(edge_zero, 1)
                dve.sem_inc(fh_ready, FREE)
                dve.sem_inc(y_for_ffn, START)
                for l in range(LAYERS):
                    for tab, const, by in ((rot_cos, cos, scale), (rot_sin, sin, scale_swapped)):
                        nc.vector.tensor_tensor(tab[:, T * l:T * (l + 1)], const[:],
                                                by[:, l:l + 1].broadcast_to([P, T, 2, HEAD_DIM]),
                                                ALU.mult).then_inc(tables_steps, 1)
                dve.wait_ge(tables_steps, 2 * LAYERS)
                with dve.Fori(0, TILES // (2 * GT)) as g:
                    def tile(j, of=x): return of[:, bass.ts(2 * GT * g + j, 1), :]
                    norm_statistics(k, dve, outer, g, tile)
                    norm_apply(k, dve, outer, g, lambda j: tile(j, y), tile, (y_for_attn, 2 * GT // T))
                with dve.Fori(0, LAYERS) as l:
                    run_attention(dve, l, dve_attention, dve_first)
                    run_ffn(dve, l, dve_ffn)
                dve.wait_ge(y_for_attn, SEQS * (LAYERS + 1))
                with dve.Fori(0, TILES // (2 * GT)) as g:
                    rows = bass.ts(g, 2 * GT)
                    nc.vector.scalar_tensor_tensor(x[:, rows, :], y[:, rows, :], 0.5, x[:, rows, :],
                                                   ALU.mult, ALU.add)

            @block.scalar
            def _(act):
                for started in (raw_ready, qkT_ready, v_ready, oT_ready):
                    act.sem_inc(started, START)
                with act.Fori(0, LAYERS) as l:
                    run_attention(act, l, act_attention, act_first)
                    run_ffn(act, l, act_ffn)

            @block.gpsimd
            def _(pool):
                with pool.Fori(0, TILES // (2 * GT)) as g:
                    norm_rstd(k, pool, outer, g)
                pool.wait_ge(tables_steps, 2 * LAYERS)
                with pool.Fori(0, LAYERS) as l:
                    run_attention(pool, l, pool_attention, pool_first)
                    run_ffn(pool, l, pool_ffn)


def store_stage(k):
    nc = k.nc
    stored = k.sem("stored")
    with nc.Block() as block:
        @block.sync
        def _(sp):
            sp.dma_start(k.dram["out"], k.x[:]).then_inc(stored, 16)
            sp.wait_ge(stored, 16)


STAGES = {
    "moe1": (moe_stage, "moe", "moe1"),
    "l0": (linear_attention_stage, "lin", "lin"),
    "moe2": (moe_stage, "moe", "moe2"),
    "l1a": (local_attention_stage, "loc", "loc1"),
    "mamba": (state_space_stage, "ssm", "ssm"),
    "l1b": (local_attention_stage, "loc", "loc2"),
}


def build(nc, dram, stages):
    with ExitStack() as stack:
        k = Core(nc, dram, stack)
        load_stage(k)
        done = set()
        for s in stages:
            stage, kind, name = STAGES[s]
            if kind in done:
                k.clear(kind)
            done.add(kind)
            stage(k, name)
        store_stage(k)


def shape_constants():
    c = {"ident": np.eye(P, dtype=np.float32)}
    expert_of = 2 * np.arange(MOE_CHUNKS)[:, None] + np.arange(P)[None, :] // EXPERT_HID
    c["b_moe_sel"] = (np.arange(EXPERTS)[:, None, None] == expert_of[None]).astype(np.float32)
    c["c_moe_rank"] = np.broadcast_to(EXPERTS - np.arange(EXPERTS, dtype=np.float32), (P, 4, EXPERTS))
    pick = np.zeros((P, 2 * SSM_STATE, P), np.float32)
    for n in range(2 * SSM_STATE):
        pick[32 + n::32, n, :] = 1.0
    c["b_ssm_pick"] = pick.astype(np.float32)
    f = np.float32
    half = np.arange(0, HEAD_DIM, 2, dtype=f)
    inv_freq = f(1.0) / f(10000.0) ** (half / f(HEAD_DIM))
    pos = np.arange(SEQ_LEN, dtype=f)
    angle = pos[:, None] * inv_freq[None, :]
    base = (half + f(0.4 * HEAD_DIM)) / f(1.4 * HEAD_DIM)
    stretch = base[None, :] ** ((pos - SEQ_LEN // 2) / f(WINDOW // 2))[:, None]
    both = np.stack([8 * stretch, 1 / stretch], axis=1)
    cos, sin = np.cos(angle)[:, None] * both, np.sin(angle)[:, None] * both

    def by_tile(v):
        return v.reshape(SEQ_LEN // P, P, 2, HEAD_DIM).swapaxes(0, 1).astype(f)
    c["c_loc_cos"] = by_tile(np.concatenate([cos, cos], axis=-1))
    c["c_loc_sin"] = by_tile(np.concatenate([-sin, sin], axis=-1))
    i, j = np.arange(WINDOW)[:, None], np.arange(WINDOW)[None, :]
    own, before, never = j <= i, j >= i, np.zeros((WINDOW, WINDOW), bool)
    rows = [np.concatenate([own, never], 1), np.concatenate([before, own], 1),
            np.concatenate([own, before], 1), np.concatenate([before, own], 1)]
    pairs = np.concatenate([np.concatenate(rows[0:2]), np.concatenate(rows[2:4])], axis=1)
    c["b_loc_mask"] = np.where(np.tile(pairs, (1, 2)), 0, MASKED).astype(np.float32)
    c["b_loc_ident"] = np.eye(P).astype(np.float32)
    return c


def layouts(i):
    a = {}
    a["x"] = i["L0_attn_x"].reshape(TILES, P, DIM).transpose(1, 0, 2)
    a["c_moe_gate"] = i["L0_ffn_gate_w"].T
    a["c_moe_wg"] = i["L0_ffn_w_gate"].reshape(EXPERTS * EXPERT_HID, DIM).T
    a["c_moe_wu"] = i["L0_ffn_w_up"].reshape(EXPERTS * EXPERT_HID, DIM).T
    a["c_moe_wd"] = i["L0_ffn_w_down"].transpose(0, 2, 1).reshape(MOE_CHUNKS, P, DIM).transpose(1, 0, 2)
    qkv = i["L0_attn_w_qkv"]
    a["lin_w"] = np.concatenate([qkv[:, :, 0:DIM], qkv[:, :, DIM:2 * DIM],
                                 qkv[:, :, 2 * DIM:3 * DIM].transpose(0, 2, 1), i["L0_attn_w_out"]], axis=2)
    a["c_lin_gamma"] = i["L0_attn_gamma"].T
    a["c_lin_beta"] = i["L0_attn_beta"].T
    a["c_lin_bias"] = np.broadcast_to(i["L0_attn_b_out"], (P,) + i["L0_attn_b_out"].shape)
    chunks = SSM_INNER // P

    def by_chunk(v):
        return v.reshape((chunks, P) + v.shape[1:]).swapaxes(0, 1)
    a["c_ssm_win"] = i["L1_attn_W_in"]
    wx = i["L1_attn_W_xproj"]
    low, rows = wx[:, :SSM_RANK], wx[:, SSM_RANK:]
    a["c_ssm_wx"] = by_chunk(np.concatenate([low, np.zeros_like(low), rows, rows, rows], axis=1))
    a["c_ssm_wdt"] = i["L1_attn_W_dt"]
    a["c_ssm_wout"] = by_chunk(i["L1_attn_W_out"])
    a["c_ssm_taps"] = by_chunk(i["L1_attn_conv_k"][:, 0, :].T)
    a["c_ssm_convb"] = by_chunk(i["L1_attn_conv_b"])
    a["c_ssm_bdt"] = by_chunk(i["L1_attn_b_dt"])
    a["c_ssm_d"] = by_chunk(i["L1_attn_D"])
    a["c_ssm_alog"] = by_chunk(i["L1_attn_A_log"])
    layers = i["L1_ffn_wo"].shape[0]
    w_o = i["L1_ffn_wo"].reshape(layers, INNER // P, P, DIM).transpose(0, 2, 1, 3).reshape(layers, P, -1)
    a["loc_wa"] = np.concatenate([i["L1_ffn_wqkv"], w_o], axis=2)
    hid = i["L1_ffn_w2"].shape[1]

    def pad(v, axis):
        width = [(0, 0)] * v.ndim
        width[axis] = (0, HID_CHUNKS * P - hid)
        return np.pad(v, width)
    w1, b1 = i["L1_ffn_w1"], i["L1_ffn_b1"]
    w2 = pad(i["L1_ffn_w2"], 1).reshape(layers, HID_CHUNKS, P, DIM).transpose(0, 2, 1, 3).reshape(layers, P, -1)
    a["loc_wf"] = np.concatenate([pad(w1[..., :hid], 2), pad(w1[..., hid:], 2), w2], axis=2)
    b1 = np.stack([pad(b1[:, :hid], 1), pad(b1[:, hid:], 1)], axis=1)
    a["c_loc_b1"] = b1.reshape(layers * 2 * HID_CHUNKS, P).T
    a["c_loc_b2"] = np.broadcast_to(i["L1_ffn_b2"], (P,) + i["L1_ffn_b2"].shape)
    a["c_loc_lng"] = i["L1_ffn_ln_g"].T
    a["c_loc_lnb"] = i["L1_ffn_ln_b"].T
    scale = np.stack([i["L1_ffn_q_scale"], i["L1_ffn_k_scale"]], axis=1)
    a["c_loc_scale"] = np.broadcast_to(scale, (P,) + scale.shape)
    a["c_loc_scale_swapped"] = np.broadcast_to(np.roll(scale, HEAD_DIM // 2, axis=-1), (P,) + scale.shape)
    return a


ALL = ("moe1", "l0", "moe2", "l1a", "mamba", "l1b")


def program(nc, inputs, stages=ALL):
    arrays = {n: np.ascontiguousarray(a) for n, a in
              (layouts({n: np.asarray(v) for n, v in inputs.items()}) | shape_constants()).items()}
    dram = {n: nc.dram_tensor(n, a.shape, mybir.dt.from_np(a.dtype), kind="ExternalInput").ap()
            for n, a in arrays.items()}
    dram["out"] = nc.dram_tensor("out", (P, TILES, DIM), FP32, kind="ExternalOutput").ap()
    build(nc, dram, stages)
    return arrays


def kernel(**inputs):
    import concourse.bacc as _bacc
    from concourse.bass_utils import run_bass_kernel_spmd as _run

    nc = _bacc.Bacc("TRN2", target_bir_lowering=False, num_devices=1)
    arrays = program(nc, inputs)
    out = _run(nc, [arrays], core_ids=[0]).results[0]["out"]
    return out.transpose(1, 0, 2).reshape(SEQS, SEQ_LEN, DIM)
```

```python
from contextlib import ExitStack

import numpy as np
import concourse.bass as bass
from concourse import mybir

FP32 = mybir.dt.float32
BF16 = mybir.dt.bfloat16
ALU = mybir.AluOpType
ACT = mybir.ActivationFunctionType
AX = mybir.AxisListType

P = 128
SEQS, SEQ_LEN, DIM = 16, 256, 128
TOKENS = SEQS * SEQ_LEN
TILES = TOKENS // P
EPS = 1e-5

EXPERTS, EXPERT_HID = 8, 64
MOE_CHUNKS = EXPERTS * EXPERT_HID // P


class Core:

    def __init__(self, nc, dram, stack):
        self.nc, self.dram, self.stack, self.sems = nc, dram, stack, {}

    def sbuf(self, name, shape, dtype=FP32, stack=None):
        return (stack or self.stack).enter_context(self.nc.sbuf_tensor(f"{name}_sb", shape, dtype))

    def sem(self, name):
        if name not in self.sems:
            self.sems[name] = self.stack.enter_context(self.nc.semaphore(name))
        return self.sems[name]

    def clear(self, kind):
        with self.nc.Block() as block:
            @block.gpsimd
            def _(pool):
                for name, sem in self.sems.items():
                    if name.startswith(f"{kind}_"):
                        pool.sem_clear(sem)


def load_stage(k):
    nc, dram = k.nc, k.dram
    k.psum = k.stack.enter_context(nc.psum_tensor("psum", [P, 8, 512], FP32))
    k.x = k.sbuf("x", [P, TILES, DIM])
    k.y = k.sbuf("y", [P, TILES, DIM])
    k.ident = k.sbuf("ident", [P, P])
    k.neg_half = k.sbuf("neg_half", [P, 32])
    k.loaded = k.sem("loaded")
    k.loaded_late = k.sem("loaded_late")
    k.const = {}
    small = [n for n in dram if n.startswith(("c_", "b_"))]
    early = [n for n in small if n[2:].startswith("moe_")]
    late = [n for n in small if n not in early]
    landing = ExitStack()
    for n in small:
        k.const[n[2:]] = k.sbuf(n, list(dram[n].shape), FP32 if n.startswith("c_") else BF16)
    landed = {n: k.sbuf(f"{n}_landing", list(dram[n].shape), FP32, landing) if n.startswith("b_") else k.const[n[2:]]
              for n in small}
    consts_done = k.sem("consts_done")
    with nc.Block() as block:
        @block.sync
        def _(sp):
            sp.dma_start(k.x[:], dram["x"]).then_inc(k.loaded, 16)
            sp.dma_start(k.ident[:], dram["ident"]).then_inc(k.loaded, 16)
            for n in early:
                sp.dma_start(landed[n][:], dram[n]).then_inc(k.loaded, 16)
            for n in late:
                sp.dma_start(landed[n][:], dram[n]).then_inc(k.loaded_late, 16)
            sp.wait_ge(k.loaded, 16 * (len(early) + 2))

        @block.vector
        def _(dve):
            nc.vector.memset(k.neg_half[:], -0.5).then_inc(consts_done, 1)
            dve.wait_ge(k.loaded, 16 * (len(early) + 2))
            round_constants(k, early, landed)

    def load_rest():
        with nc.Block() as block:
            @block.vector
            def _(dve):
                dve.wait_ge(k.loaded_late, 16 * len(late))
                round_constants(k, late, landed)
        landing.close()
    return load_rest


def round_constants(k, names, landed):
    for n in names:
        if n.startswith("b_"):
            k.nc.vector.tensor_copy(k.const[n[2:]][:], landed[n][:])


def settle(eng, sem, value):
    eng.wait_ge(sem, value)
    eng.nop(nofuse=True)


def add_norm_buffers(k, name, kind, tiles, mem):
    b = type("NormBuffers", (), {})()
    b.tiles = tiles
    b.stats = k.sbuf(f"{name}_stats", [P, tiles, 6], FP32, mem)
    b.mv = k.sbuf(f"{name}_mv", [P, tiles, 2], FP32, mem)
    b.var_eps = k.sbuf(f"{name}_var_eps", [P, tiles], FP32, mem)
    b.rstd = k.sbuf(f"{name}_rstd", [P, tiles], FP32, mem)
    b.stats_done = k.sem(f"{kind}_stats_done")
    b.mean_done = k.sem(f"{kind}_mean_done")
    b.var_ready = k.sem(f"{kind}_var_ready")
    b.rstd_ready = k.sem(f"{kind}_rstd_ready")
    return b


def norm_statistics(k, dve, b, t, tile):
    nc = k.nc
    for j in range(b.tiles):
        last = nc.vector.bn_stats(b.stats[:, j, :], tile(j))
    last.then_inc(b.stats_done, 1)
    settle(dve, b.stats_done, t + 1)
    for j in range(b.tiles):
        last = nc.vector.bn_aggr(b.mv[:, j, :], b.stats[:, j, :])
    last.then_inc(b.mean_done, 1)
    dve.wait_ge(b.mean_done, t + 1)
    nc.vector.tensor_scalar(b.var_eps[:], b.mv[:, :, 1], EPS, None, ALU.add).then_inc(b.var_ready, 1)


def norm_rstd(k, pool, b, t):
    pool.wait_ge(b.var_ready, t + 1)
    k.nc.gpsimd.tensor_tensor(b.rstd[:], b.var_eps[:], k.neg_half[:, 0:b.tiles], ALU.pow).then_inc(b.rstd_ready, 1)


def norm_apply(k, dve, b, t, out, tile, done):
    dve.wait_ge(b.rstd_ready, t + 1)
    for j in range(b.tiles):
        last = k.nc.vector.tensor_scalar(out(j), tile(j), b.mv[:, j, 0:1], b.rstd[:, j:j + 1],
                                         ALU.subtract, ALU.mult)
    last.then_inc(*done)


def moe_stage(k, name):
    nc, psum, x = k.nc, k.psum, k.x
    wg, wu, wd = k.const["moe_wg"], k.const["moe_wu"], k.const["moe_wd"]
    gate_w, sel, rank = k.const["moe_gate"], k.const["moe_sel"], k.const["moe_rank"]
    GT = 4
    GROUPS = TILES // GT
    W = GT * P
    C = MOE_CHUNKS

    with ExitStack() as mem:
        def sb(n, shape, dtype=FP32):
            return k.sbuf(f"{name}_{n}", shape, dtype, mem)

        stats = sb("stats", [P, 2, GT, 6])
        mv = sb("mv", [P, 2, GT, 2])
        var_eps = sb("var_eps", [P, 2, GT])
        rstd = sb("rstd", [P, 2, GT])
        h = sb("h", [P, 2, GT, P])
        hT = sb("hT", [P, 2, W])
        top = sb("top", [P, 2, GT])
        is_top = sb("is_top", [P, 2, GT, EXPERTS])
        ranked = sb("ranked", [P, 2, GT, EXPERTS])
        first = sb("first", [P, 2, GT])
        onehot = sb("onehot", [P, 2, GT, EXPERTS])
        tanh = sb("tanh", [P, 2, GT])
        rw = sb("rw", [P, 2, GT])
        hs = sb("hs", [P, 2, GT, P])
        hsT = sb("hsT", [P, 2, W])
        maskT = sb("maskT", [EXPERTS, 2, W], BF16)
        silu = sb("silu", [P, 2, W])
        su = sb("su", [P, 2, W])
        hid = sb("hid", [P, 2, W])

        var_ready = k.sem(f"moe_var_ready")
        rstd_ready = k.sem(f"moe_rstd_ready")
        h_ready = k.sem(f"moe_h_ready")
        hT_in_psum = k.sem(f"moe_hT_in_psum")
        hT_ready = k.sem(f"moe_hT_ready")
        logits_ready = k.sem(f"moe_logits_ready")
        top_ready = k.sem(f"moe_top_ready")
        tanh_ready = k.sem(f"moe_tanh_ready")
        hs_ready = k.sem(f"moe_hs_ready")
        hsT_in_psum = k.sem(f"moe_hsT_in_psum")
        hsT_ready = k.sem(f"moe_hsT_ready")
        up_done = k.sem(f"moe_up_done")
        silu_ready = k.sem(f"moe_silu_ready")
        hid_ready = k.sem(f"moe_hid_ready")
        out_ready = k.sem(f"moe_out_ready")
        front = k.sem(f"moe_front_steps")
        FRONT = 6
        su_ready = k.sem(f"moe_su_ready")

        def bank(u):
            return psum[:, u, :]

        def slot(s, what):
            return psum[:, 2 + 3 * s + what, :]

        mask_bank = slot(C % 2, 2)

        def tiles(ap, t):
            return ap[:, bass.ts(t, GT), :]

        def run(eng, work):
            work(eng, None, None, 0, 0)
            with eng.Fori(0, GROUPS // 2 - 1) as i:
                work(eng, 2 * i, 0, 2 * i + 1, 1)
                work(eng, 2 * i + 1, 1, 2 * i + 2, 0)
            work(eng, GROUPS - 2, 0, GROUPS - 1, 1)
            work(eng, GROUPS - 1, 1, None, None)

        def transpose_h(pe, t, u):
            pe.wait_ge(h_ready, t + 1)
            for j in range(GT):
                last = nc.tensor.transpose(bank(u)[:, j * P:(j + 1) * P], h[:, u, j, :], k.ident[:])
            last.then_inc(hT_in_psum, 1)

        def gate(pe, t, u):
            pe.wait_ge(hT_ready, t + 1)
            for j in range(GT):
                last = nc.tensor.matmul(bank(u)[:, j * EXPERTS:(j + 1) * EXPERTS],
                                        hT[:, u, j * P:(j + 1) * P], gate_w[:], start=True, stop=True)
            last.then_inc(logits_ready, 1)

        def transpose_scaled(pe, t, u):
            pe.wait_ge(hs_ready, t + 1)
            for j in range(GT):
                nc.tensor.transpose(bank(u)[:, j * P:(j + 1) * P], hs[:, u, j, :], k.ident[:])
            for j in range(GT):
                last = nc.tensor.transpose(mask_bank[0:EXPERTS, j * P:(j + 1) * P],
                                           onehot[:, u, j, :], k.ident[:])
            last.then_inc(hsT_in_psum, 1)

        def up(t, u, c):
            s = c % 2
            nc.tensor.matmul(slot(s, 0), wg[:, c * P:(c + 1) * P], hsT[:, u, :], start=True, stop=True)
            nc.tensor.matmul(slot(s, 1), wu[:, c * P:(c + 1) * P], hsT[:, u, :], start=True, stop=True)
            nc.tensor.matmul(slot(s, 2), sel[:, c, :], maskT[:, u, :], start=True, stop=True).then_inc(up_done, 1)

        def down(pe, t, u, c):
            pe.wait_ge(hid_ready, C * t + c + 1)
            for j in range(GT):
                last = nc.tensor.matmul(bank(u)[:, j * P:(j + 1) * P], hid[:, c % 2, j * P:(j + 1) * P],
                                        wd[:, c, :], start=(c == 0 and j == 0), stop=(c == C - 1),
                                        skip_group_check=True)
            if c == C - 1:
                last.then_inc(out_ready, 1)

        def pe_work(pe, t, u, n, un):
            if t is not None:
                pe.wait_ge(hsT_ready, t + 1)
                up(t, u, 0)
            for c in range(C):
                if t is not None and c + 1 < C:
                    up(t, u, c + 1)
                if n is not None and c == C - 1:
                    transpose_scaled(pe, n, un)
                if t is not None:
                    down(pe, t, u, c)
                if n is not None and c == 0:
                    transpose_h(pe, n, un)
                if n is not None and c == 1:
                    gate(pe, n, un)

        def row_statistics(dve, t, u):
            for j in range(GT):
                last = nc.vector.bn_stats(stats[:, u, j, :], x[:, bass.ts(GT * t + j, 1), :])
            last.then_inc(front, 1)
            settle(dve, front, FRONT * t + 1)
            for j in range(GT):
                last = nc.vector.bn_aggr(mv[:, u, j, :], stats[:, u, j, :])
            last.then_inc(front, 1)
            dve.wait_ge(front, FRONT * t + 2)
            nc.vector.tensor_scalar(var_eps[:, u, :], mv[:, u, :, 1], EPS, None, ALU.add).then_inc(var_ready, 1)

        def normalize(dve, t, u):
            dve.wait_ge(rstd_ready, t + 1)
            for j in range(GT):
                last = nc.vector.tensor_scalar(h[:, u, j, :], x[:, bass.ts(GT * t + j, 1), :], mv[:, u, j, 0:1],
                                               rstd[:, u, j:j + 1], ALU.subtract, ALU.mult)
            last.then_inc(h_ready, 1)

        def choose(dve, t, u):
            dve.wait_ge(logits_ready, t + 1)
            logits = bank(u)[:, 0:GT * EXPERTS].rearrange("p (j e) -> p j e", e=EXPERTS)
            nc.vector.tensor_reduce(top[:, u, :], logits, AX.X, ALU.max).then_inc(top_ready, 1)
            dve.wait_ge(top_ready, t + 1)
            nc.vector.tensor_tensor(is_top[:, u], logits,
                                    top[:, u, :].unsqueeze(2).broadcast_to([P, GT, EXPERTS]),
                                    ALU.is_equal).then_inc(front, 1)
            dve.wait_ge(front, FRONT * t + 3)
            nc.vector.tensor_tensor(ranked[:, u], is_top[:, u], rank[:], ALU.mult).then_inc(front, 1)
            dve.wait_ge(front, FRONT * t + 4)
            nc.vector.tensor_reduce(first[:, u, :], ranked[:, u], AX.X, ALU.max).then_inc(front, 1)
            dve.wait_ge(front, FRONT * t + 5)
            nc.vector.tensor_tensor(onehot[:, u], ranked[:, u],
                                    first[:, u, :].unsqueeze(2).broadcast_to([P, GT, EXPERTS]), ALU.is_equal)
            dve.wait_ge(tanh_ready, t + 1)
            nc.vector.tensor_scalar(rw[:, u, :], tanh[:, u, :], 0.5, 0.5, ALU.mult, ALU.add).then_inc(front, 1)
            dve.wait_ge(front, FRONT * t + 6)
            for j in range(GT):
                last = nc.vector.tensor_scalar(hs[:, u, j, :], h[:, u, j, :], rw[:, u, j:j + 1], None, ALU.mult)
            last.then_inc(hs_ready, 1)

        def hidden(dve, t, u, c):
            s = c % 2
            dve.wait_ge(silu_ready, C * t + c + 1)
            nc.vector.tensor_tensor(su[:, s, :], silu[:, s, :], slot(s, 1), ALU.mult).then_inc(su_ready, 1)
            dve.wait_ge(su_ready, C * t + c + 1)
            nc.vector.tensor_tensor(hid[:, s, :], su[:, s, :], slot(s, 2), ALU.mult).then_inc(hid_ready, 1)

        def dve_work(dve, t, u, n, un):
            if n is not None:
                row_statistics(dve, n, un)
            for c in range(C):
                if t is not None:
                    hidden(dve, t, u, c)
                if n is not None and c == 0:
                    normalize(dve, n, un)
                if n is not None and c == 2:
                    choose(dve, n, un)
            if t is not None:
                dve.wait_ge(out_ready, t + 1)
                nc.vector.scalar_tensor_tensor(tiles(x, t), bank(u).rearrange("p (j f) -> p j f", f=DIM), 0.5,
                                               tiles(x, t), ALU.mult, ALU.add)

        def act_work(act, t, u, n, un):
            for c in range(C):
                if t is not None:
                    act.wait_ge(up_done, C * t + c + 1)
                    nc.scalar.activation(silu[:, c % 2, :], slot(c % 2, 0), ACT.Silu).then_inc(silu_ready, 1)
                if n is not None and c == 1:
                    act.wait_ge(hT_in_psum, n + 1)
                    nc.scalar.activation(hT[:, un, :], bank(un), ACT.Copy).then_inc(hT_ready, 1)
                if n is not None and c == 2:
                    act.wait_ge(top_ready, n + 1)
                    nc.scalar.activation(tanh[:, un, :], top[:, un, :], ACT.Tanh, scale=0.5).then_inc(tanh_ready, 1)
            if n is not None:
                act.wait_ge(hsT_in_psum, n + 1)
                nc.scalar.activation(hsT[:, un, :], bank(un), ACT.Copy)
                nc.scalar.activation(maskT[:, un, :], mask_bank[0:EXPERTS, :], ACT.Copy).then_inc(hsT_ready, 1)

        def pool_work(pool, t, u, n, un):
            if n is not None:
                pool.wait_ge(var_ready, n + 1)
                nc.gpsimd.tensor_tensor(rstd[:, un, :], var_eps[:, un, :], k.neg_half[:, 0:GT],
                                        ALU.pow).then_inc(rstd_ready, 1)

        with nc.Block() as block:
            @block.tensor
            def _(pe):
                run(pe, pe_work)

            @block.vector
            def _(dve):
                run(dve, dve_work)

            @block.scalar
            def _(act):
                run(act, act_work)

            @block.gpsimd
            def _(pool):
                run(pool, pool_work)


def linear_attention_stage(k, name="lin"):
    nc, psum, x, y = k.nc, k.psum, k.x, k.y
    S = 4
    GROUPS = SEQS // S
    T = SEQ_LEN // P
    T_LAG, M_LAG, G_LAG, F_LAG = 2, 6, 9, 13
    gamma, beta, bias = k.const["lin_gamma"], k.const["lin_beta"], k.const["lin_bias"]
    w_dram = k.dram["lin_w"]

    with ExitStack() as mem:
        def sb(n, shape):
            return k.sbuf(f"{name}_{n}", shape, FP32, mem)

        w = sb("w", [P, 2, 4 * P])
        h = sb("h", [P, S * T, P])
        hT = sb("hT", [P, S, SEQ_LEN])
        neg_max = sb("neg_max", [P, S, 1 + T])
        expq_T = sb("expq_T", [P, S, SEQ_LEN])
        expk = sb("expk", [P, S, T, P])
        sums = sb("sums", [P, S, 1 + T])
        inv = sb("inv", [P, S, 1 + T])
        expq = sb("expq", [P, S, T, P])
        MT = sb("MT", [P, S, P])
        G = sb("G", [P, S, P])
        F = sb("F", [P, S, P])
        outer = [add_norm_buffers(k, f"{name}_outer{b}", f"{name}_outer{b}", S * T, mem) for b in range(2)]
        inner = add_norm_buffers(k, f"{name}_inner", f"{name}_inner", S * T, mem)

        w_loaded = [k.sem(f"{name}_w_loaded{p}") for p in range(2)]
        y_ready = k.sem(f"{name}_y_ready")
        h_ready = k.sem(f"{name}_h_ready")
        bias_added = k.sem(f"{name}_bias_added")
        hT_in_psum = k.sem(f"{name}_hT_in_psum")
        hT_ready = k.sem(f"{name}_hT_ready")
        qk_in_psum = k.sem(f"{name}_qk_in_psum")
        max_ready = k.sem(f"{name}_max_ready")
        exp_ready = k.sem(f"{name}_exp_ready")
        inv_ready = k.sem(f"{name}_inv_ready")
        expq_in_psum = k.sem(f"{name}_expq_in_psum")
        expq_ready = k.sem(f"{name}_expq_ready")
        MT_in_psum = k.sem(f"{name}_MT_in_psum")
        MT_ready = k.sem(f"{name}_MT_ready")
        G_in_psum = k.sem(f"{name}_G_in_psum")
        G_ready = k.sem(f"{name}_G_ready")
        F_in_psum = k.sem(f"{name}_F_in_psum")
        F_ready = k.sem(f"{name}_F_ready")
        out_in_psum = k.sem(f"{name}_out_in_psum")

        LAYERS = k.dram["lin_w"].shape[0]

        def Wq(p): return w[:, p, 0:P]
        def Wk(p): return w[:, p, P:2 * P]
        def WvT(p): return w[:, p, 2 * P:3 * P]
        def Wout(p): return w[:, p, 3 * P:4 * P]

        def q_ps(s): return psum[:, s, 0:SEQ_LEN]
        def k_ps(s): return psum[:, s, SEQ_LEN:2 * SEQ_LEN]
        def F_ps(s): return psum[:, s, 0:P]
        def out_ps(s): return psum[:, s, SEQ_LEN:2 * SEQ_LEN]
        def tr_ps(s): return psum[:, 4 + s, 0:SEQ_LEN]
        def MT_ps(s): return psum[:, 4 + s, 2 * P:3 * P]
        def G_ps(s): return psum[:, 4 + s, 3 * P:4 * P]

        def run(eng, work, front):
            def layer(l, p, last):
                with eng.Fori(0, GROUPS - 2) as g:
                    work(eng, l, p, g, (l, g + 1), (l, g + 2))
                work(eng, l, p, GROUPS - 2, (l, GROUPS - 1), None if last else (l + 1, 0))
                work(eng, l, p, GROUPS - 1, None if last else (l + 1, 0), None if last else (l + 1, 1))
            front(eng, 0, 0)
            with eng.Fori(0, LAYERS // 2 - 1) as i:
                layer(2 * i, 0, False)
                layer(2 * i + 1, 1, False)
            layer(LAYERS - 2, 0, False)
            layer(LAYERS - 1, 1, True)

        def unit(l, g, s):
            return SEQS * l + S * g + s

        def pe_front(pe, l, g):
            for s in range(S):
                if s == 0:
                    pe.wait_ge(h_ready, GROUPS * l + g + 1)
                for j in range(T):
                    last = nc.tensor.transpose(tr_ps(s)[:, j * P:(j + 1) * P], h[:, T * s + j, :], k.ident[:])
                last.then_inc(hT_in_psum, 1)

        def pe_project(pe, l, p, g, s):
            if s == 0:
                pe.wait_ge(w_loaded[p], 8 * (l - p) + 16)
            pe.wait_ge(hT_ready, unit(l, g, s) + 1)
            pe.wait_ge(y_ready, unit(l, g, s) + 1 + SEQS - S)
            nc.tensor.matmul(q_ps(s), Wq(p), hT[:, s, :], start=True, stop=True)
            for j in range(T):
                last = nc.tensor.matmul(k_ps(s)[:, j * P:(j + 1) * P], hT[:, s, j * P:(j + 1) * P], Wk(p),
                                        start=True, stop=True)
            last.then_inc(qk_in_psum, 1)

        def pe_transpose_q(pe, l, g, s):
            pe.wait_ge(exp_ready, unit(l, g, s) + 1)
            for j in range(T):
                last = nc.tensor.transpose(tr_ps(s)[:, j * P:(j + 1) * P], expq_T[:, s, j * P:(j + 1) * P],
                                           k.ident[:])
            last.then_inc(expq_in_psum, 1)

        def pe_M(pe, l, g, s):
            pe.wait_ge(expq_ready, unit(l, g, s) + 1)
            for j in range(T):
                last = nc.tensor.matmul(MT_ps(s), expq[:, s, j, :], expk[:, s, j, :],
                                        start=(j == 0), stop=(j == T - 1))
            last.then_inc(MT_in_psum, 1)

        def pe_G(pe, l, p, g, s):
            pe.wait_ge(MT_ready, unit(l, g, s) + 1)
            nc.tensor.matmul(G_ps(s), MT[:, s, :], Wout(p), start=True, stop=True).then_inc(G_in_psum, 1)

        def pe_F(pe, l, p, g, s):
            pe.wait_ge(G_ready, unit(l, g, s) + 1)
            nc.tensor.matmul(F_ps(s), WvT(p), G[:, s, :], start=True, stop=True).then_inc(F_in_psum, 1)

        def pe_out(pe, l, g, s):
            pe.wait_ge(F_ready, unit(l, g, s) + 1)
            for j in range(T):
                last = nc.tensor.matmul(out_ps(s)[:, j * P:(j + 1) * P], hT[:, s, j * P:(j + 1) * P],
                                        F[:, s, :], start=True, stop=True)
            last.then_inc(out_in_psum, 1)

        def pe_work(pe, l, p, g, nxt, after):
            for step in range(S + F_LAG):
                if step < S:
                    pe_project(pe, l, p, g, step)
                if 0 <= step - T_LAG < S:
                    pe_transpose_q(pe, l, g, step - T_LAG)
                if 0 <= step - M_LAG < S:
                    pe_M(pe, l, g, step - M_LAG)
                if 0 <= step - G_LAG < S:
                    pe_G(pe, l, p, g, step - G_LAG)
                if 0 <= step - F_LAG < S:
                    pe_F(pe, l, p, g, step - F_LAG)
            if nxt is not None:
                pe_front(pe, *nxt)
            for s in range(S):
                pe_out(pe, l, g, s)

        def y_tile(g, j):
            return y[:, bass.ts(S * T * g + j, 1), :]

        def dve_statistics(dve, l, g):
            dve.wait_ge(y_ready, SEQS * l + S * g + S)
            norm_statistics(k, dve, inner, GROUPS * l + g, lambda j: y_tile(g, j))

        def dve_normalize(dve, l, g, s):
            t = GROUPS * l + g
            if s == 0:
                dve.wait_ge(inner.rstd_ready, t + 1)
            for j in range(T * s, T * (s + 1)):
                last = nc.vector.tensor_scalar(h[:, j:j + 1, :], y_tile(g, j), inner.mv[:, j, 0:1],
                                               inner.rstd[:, j:j + 1], ALU.subtract, ALU.mult)
            if s == S - 1:
                last.then_inc(h_ready, 1)

        def dve_front(dve, l, g):
            dve_statistics(dve, l, g)
            for s in range(S):
                dve_normalize(dve, l, g, s)
            dve_statistics(dve, l, g + 1)

        def dve_max(dve, l, g, s):
            dve.wait_ge(qk_in_psum, unit(l, g, s) + 1)
            nc.vector.tensor_reduce(neg_max[:, s, 0:1], q_ps(s), AX.X, ALU.max, negate=True)
            nc.vector.tensor_reduce(neg_max[:, s, 1:1 + T], k_ps(s).rearrange("p (j c) -> p j c", c=P),
                                    AX.X, ALU.max, negate=True).then_inc(max_ready, 1)

        def dve_scale_q(dve, l, g, s):
            dve.wait_ge(exp_ready, unit(l, g, s) + 1)
            nc.vector.reciprocal(inv[:, s, :], sums[:, s, :]).then_inc(inv_ready, 1)
            dve.wait_ge(expq_in_psum, unit(l, g, s) + 1)
            dve.wait_ge(inv_ready, unit(l, g, s) + 1)
            for j in range(T):
                last = nc.vector.tensor_scalar(expq[:, s, j, :], tr_ps(s)[:, j * P:(j + 1) * P],
                                               inv[:, s, 1 + j:2 + j], None, ALU.mult)
            last.then_inc(expq_ready, 1)

        def dve_scale_M(dve, l, g, s):
            dve.wait_ge(MT_in_psum, unit(l, g, s) + 1)
            nc.vector.tensor_scalar(MT[:, s, :], MT_ps(s), inv[:, s, 0:1], None, ALU.mult).then_inc(MT_ready, 1)

        def dve_work(dve, l, p, g, nxt, after):
            for step in range(S + M_LAG):
                if step < S:
                    dve_max(dve, l, g, step)
                    if nxt is not None:
                        dve_normalize(dve, *nxt, step)
                if 0 <= step - T_LAG < S:
                    dve_scale_q(dve, l, g, step - T_LAG)
                if 0 <= step - M_LAG < S:
                    dve_scale_M(dve, l, g, step - M_LAG)
            if after is not None:
                dve_statistics(dve, *after)
            for s in range(S):
                dve.wait_ge(out_in_psum, unit(l, g, s) + 1)
                dve.wait_ge(bias_added, unit(l, g, s) + 1)
                rows = y[:, bass.ts(S * g + s, T), :]
                nc.vector.tensor_tensor(rows, out_ps(s).rearrange("p (j f) -> p j f", f=DIM), rows,
                                        ALU.add).then_inc(y_ready, 1)

        def act_front(act, l, g, before=None):
            for s in range(S):
                settle(act, hT_in_psum, unit(l, g, s) + 1)
                if before is not None:
                    settle(act, out_in_psum, unit(*before, s) + 1)
                nc.scalar.activation(hT[:, s, :], tr_ps(s), ACT.Identity, bias=beta[:, bass.ts(l, 1)],
                                     scale=gamma[:, bass.ts(l, 1)]).then_inc(hT_ready, 1)

        def act_exp(act, l, g, s):
            act.wait_ge(max_ready, unit(l, g, s) + 1)
            nc.scalar.activation(expq_T[:, s, :], q_ps(s), ACT.Exp, bias=neg_max[:, s, 0:1],
                                 accum_out=sums[:, s, 0:1])
            for j in range(T):
                last = nc.scalar.activation(expk[:, s, j, :], k_ps(s)[:, j * P:(j + 1) * P], ACT.Exp,
                                            bias=neg_max[:, s, 1 + j:2 + j], accum_out=sums[:, s, 1 + j:2 + j])
            last.then_inc(exp_ready, 1)

        def act_G(act, l, g, s):
            act.wait_ge(G_in_psum, unit(l, g, s) + 1)
            nc.scalar.activation(G[:, s, :], G_ps(s), ACT.Copy).then_inc(G_ready, 1)

        def act_F(act, l, g, s):
            act.wait_ge(F_in_psum, unit(l, g, s) + 1)
            nc.scalar.activation(F[:, s, :], F_ps(s), ACT.Copy).then_inc(F_ready, 1)

        def act_work(act, l, p, g, nxt, after):
            for step in range(S + F_LAG):
                if step < S:
                    act_exp(act, l, g, step)
                if 0 <= step - G_LAG < S:
                    act_G(act, l, g, step - G_LAG)
                if 0 <= step - F_LAG < S:
                    act_F(act, l, g, step - F_LAG)
            if nxt is not None:
                act_front(act, *nxt, before=(l, g))

        def pool_bias(pool, l, g):
            settle(pool, h_ready, GROUPS * l + g + 1)
            for s in range(S):
                rows = y[:, bass.ts(S * g + s, T), :]
                nc.gpsimd.tensor_tensor(rows, rows, bias[:, bass.ts(l, 1), :].broadcast_to([P, T, DIM]),
                                        ALU.add).then_inc(bias_added, 1)

        def pool_front(pool, l, g):
            norm_rstd(k, pool, inner, GROUPS * l + g)
            pool_bias(pool, l, g)
            norm_rstd(k, pool, inner, GROUPS * l + g + 1)

        def pool_work(pool, l, p, g, nxt, after):
            if nxt is not None:
                pool_bias(pool, *nxt)
            if after is not None:
                norm_rstd(k, pool, inner, GROUPS * after[0] + after[1])

        with nc.Block() as block:
            @block.sync
            def _(sp):
                for p in range(2):
                    sp.dma_start(w[:, p, :], w_dram[p]).then_inc(w_loaded[p], 16)
                with sp.Fori(0, LAYERS // 2 - 1) as i:
                    for p in range(2):
                        sp.wait_ge(out_in_psum, SEQS * (2 * i + p + 1))
                        sp.dma_start(w[:, p, :], w_dram[bass.ts(2 * i + p + 2, 1)].rearrange("a p n -> p (a n)"))\
                          .then_inc(w_loaded[p], 16)

            @block.tensor
            def _(pe):
                run(pe, pe_work, pe_front)

            @block.vector
            def _(dve):
                with dve.Fori(0, GROUPS // 2) as i:
                    def x_tile(b):
                        return lambda j: x[:, bass.ts(S * T * (2 * i + b) + j, 1), :]
                    for b in range(2):
                        norm_statistics(k, dve, outer[b], i, x_tile(b))
                    for b in range(2):
                        norm_apply(k, dve, outer[b], i, lambda j: y_tile(2 * i + b, j), x_tile(b), (y_ready, S))
                run(dve, dve_work, dve_front)
                dve.wait_ge(y_ready, SEQS * (LAYERS + 1))
                with dve.Fori(0, GROUPS) as g:
                    rows = bass.ts(g, S * T)
                    nc.vector.tensor_tensor(x[:, rows, :], x[:, rows, :], y[:, rows, :], ALU.add)

            @block.scalar
            def _(act):
                run(act, act_work, act_front)

            @block.gpsimd
            def _(pool):
                with pool.Fori(0, GROUPS // 2) as i:
                    for b in range(2):
                        norm_rstd(k, pool, outer[b], i)
                run(pool, pool_work, pool_front)


SSM_INNER, SSM_STATE, SSM_RANK, SSM_TAPS = 256, 16, 16, 4


def state_space_stage(k, name="ssm"):
    nc, psum, x = k.nc, k.psum, k.x
    GT = 4
    GROUPS = TILES // GT
    W = GT * P
    GS = W // SEQ_LEN
    C = SSM_INNER // P
    N = SSM_STATE
    PAD = SSM_TAPS - 1
    DEPTH = 4
    GATE_AT, OUT_AT = 3, 4
    LAG = 2
    w_in, w_x, w_dt, w_out = k.const["ssm_win"], k.const["ssm_wx"], k.const["ssm_wdt"], k.const["ssm_wout"]
    taps, conv_b, b_dt, skip = k.const["ssm_taps"], k.const["ssm_convb"], k.const["ssm_bdt"], k.const["ssm_d"]
    a_log, pick = k.const["ssm_alog"], k.const["ssm_pick"]

    with ExitStack() as mem:
        def sb(n, shape, dtype=FP32):
            return k.sbuf(f"{name}_{n}", shape, dtype, mem)

        A = sb("A", [P, C, N])
        h = sb("h", [P, GT, P])
        hT = sb("hT", [P, W])
        padded = sb("padded", [P, C, GS, PAD + SEQ_LEN])
        conv = sb("conv", [P, C, GS, SEQ_LEN])
        u_act = sb("u_act", [P, 2, C, W])
        z_act = sb("z_act", [P, 2, C, W])
        bc = sb("bc", [P, 2, W], BF16)
        high = sb("high", [P, W], BF16)
        rest = sb("rest", [P, W])
        dt_low = sb("dt_low", [SSM_RANK, W])
        soft = sb("soft", [P, C, W])
        soft_pos = sb("soft_pos", [P, C, W])
        dt = sb("dt", [P, 2, C, W])
        dtu = sb("dtu", [P, 2, C, W])
        decay = sb("decay", [P, DEPTH, C * GS, SEQ_LEN])
        drive = sb("drive", [P, DEPTH, C, W])
        state = sb("state", [P, DEPTH, C, W])
        c_row = sb("c_row", [P, DEPTH, W])
        read = sb("read", [P, DEPTH, C, W])
        gated = sb("gated", [P, C, W])
        norm = add_norm_buffers(k, f"{name}_norm", f"{name}_norm", GT, mem)

        A_exp_ready = k.sem(f"{name}_A_exp_ready")
        A_ready = k.sem(f"{name}_A_ready")
        starts_zero = k.sem(f"{name}_starts_zero")
        padding_zero = k.sem(f"{name}_padding_zero")
        h_ready = k.sem(f"{name}_h_ready")
        hT_in_psum = k.sem(f"{name}_hT_in_psum")
        hT_ready = k.sem(f"{name}_hT_ready")
        xin_in_psum = k.sem(f"{name}_xin_in_psum")
        xin_ready = k.sem(f"{name}_xin_ready")
        z_in_psum = k.sem(f"{name}_z_in_psum")
        conv_steps = k.sem(f"{name}_conv_steps")
        u_ready = k.sem(f"{name}_u_ready")
        xdbl_in_psum = k.sem(f"{name}_xdbl_in_psum")
        split_steps = k.sem(f"{name}_split_steps")
        bc_ready = k.sem(f"{name}_bc_ready")
        low_ready = k.sem(f"{name}_low_ready")
        dt_in_psum = k.sem(f"{name}_dt_in_psum")
        soft_steps = k.sem(f"{name}_soft_steps")
        soft_ready = k.sem(f"{name}_soft_ready")
        dt_ready = k.sem(f"{name}_dt_ready")
        dtu_ready = k.sem(f"{name}_dtu_ready")
        rows_in_psum = k.sem(f"{name}_rows_in_psum")
        decay_ready = k.sem(f"{name}_decay_ready")
        c_ready = k.sem(f"{name}_c_ready")
        drive_ready = k.sem(f"{name}_drive_ready")
        state_ready = k.sem(f"{name}_state_ready")
        read_ready = k.sem(f"{name}_read_ready")
        y_added = k.sem(f"{name}_y_added")
        y_left = k.sem(f"{name}_y_left")
        gated_ready = k.sem(f"{name}_gated_ready")
        out_in_psum = k.sem(f"{name}_out_in_psum")
        x_done = k.sem(f"{name}_x_done")

        def b_bank(n): return psum[:, n % 2, :]
        def c_bank(n): return psum[:, 2 + n % 2, :]
        def y_bank(c): return psum[:, 4 + c, :]
        FA, FB = psum[:, 6, :], psum[:, 7, :]

        def run(eng, work, first, front, last):
            for n in range(N):
                front(eng, n, 0, 0)
            first(eng)
            work(eng, 0, 0, 1, None)
            work(eng, 1, 1, 2, 0)
            with eng.Fori(1, GROUPS // 2 - 1) as i:
                work(eng, 2 * i, 0, 2 * i + 1, 2 * i - 1)
                work(eng, 2 * i + 1, 1, 2 * i + 2, 2 * i)
            work(eng, GROUPS - 2, 0, GROUPS - 1, GROUPS - 3)
            work(eng, GROUPS - 1, 1, None, GROUPS - 2)
            last(eng)

        def ahead(t, u, nxt, m):
            return (t, u, m) if m < N else (nxt, 1 - u, m - N)

        def pe_front(pe, n, t, u, prev=None):
            if n == 3:
                pe.wait_ge(h_ready, t + 1)
                for j in range(GT):
                    last = nc.tensor.transpose(FB[:, j * P:(j + 1) * P], h[:, j, :], k.ident[:])
                last.then_inc(hT_in_psum, 1)
            if n == 4:
                pe.wait_ge(hT_ready, t + 1)
                if prev is not None:
                    pe.wait_ge(x_done, prev + 1)
                for c, bank in enumerate((FA, FB)):
                    last = nc.tensor.matmul(bank, w_in[:, c * P:(c + 1) * P], hT[:], start=True, stop=True)
                last.then_inc(xin_in_psum, 1)
            if n == 6:
                pe.wait_ge(xin_ready, t + 1)
                for c, bank in enumerate((FA, FB)):
                    last = nc.tensor.matmul(bank, w_in[:, (C + c) * P:(C + c + 1) * P], hT[:], start=True, stop=True)
                last.then_inc(z_in_psum, 1)
            if n == 9:
                pe.wait_ge(u_ready, t + 1)
                for c in range(C):
                    last = nc.tensor.matmul(FA, w_x[:, c, :], u_act[:, u, c, :], start=(c == 0), stop=(c == C - 1))
                last.then_inc(xdbl_in_psum, 1)
            if n == 10:
                pe.wait_ge(bc_ready, t + 1)
                pe.wait_ge(low_ready, t + 1)
                for c, bank in enumerate((FA, FB)):
                    last = nc.tensor.matmul(bank, w_dt[:, c * P:(c + 1) * P], dt_low[:], start=True, stop=True)
                last.then_inc(dt_in_psum, 1)

        def rows(t, u, n):
            nc.tensor.matmul(b_bank(n), pick[:, n, :], bc[:, u, :], start=True, stop=True)
            nc.tensor.matmul(c_bank(n), pick[:, N + n, :], bc[:, u, :], start=True, stop=True).then_inc(rows_in_psum, 1)

        def pe_rows_ahead(pe, t, u, nxt, n):
            g, v, m = ahead(t, u, nxt, n + 2)
            if g is not None:
                pe.wait_ge(drive_ready, N * t + n + 1)
                pe.wait_ge(c_ready, N * t + n + 1)
                if m == 0:
                    pe.wait_ge(bc_ready, g + 1)
                rows(g, v, m)

        def accumulate(pe, t, n, before):
            pe.wait_ge(read_ready, DEPTH + N * t + n + 1)
            if n == 0 and before is not None:
                pe.wait_ge(y_left, before + 1)
            for c in range(C):
                last = nc.tensor.matmul(y_bank(c), k.ident[:], read[:, n % DEPTH, c, :],
                                        start=(n == 0), stop=(n == N - 1))
            last.then_inc(y_added, 1)

        def pe_out(pe, t):
            pe.wait_ge(gated_ready, t + 1)
            for j in range(GT):
                for c in range(C):
                    last = nc.tensor.matmul(FA[:, j * P:(j + 1) * P], gated[:, c, j * P:(j + 1) * P],
                                            w_out[:, c, :], start=(c == 0), stop=(c == C - 1))
            last.then_inc(out_in_psum, 1)

        def pe_first(pe):
            pe.wait_ge(bc_ready, 1)
            rows(0, 0, 0)
            rows(0, 0, 1)

        def pe_work(pe, t, u, nxt, prev):
            for n in range(N):
                pe_rows_ahead(pe, t, u, nxt, n)
                if n >= LAG:
                    accumulate(pe, t, n - LAG, prev)
                elif prev is not None:
                    accumulate(pe, prev, N + n - LAG, None)
                if n == OUT_AT and prev is not None:
                    pe_out(pe, prev)
                if nxt is not None:
                    pe_front(pe, n, nxt, 1 - u, prev)

        def pe_last(pe):
            for n in range(N - LAG, N):
                accumulate(pe, GROUPS - 1, n, None)
            pe_out(pe, GROUPS - 1)

        def dve_front(dve, n, t, u):
            def tile(j): return x[:, bass.ts(GT * t + j, 1), :]
            if n == 2:
                norm_statistics(k, dve, norm, t, tile)
            if n == 3:
                norm_apply(k, dve, norm, t, lambda j: h[:, j:j + 1, :], tile, (h_ready, 1))
            if 5 <= n < 5 + SSM_TAPS:
                tap = n - 5
                if tap == 0:
                    dve.wait_ge(xin_ready, t + 1)
                for c in range(C):
                    src = padded[:, c, :, tap:tap + SEQ_LEN]
                    if tap == 0:
                        nc.vector.tensor_scalar(conv[:, c], src, taps[:, c, 0:1], conv_b[:, c:c + 1],
                                                ALU.mult, ALU.add).then_inc(conv_steps, 1)
                    else:
                        dve.wait_ge(conv_steps, C * SSM_TAPS * t + C * (tap - 1) + c + 1)
                        nc.vector.scalar_tensor_tensor(conv[:, c], src, taps[:, c, tap:tap + 1], conv[:, c],
                                                       ALU.mult, ALU.add).then_inc(conv_steps, 1)
            if n == 10:
                dve.wait_ge(xdbl_in_psum, t + 1)
                nc.vector.tensor_copy(high[64:P, :], FA[64:P, :]).then_inc(split_steps, 1)
                dve.wait_ge(split_steps, 3 * t + 1)
                nc.vector.tensor_tensor(rest[64:P, :], FA[64:P, :], high[64:P, :], ALU.subtract).then_inc(split_steps, 1)
                dve.wait_ge(split_steps, 3 * t + 2)
                nc.vector.tensor_copy(high[96:P, :], rest[96:P, :]).then_inc(split_steps, 1)
                nc.vector.tensor_copy(bc[64:96, u, :], rest[64:96, :])
                dve.wait_ge(split_steps, 3 * t + 3)
                nc.vector.tensor_tensor(bc[96:P, u, :], rest[96:P, :], high[96:P, :], ALU.subtract).then_inc(bc_ready, 1)
            if n == 13:
                dve.wait_ge(soft_ready, t + 1)
                nc.vector.tensor_tensor(dt[:, u], soft[:], soft_pos[:], ALU.add).then_inc(dt_ready, 1)
                dve.wait_ge(dt_ready, t + 1)
                nc.vector.tensor_tensor(dtu[:, u], dt[:, u], u_act[:, u], ALU.mult).then_inc(dtu_ready, 1)

        def dve_gate(dve, t, u):
            dve.wait_ge(y_added, DEPTH + N * (t + 1))
            for c in range(C):
                last = nc.vector.scalar_tensor_tensor(gated[:, c, :], u_act[:, u, c, :], skip[:, c:c + 1],
                                                      y_bank(c), ALU.mult, ALU.add)
            last.then_inc(y_left, 1)

        def pool_gate(pool, t, u):
            settle(pool, y_left, t + 1)
            nc.gpsimd.tensor_tensor(gated[:], gated[:], z_act[:, u], ALU.mult).then_inc(gated_ready, 1)

        def dve_out(dve, t):
            dve.wait_ge(out_in_psum, t + 1)
            group = x[:, bass.ts(t, GT), :]
            nc.vector.tensor_tensor(group, FA.rearrange("p (j f) -> p j f", f=DIM), group, ALU.add).then_inc(x_done, 1)

        def dve_drive(dve, t, u, n):
            if n == 0:
                dve.wait_ge(dtu_ready, t + 1)
            dve.wait_ge(rows_in_psum, N * t + n + 1)
            dve.wait_ge(state_ready, N * t + n + 1)
            nc.vector.tensor_tensor(drive[:, n % DEPTH], dtu[:, u],
                                    psum[:, n % 2:n % 2 + 1, :].broadcast_to([P, C, W]), ALU.mult).then_inc(drive_ready, 1)

        def dve_scan(dve, t, n):
            idx = N * t + n
            dve.wait_ge(drive_ready, idx + 1)
            dve.wait_ge(decay_ready, idx + 1)
            dve.wait_ge(read_ready, idx + 1)
            nc.vector.tensor_tensor_scan(state[:, n % DEPTH].rearrange("p c w -> p (c w)"),
                                         decay[:, n % DEPTH].rearrange("p s l -> p (s l)"),
                                         drive[:, n % DEPTH].rearrange("p c w -> p (c w)"), 0.0, ALU.mult, ALU.add)\
              .then_inc(state_ready, 1)

        def dve_first(dve):
            dve_drive(dve, 0, 0, 0)

        def dve_work(dve, t, u, nxt, prev):
            for n in range(N):
                g, v, m = ahead(t, u, nxt, n + 1)
                if g is not None:
                    dve_drive(dve, g, v, m)
                dve_scan(dve, t, n)
                if prev is not None:
                    if n == 2:
                        dve_gate(dve, prev, 1 - u)
                    if n == OUT_AT + 1:
                        dve_out(dve, prev)
                if nxt is not None:
                    dve_front(dve, n, nxt, 1 - u)

        def dve_last(dve):
            dve_gate(dve, GROUPS - 1, 1)
            dve_out(dve, GROUPS - 1)

        def act_front(act, n, t, u):
            if n == 4:
                act.wait_ge(hT_in_psum, t + 1)
                nc.scalar.activation(hT[:], FB, ACT.Copy).then_inc(hT_ready, 1)
                act.wait_ge(xin_in_psum, t + 1)
                for c, bank in enumerate((FA, FB)):
                    last = nc.scalar.activation(padded[:, c, :, PAD:PAD + SEQ_LEN],
                                                bank.rearrange("p (q l) -> p q l", l=SEQ_LEN), ACT.Copy)
                last.then_inc(xin_ready, 1)
            if n == 9:
                act.wait_ge(z_in_psum, t + 1)
                for c, bank in enumerate((FA, FB)):
                    nc.scalar.activation(z_act[:, u, c, :], bank, ACT.Silu)
                act.wait_ge(conv_steps, C * SSM_TAPS * (t + 1))
                nc.scalar.activation(u_act[:, u], conv[:].rearrange("p c q l -> p c (q l)"), ACT.Silu).then_inc(u_ready, 1)
            if n == 10:
                act.wait_ge(xdbl_in_psum, t + 1)
                nc.scalar.activation(dt_low[:], FA[0:SSM_RANK, :], ACT.Copy)
                nc.scalar.activation(bc[0:64, u, :], FA[0:64, :], ACT.Copy).then_inc(low_ready, 1)
            if n == 12:
                act.wait_ge(dt_in_psum, t + 1)
                for c, bank in enumerate((FA, FB)):
                    nc.scalar.activation(soft_pos[:, c, :], bank, ACT.Relu, bias=b_dt[:, c:c + 1])
                    last = nc.scalar.activation(soft[:, c, :], bank, ACT.Abs, bias=b_dt[:, c:c + 1])
                last.then_inc(soft_steps, 1)
                act.wait_ge(soft_steps, 2 * t + 1)
                nc.scalar.activation(soft[:], soft[:], ACT.Exp, scale=-1.0).then_inc(soft_steps, 1)
                act.wait_ge(soft_steps, 2 * t + 2)
                nc.scalar.activation(soft[:], soft[:], ACT.Ln, bias=1.0).then_inc(soft_ready, 1)

        def act_decay(act, t, u, n):
            if n == 0:
                act.wait_ge(dt_ready, t + 1)
            act.wait_ge(state_ready, N * t + n + 1)
            for c in range(C):
                last = nc.scalar.activation(decay[:, n % DEPTH, GS * c:GS * (c + 1), 1:SEQ_LEN],
                                            dt[:, u, c, :].rearrange("p (q l) -> p q l", l=SEQ_LEN)[:, :, 1:SEQ_LEN],
                                            ACT.Exp, scale=A[:, c, n:n + 1])
            last.then_inc(decay_ready, 1)

        def act_first(act):
            act.wait_ge(starts_zero, 1)
            act_decay(act, 0, 0, 0)

        def act_work(act, t, u, nxt, prev):
            for n in range(N):
                act.wait_ge(rows_in_psum, N * t + n + 1)
                act.wait_ge(read_ready, N * t + n + 1)
                nc.scalar.activation(c_row[:, n % DEPTH, :], c_bank(n), ACT.Copy).then_inc(c_ready, 1)
                g, v, m = ahead(t, u, nxt, n + 1)
                if g is not None:
                    act_decay(act, g, v, m)
                if nxt is not None:
                    act_front(act, n, nxt, 1 - u)

        def pool_front(pool, n, t, u):
            if n == 2:
                norm_rstd(k, pool, norm, t)

        def pool_work(pool, t, u, nxt, prev):
            for n in range(N):
                s = n % DEPTH
                pool.wait_ge(state_ready, DEPTH + N * t + n + 1)
                pool.wait_ge(c_ready, N * t + n + 1)
                settle(pool, y_added, N * t + n + 1)
                nc.gpsimd.tensor_tensor(read[:, s], state[:, s],
                                        c_row[:, s:s + 1, :].broadcast_to([P, C, W]), ALU.mult).then_inc(read_ready, 1)
                if n == GATE_AT and prev is not None:
                    pool_gate(pool, prev, 1 - u)
                if nxt is not None:
                    pool_front(pool, n, nxt, 1 - u)

        def pool_last(pool):
            pool_gate(pool, GROUPS - 1, 1)

        def nothing(eng, *step):
            pass

        with nc.Block() as block:
            @block.tensor
            def _(pe):
                pe.sem_inc(y_added, DEPTH)
                run(pe, pe_work, pe_first, pe_front, pe_last)

            @block.vector
            def _(dve):
                dve.sem_inc(state_ready, DEPTH)
                nc.vector.memset(padded[:], 0.0).then_inc(padding_zero, 1)
                nc.vector.memset(decay[:, :, :, 0:1], 0.0).then_inc(starts_zero, 1)
                dve.wait_ge(A_exp_ready, 1)
                nc.vector.tensor_scalar(A[:], A[:], -1.0, None, ALU.mult).then_inc(A_ready, 1)
                run(dve, dve_work, dve_first, dve_front, dve_last)

            @block.scalar
            def _(act):
                nc.scalar.activation(A[:], a_log[:], ACT.Exp).then_inc(A_exp_ready, 1)
                act.wait_ge(A_ready, 1)
                act.wait_ge(padding_zero, 1)
                run(act, act_work, act_first, act_front, nothing)

            @block.gpsimd
            def _(pool):
                pool.sem_inc(read_ready, DEPTH)
                run(pool, pool_work, nothing, pool_front, pool_last)


HEADS, HEAD_DIM, WINDOW = 8, 64, 64
INNER = HEADS * HEAD_DIM
HID_CHUNKS = 3
MASKED = -1e30


def local_attention_stage(k, name):
    nc, psum, x, y = k.nc, k.psum, k.x, k.y
    T = SEQ_LEN // P
    LAYERS = k.dram["loc_wa"].shape[0]
    HP = HEADS // 2
    HALF = HP // 2
    STEPS = 4
    QK = 2 * INNER
    GT = 4
    FGROUPS = TILES // GT
    GS = GT // T
    cos, sin, scale, scale_swapped = (k.const[f"loc_{n}"] for n in ("cos", "sin", "scale", "scale_swapped"))
    mask, ident_bf = k.const["loc_mask"], k.const["loc_ident"]
    ln_g, ln_b, b1, b2 = (k.const[f"loc_{n}"] for n in ("lng", "lnb", "b1", "b2"))

    with ExitStack() as mem:
        def sb(n, shape, dtype=FP32):
            return k.sbuf(f"{name}_{n}", shape, dtype, mem)

        rows_a = sb("rows_a", [P, 2, T, DIM])
        rows_f = sb("rows_f", [P, 2, GT, DIM])
        wa = sb("wa", [P, 3 * INNER + HP * DIM])
        w_qkv, w_o = wa[:, 0:3 * INNER], wa[:, 3 * INNER:].rearrange("p (c n) -> p c n", n=DIM)
        wf = sb("wf", [P, 2 * HID_CHUNKS * P + HID_CHUNKS * DIM])
        w_1 = wf[:, 0:2 * HID_CHUNKS * P].rearrange("p (c n) -> p c n", n=P)
        w_2 = wf[:, 2 * HID_CHUNKS * P:].rearrange("p (c n) -> p c n", n=DIM)
        rot_cos = sb("rot_cos", [P, LAYERS * T, 2, HEAD_DIM])
        rot_sin = sb("rot_sin", [P, LAYERS * T, 2, HEAD_DIM])
        hT = sb("hT", [P, SEQ_LEN])
        raw = sb("raw", [P, T, QK])
        square = sb("square", [P, T, QK])
        ss = sb("ss", [P, T, 2 * HEADS])
        ss_guard = sb("ss_guard", [P, T, 2 * HEADS])
        inv_norm = sb("inv_norm", [P, T, 2 * HEADS])
        by_sin = sb("by_sin", [P, T, QK])
        qk = sb("qk", [P, T, QK])
        qT = sb("qT", [P, 2, HP, SEQ_LEN])
        kT = sb("kT", [P, 2, HP, SEQ_LEN])
        v = sb("v", [P, 2, T, INNER])
        v_mid = sb("v_mid", [P, 2, INNER])
        neg_top = sb("neg_top", [P, STEPS, STEPS])
        total = sb("total", [P, STEPS, STEPS])
        inv_total = sb("inv_total", [P, STEPS, STEPS])
        prob = sb("prob", [P, STEPS, 512])
        prob_T = sb("prob_T", [P, 2, 512])
        oT = sb("oT", [P, HP, SEQ_LEN])
        fh = sb("fh", [P, GT, P])
        fhT = sb("fhT", [P, 2, GT * P])
        gelu = sb("gelu", [P, HID_CHUNKS, GT * P])
        hid = sb("hid", [P, HID_CHUNKS, GT * P])
        outer = [add_norm_buffers(k, f"{name}_outer{b}", f"loc_outer{b}", 2 * GT, mem) for b in range(2)]
        inner = add_norm_buffers(k, f"{name}_inner", "loc_inner", GT, mem)

        def sem(n):
            return k.sem(f"loc_{n}")
        tables_steps, wa_loaded, wf_loaded, edge_zero = sem("tables_steps"), sem("wa_loaded"), sem("wf_loaded"), sem("edge_zero")
        y_for_attn, y_for_ffn = sem("y_for_attn"), sem("y_for_ffn")
        sh_for_attn = [sem(f"sh_for_attn{u}") for u in range(2)]
        sh_for_ffn = [sem(f"sh_for_ffn{u}") for u in range(2)]
        hT_in_psum, hT_ready = sem("hT_in_psum"), sem("hT_ready")
        qk_in_psum, v_in_psum = sem("qk_in_psum"), sem("v_in_psum")
        raw_ready, square_ready, v_ready = sem("raw_ready"), sem("square_ready"), sem("v_ready")
        ss_ready, guard_ready, inv_norm_ready = sem("ss_ready"), sem("guard_ready"), sem("inv_norm_ready")
        by_cos_ready, by_sin_ready, sum_ready, rot_ready = sem("by_cos_ready"), sem("by_sin_ready"), sem("sum_ready"), sem("rot_ready")
        qkT_in_psum, qkT_ready = sem("qkT_in_psum"), sem("qkT_ready")
        scores_in_psum, top_ready = sem("scores_in_psum"), sem("top_ready")
        exp_ready, inv_total_ready = sem("exp_ready"), sem("inv_total_ready")
        prob_ready, prob_T_in_psum, prob_T_ready = sem("prob_ready"), sem("prob_T_in_psum"), sem("prob_T_ready")
        oT_in_psum, oT_ready, attn_in_psum = sem("oT_in_psum"), sem("oT_ready"), sem("attn_in_psum")
        fh_ready, fhT_in_psum, fhT_ready = sem("fh_ready"), sem("fhT_in_psum"), sem("fhT_ready")
        up_done, gelu_ready, hid_ready = sem("up_done"), sem("gelu_ready"), sem("hid_ready")
        ffn_in_psum, bias_added = sem("ffn_in_psum"), sem("bias_added")

        QK_BANKS = psum[:, 0:2, :]
        V_BANK = psum[:, 2, :]
        HT = psum[:, 3, 0:SEQ_LEN]
        ATTN = psum[:, 3, SEQ_LEN:2 * SEQ_LEN]
        PT_BANK = psum[:, 6, :]
        OT_BANK = psum[:, 7, :]

        def score_bank(e):
            return psum[:, 4 + e, :]

        def run_attention(eng, l, work, first):
            first(eng, l)
            with eng.Fori(0, SEQS // 2 - 1) as i:
                work(eng, l, 2 * i, 0, 2 * i + 1, 2 * i + 2, i + 1)
                work(eng, l, 2 * i + 1, 1, 2 * i + 2, 2 * i + 3, i + 1)
            work(eng, l, SEQS - 2, 0, SEQS - 1, None, None)
            work(eng, l, SEQS - 1, 1, None, None, None)

        def seq(l, t):
            return SEQS * l + t

        START = 1
        FREE = 2

        def transpose_rows(pe, l, t, u, pair):
            pe.wait_ge(sh_for_attn[u], 48 * (SEQS // 2 * l + pair + 1))
            for j in range(T):
                last = nc.tensor.transpose(HT[:, j * P:(j + 1) * P], rows_a[:, u, j, :], k.ident[:])
            last.then_inc(hT_in_psum, 1)

        def project_qk(pe, l, t, j):
            i = T * seq(l, t) + j
            if j == 0:
                pe.wait_ge(hT_ready, seq(l, t) + 1)
                pe.wait_ge(qkT_ready, START + 2 * i)
            else:
                pe.wait_ge(raw_ready, START + i)
            for b in range(2):
                last = nc.tensor.matmul(QK_BANKS[:, b, :], hT[:, j * P:(j + 1) * P],
                                        w_qkv[:, b * INNER:(b + 1) * INNER], start=True, stop=True)
            last.then_inc(qk_in_psum, 1)

        def project_v(pe, l, t, j):
            pe.wait_ge(v_ready, START + T * seq(l, t) + j)
            nc.tensor.matmul(V_BANK, hT[:, j * P:(j + 1) * P], w_qkv[:, QK:QK + INNER], start=True, stop=True)\
              .then_inc(v_in_psum, 1)

        def transpose_qk(pe, l, t, j, b):
            i = T * seq(l, t) + j
            pe.wait_ge(rot_ready, 2 * i + b + 1)
            if j == 0:
                pe.wait_ge(raw_ready, START + i + T)
            else:
                pe.wait_ge(qkT_ready, START + 2 * i + b - 1)
            for c in range(HP):
                last = nc.tensor.transpose(QK_BANKS[:, b, c * P:(c + 1) * P],
                                           qk[:, j, b * INNER + c * P:b * INNER + (c + 1) * P], k.ident[:])
            last.then_inc(qkT_in_psum, 1)

        def scores(pe, l, t, u, half):
            if half == 0:
                pe.wait_ge(qkT_ready, START + 2 * T * (seq(l, t) + 1))
            else:
                pe.wait_ge(exp_ready, STEPS * seq(l, t) + 2)
            for e in range(2):
                last = nc.tensor.matmul(score_bank(e), ident_bf[:], mask[:], start=True, stop=False,
                                        skip_group_check=True)
            for c in range(HALF):
                for w in range(SEQ_LEN // WINDOW):
                    rows = slice(WINDOW * (w % 2), WINDOW * (w % 2) + WINDOW)
                    col = (c * 2 + w // 2) * P
                    if w == 2:
                        parts = [(col, w * WINDOW, WINDOW), (col + WINDOW, (w - 1) * WINDOW, WINDOW)]
                    else:
                        parts = [(col, (w // 2) * P, P)]
                    for at, key, n in parts:
                        for e in range(2):
                            d = slice(HEAD_DIM * e, HEAD_DIM * (e + 1))
                            last = nc.tensor.matmul(score_bank(e)[rows, at:at + n],
                                                    qT[d, u, HALF * half + c, w * WINDOW:(w + 1) * WINDOW],
                                                    kT[d, u, HALF * half + c, key:key + n],
                                                    start=False, stop=True, skip_group_check=True)
            last.then_inc(scores_in_psum, 1)

        def transpose_prob(pe, l, t, a):
            pe.wait_ge(prob_ready, STEPS * seq(l, t) + a + 1)
            for i in range(4):
                last = nc.tensor.transpose(PT_BANK[:, i * P:(i + 1) * P], prob[:, a, i * P:(i + 1) * P], k.ident[:])
            last.then_inc(prob_T_in_psum, 1)

        def weighted(pe, l, t, u, a):
            half, e = a // 2, a % 2
            if a == 0:
                pe.wait_ge(v_ready, START + T * (seq(l, t) + 1))
            if e == 0:
                pe.wait_ge(oT_ready, START + 2 * seq(l, t) + half)
            pe.wait_ge(prob_T_ready, STEPS * seq(l, t) + a + 1)
            for c in range(HALF):
                head = 2 * (HALF * half + c) + e
                d = slice(HEAD_DIM * head, HEAD_DIM * (head + 1))
                out = OT_BANK[HEAD_DIM * e:HEAD_DIM * (e + 1), c * SEQ_LEN:(c + 1) * SEQ_LEN]
                p0 = prob_T[:, a % 2, 2 * c * P:(2 * c + 1) * P]
                p1 = prob_T[:, a % 2, (2 * c + 1) * P:(2 * c + 2) * P]
                nc.tensor.matmul(out[:, 0:P], v[:, u, 0, d], p0, start=True, stop=True)
                nc.tensor.matmul(out[:, P:P + WINDOW], v_mid[:, u, d], p1[:, 0:WINDOW], start=True, stop=True)
                last = nc.tensor.matmul(out[:, P + WINDOW:2 * P], v[:, u, 1, d], p1[:, WINDOW:P], start=True, stop=True)
            last.then_inc(oT_in_psum, 1)

        def attention_out(pe, l, t, after):
            pe.wait_ge(oT_ready, START + 2 * seq(l, t) + 2)
            if after is not None:
                pe.wait_ge(hT_ready, seq(l, after) + 1)
            for j in range(T):
                for c in range(HP):
                    last = nc.tensor.matmul(ATTN[:, j * P:(j + 1) * P], oT[:, c, j * P:(j + 1) * P], w_o[:, c, :],
                                            start=(c == 0), stop=(c == HP - 1))
            last.then_inc(attn_in_psum, 1)

        def pe_first(pe, l):
            transpose_rows(pe, l, 0, 0, 0)
            for j in range(T):
                project_qk(pe, l, 0, j)
                project_v(pe, l, 0, j)
            transpose_rows(pe, l, 1, 1, 0)
            pe.wait_ge(y_for_attn, SEQS * (l + 1))
            for j in range(T):
                for b in range(2):
                    transpose_qk(pe, l, 0, j, b)

        def pe_attention(pe, l, t, u, nxt, after, pair):
            scores(pe, l, t, u, 0)
            if nxt is not None:
                project_qk(pe, l, nxt, 0)
                project_qk(pe, l, nxt, 1)
                project_v(pe, l, nxt, 0)
            scores(pe, l, t, u, 1)
            transpose_prob(pe, l, t, 0)
            if nxt is not None:
                project_v(pe, l, nxt, 1)
            weighted(pe, l, t, u, 0)
            transpose_prob(pe, l, t, 1)
            if after is not None:
                pe.wait_ge(y_for_ffn, START + seq(l, t))
                transpose_rows(pe, l, after, u, pair)
            weighted(pe, l, t, u, 1)
            transpose_prob(pe, l, t, 2)
            if nxt is not None:
                transpose_qk(pe, l, nxt, 0, 0)
                transpose_qk(pe, l, nxt, 0, 1)
            else:
                pe_ffn_front(pe, l, 0, psum[:, 0, :])
            weighted(pe, l, t, u, 2)
            transpose_prob(pe, l, t, 3)
            if nxt is not None:
                transpose_qk(pe, l, nxt, 1, 0)
            weighted(pe, l, t, u, 3)
            if nxt is not None:
                transpose_qk(pe, l, nxt, 1, 1)
            attention_out(pe, l, t, after)

        def heads(ap):
            return ap.rearrange("p (s h d) -> p s h d", s=2, d=HEAD_DIM)

        def by_head(ap):
            return ap.rearrange("p (h d) -> p h d", d=HEAD_DIM)

        def table(tab, l, j, cols=slice(0, HEAD_DIM)):
            one = tab[:, bass.ts(T * l + j, 1), :, cols].rearrange("p a s d -> p (a s) d")
            return one.unsqueeze(2).broadcast_to([P, 2, HEADS, cols.stop - cols.start])

        def head_squares(dve, l, t, j):
            i = T * seq(l, t) + j
            dve.wait_ge(square_ready, i + 1)
            nc.vector.tensor_reduce(ss[:, j], by_head(square[:, j]), AX.X, ALU.add).then_inc(ss_ready, 1)
            dve.wait_ge(ss_ready, i + 1)
            nc.vector.tensor_scalar(ss_guard[:, j], ss[:, j], 1e-24, None, ALU.max).then_inc(guard_ready, 1)

        def times_cos(dve, l, t, j):
            dve.wait_ge(raw_ready, START + T * seq(l, t) + j + 1)
            nc.vector.tensor_tensor(heads(qk[:, j]), heads(raw[:, j]), table(rot_cos, l, j), ALU.mult)\
              .then_inc(by_cos_ready, 1)

        def rotated(dve, l, t, j, b):
            i = T * seq(l, t) + j
            dve.wait_ge(by_cos_ready, i + 1)
            dve.wait_ge(by_sin_ready, i + 1)
            half = slice(b * INNER, (b + 1) * INNER)
            nc.vector.tensor_tensor(qk[:, j, half], qk[:, j, half], by_sin[:, j, half], ALU.add).then_inc(sum_ready, 1)

        def unit_norm(dve, l, t, j, b):
            i = T * seq(l, t) + j
            dve.wait_ge(sum_ready, 2 * i + b + 1)
            dve.wait_ge(inv_norm_ready, i + 1)
            half = by_head(qk[:, j])[:, b * HEADS:(b + 1) * HEADS]
            nc.vector.tensor_tensor(half, half, inv_norm[:, j, b * HEADS:(b + 1) * HEADS].unsqueeze(2)
                                    .broadcast_to([P, HEADS, HEAD_DIM]), ALU.mult).then_inc(rot_ready, 1)

        def by_row(ap):
            return ap.rearrange("p (g c) -> p g c", c=P)

        def row_tops(dve, l, t, a):
            dve.wait_ge(scores_in_psum, 2 * seq(l, t) + a // 2 + 1)
            nc.vector.tensor_reduce(neg_top[:, a, :], by_row(score_bank(a % 2)), AX.X, ALU.max, negate=True)\
              .then_inc(top_ready, 1)

        def divide(dve, l, t, a):
            idx = STEPS * seq(l, t) + a
            dve.wait_ge(exp_ready, idx + 1)
            nc.vector.reciprocal(inv_total[:, a, :], total[:, a, :]).then_inc(inv_total_ready, 1)
            dve.wait_ge(inv_total_ready, idx + 1)
            nc.vector.tensor_tensor(by_row(prob[:, a]), by_row(prob[:, a]),
                                    inv_total[:, a, :].unsqueeze(2).broadcast_to([P, STEPS, P]),
                                    ALU.mult).then_inc(prob_ready, 1)

        def dve_first(dve, l):
            for j in range(T):
                times_cos(dve, l, 0, j)
                head_squares(dve, l, 0, j)
            for j in range(T):
                rotated(dve, l, 0, j, 0)
                rotated(dve, l, 0, j, 1)
                unit_norm(dve, l, 0, j, 0)
                unit_norm(dve, l, 0, j, 1)

        def dve_attention(dve, l, t, u, nxt, after, pair):
            row_tops(dve, l, t, 0)
            row_tops(dve, l, t, 1)
            divide(dve, l, t, 0)
            divide(dve, l, t, 1)
            if nxt is not None:
                times_cos(dve, l, nxt, 0)
                head_squares(dve, l, nxt, 0)
                times_cos(dve, l, nxt, 1)
            row_tops(dve, l, t, 2)
            if nxt is not None:
                head_squares(dve, l, nxt, 1)
                rotated(dve, l, nxt, 0, 0)
                rotated(dve, l, nxt, 0, 1)
            else:
                dve_ffn_statistics(dve, l, 0, 0, 0)
                dve_ffn_normalize(dve, l, 0, 0)
            row_tops(dve, l, t, 3)
            divide(dve, l, t, 2)
            if nxt is not None:
                unit_norm(dve, l, nxt, 0, 0)
                unit_norm(dve, l, nxt, 0, 1)
            divide(dve, l, t, 3)
            if nxt is not None:
                rotated(dve, l, nxt, 1, 0)
                unit_norm(dve, l, nxt, 1, 0)
                rotated(dve, l, nxt, 1, 1)
                unit_norm(dve, l, nxt, 1, 1)
            dve.wait_ge(attn_in_psum, START + seq(l, t) + 1)
            rows = y[:, bass.ts(t, T), :]
            nc.vector.tensor_tensor(rows, ATTN.rearrange("p (j f) -> p j f", f=DIM), rows,
                                    ALU.add).then_inc(y_for_ffn, 1)

        def copy_hT(act, l, t):
            act.wait_ge(hT_in_psum, seq(l, t) + 1 + FREE)
            nc.scalar.activation(hT[:], HT, ACT.Copy).then_inc(hT_ready, 1)

        def copy_qk(act, l, t, j):
            i = T * seq(l, t) + j
            act.wait_ge(qk_in_psum, i + 1)
            nc.scalar.activation(raw[:, j], QK_BANKS.rearrange("p b n -> p (b n)"), ACT.Copy).then_inc(raw_ready, 1)

        def square_qk(act, l, t, j):
            act.wait_ge(raw_ready, START + T * seq(l, t) + j + 1)
            nc.scalar.activation(square[:, j], raw[:, j], ACT.Square).then_inc(square_ready, 1)

        def copy_v(act, l, t, u, j):
            act.wait_ge(v_in_psum, T * seq(l, t) + j + 1)
            half = slice(64, P) if j == 0 else slice(0, 64)
            nc.scalar.activation(v_mid[half, u, :], V_BANK[half, :], ACT.Copy)
            nc.scalar.activation(v[:, u, j, :], V_BANK, ACT.Copy).then_inc(v_ready, 1)

        def copy_qkT(act, l, t, u, j, b):
            act.wait_ge(qkT_in_psum, 2 * (T * seq(l, t) + j) + b + 1)
            dst = (qT, kT)[b]
            nc.scalar.activation(dst[:, u, :, j * P:(j + 1) * P],
                                 QK_BANKS[:, b, :].rearrange("p (c n) -> p c n", n=P), ACT.Copy).then_inc(qkT_ready, 1)

        def exponential(act, l, t, a):
            act.wait_ge(top_ready, STEPS * seq(l, t) + a + 1)
            for g in range(STEPS):
                cols = slice(g * P, (g + 1) * P)
                last = nc.scalar.activation(prob[:, a, cols], score_bank(a % 2)[:, cols], ACT.Exp,
                                            bias=neg_top[:, a, g:g + 1], accum_out=total[:, a, g:g + 1])
            last.then_inc(exp_ready, 1)

        def copy_prob_T(act, l, t, a):
            act.wait_ge(prob_T_in_psum, STEPS * seq(l, t) + a + 1)
            nc.scalar.activation(prob_T[:, a % 2, :], PT_BANK, ACT.Copy).then_inc(prob_T_ready, 1)

        def copy_oT(act, l, t, half):
            act.wait_ge(oT_in_psum, STEPS * seq(l, t) + 2 * half + 2)
            nc.scalar.activation(oT[:, HALF * half:HALF * (half + 1), :],
                                 OT_BANK.rearrange("p (c n) -> p c n", n=SEQ_LEN), ACT.Copy).then_inc(oT_ready, 1)

        def act_first(act, l):
            copy_hT(act, l, 0)
            for j in range(T):
                copy_qk(act, l, 0, j)
                square_qk(act, l, 0, j)
                copy_v(act, l, 0, 0, j)
            copy_hT(act, l, 1)
            for j in range(T):
                for b in range(2):
                    copy_qkT(act, l, 0, 0, j, b)

        def act_attention(act, l, t, u, nxt, after, pair):
            exponential(act, l, t, 0)
            if nxt is not None:
                copy_qk(act, l, nxt, 0)
            exponential(act, l, t, 1)
            if nxt is not None:
                square_qk(act, l, nxt, 0)
                copy_qk(act, l, nxt, 1)
                copy_v(act, l, nxt, 1 - u, 0)
                square_qk(act, l, nxt, 1)
            copy_prob_T(act, l, t, 0)
            if nxt is not None:
                copy_v(act, l, nxt, 1 - u, 1)
            exponential(act, l, t, 2)
            copy_prob_T(act, l, t, 1)
            exponential(act, l, t, 3)
            if after is not None:
                copy_hT(act, l, after)
            copy_oT(act, l, t, 0)
            copy_prob_T(act, l, t, 2)
            if nxt is not None:
                copy_qkT(act, l, nxt, 1 - u, 0, 0)
                copy_qkT(act, l, nxt, 1 - u, 0, 1)
            else:
                act_ffn_front(act, l, 0, 0, psum[:, 0, :])
            copy_prob_T(act, l, t, 3)
            copy_oT(act, l, t, 1)
            if nxt is not None:
                copy_qkT(act, l, nxt, 1 - u, 1, 0)
                copy_qkT(act, l, nxt, 1 - u, 1, 1)

        def inverse_norms(pool, l, t, j):
            i = T * seq(l, t) + j
            pool.wait_ge(guard_ready, i + 1)
            nc.gpsimd.tensor_tensor(inv_norm[:, j], ss_guard[:, j], k.neg_half[:, 0:2 * HEADS], ALU.pow)\
              .then_inc(inv_norm_ready, 1)

        def times_sin(pool, l, t, j):
            settle(pool, raw_ready, START + T * seq(l, t) + j + 1)
            H = HEAD_DIM // 2
            lo, hi = slice(0, H), slice(H, HEAD_DIM)
            nc.gpsimd.tensor_tensor(heads(by_sin[:, j])[:, :, :, lo], heads(raw[:, j])[:, :, :, hi],
                                    table(rot_sin, l, j, lo), ALU.mult)
            nc.gpsimd.tensor_tensor(heads(by_sin[:, j])[:, :, :, hi], heads(raw[:, j])[:, :, :, lo],
                                    table(rot_sin, l, j, hi), ALU.mult).then_inc(by_sin_ready, 1)

        def pool_first(pool, l):
            for j in range(T):
                times_sin(pool, l, 0, j)
                inverse_norms(pool, l, 0, j)

        def pool_attention(pool, l, t, u, nxt, after, pair):
            if nxt is not None:
                times_sin(pool, l, nxt, 0)
                inverse_norms(pool, l, nxt, 0)
                times_sin(pool, l, nxt, 1)
                inverse_norms(pool, l, nxt, 1)
            else:
                pool_ffn_front(pool, l, 0, 0, 0)

        def a_bank(c): return psum[:, 2 * c, :]
        def g_bank(c): return psum[:, 2 * c + 1, :]
        F_OUT, F_HT = psum[:, 6, :], psum[:, 7, :]
        C = HID_CHUNKS

        def group(l, g):
            return FGROUPS * l + g

        def run_ffn(eng, l, work):
            with eng.Fori(0, FGROUPS // 2 - 1) as i:
                work(eng, l, 2 * i, 0, 2 * i + 1, 1, i)
                work(eng, l, 2 * i + 1, 1, 2 * i + 2, 0, i + 1)
            work(eng, l, FGROUPS - 2, 0, FGROUPS - 1, 1, FGROUPS // 2 - 1)
            work(eng, l, FGROUPS - 1, 1, None, None, None)

        def pe_ffn_front(pe, l, n, bank):
            pe.wait_ge(fh_ready, group(l, n) + 1 + FREE)
            for j in range(GT):
                last = nc.tensor.transpose(bank[:, j * P:(j + 1) * P], fh[:, j, :], k.ident[:])
            last.then_inc(fhT_in_psum, 1)

        def pe_ffn(pe, l, g, u, n, un, pair):
            pe.wait_ge(fhT_ready, group(l, g) + 1)
            for c in range(C):
                nc.tensor.matmul(a_bank(c), w_1[:, c, :], fhT[:, u, :], start=True, stop=True)
                nc.tensor.matmul(g_bank(c), w_1[:, C + c, :], fhT[:, u, :], start=True, stop=True).then_inc(up_done, 1)
            if n is not None:
                pe_ffn_front(pe, l, n, F_HT)
            for c in range(C):
                pe.wait_ge(hid_ready, C * group(l, g) + c + 1)
                if c == 0:
                    pe.wait_ge(y_for_attn, SEQS + GS * group(l, g))
                for j in range(GT):
                    last = nc.tensor.matmul(F_OUT[:, j * P:(j + 1) * P], hid[:, c, j * P:(j + 1) * P], w_2[:, c, :],
                                            start=(c == 0 and j == 0), stop=(c == C - 1), skip_group_check=True)
            last.then_inc(ffn_in_psum, 1)

        def dve_ffn_statistics(dve, l, n, un, pair):
            dve.wait_ge(sh_for_ffn[un], 48 * (FGROUPS // 2 * l + pair + 1))
            norm_statistics(k, dve, inner, group(l, n), lambda j: rows_f[:, un, j, :])

        def dve_ffn_normalize(dve, l, n, un):
            norm_apply(k, dve, inner, group(l, n), lambda j: fh[:, j, :], lambda j: rows_f[:, un, j, :], (fh_ready, 1))

        def dve_ffn(dve, l, g, u, n, un, pair):
            if n is not None:
                dve_ffn_statistics(dve, l, n, un, pair)
            for c in range(C):
                dve.wait_ge(gelu_ready, C * group(l, g) + c + 1)
                nc.vector.scalar_tensor_tensor(hid[:, c, :], a_bank(c), b1[:, bass.ts(2 * C * l + c, 1)],
                                               gelu[:, c, :], ALU.add, ALU.mult).then_inc(hid_ready, 1)
                if c == 0 and n is not None:
                    dve_ffn_normalize(dve, l, n, un)
            dve.wait_ge(ffn_in_psum, START + group(l, g) + 1)
            dve.wait_ge(bias_added, group(l, g) + 1)
            rows = y[:, bass.ts(g, GT), :]
            nc.vector.tensor_tensor(rows, F_OUT.rearrange("p (j f) -> p j f", f=DIM), rows,
                                    ALU.add).then_inc(y_for_attn, GS)

        def act_ffn_front(act, l, n, un, bank):
            settle(act, fhT_in_psum, group(l, n) + 1)
            nc.scalar.activation(fhT[:, un, :], bank, ACT.Identity, bias=ln_b[:, bass.ts(l, 1)],
                                 scale=ln_g[:, bass.ts(l, 1)]).then_inc(fhT_ready, 1)

        def act_ffn(act, l, g, u, n, un, pair):
            for c in range(C):
                settle(act, up_done, C * group(l, g) + c + 1)
                nc.scalar.activation(gelu[:, c, :], g_bank(c), ACT.Gelu,
                                     bias=b1[:, bass.ts(2 * C * l + C + c, 1)]).then_inc(gelu_ready, 1)
            if n is not None:
                act_ffn_front(act, l, n, un, F_HT)

        def pool_ffn_front(pool, l, n, un, pair):
            norm_rstd(k, pool, inner, group(l, n))
            settle(pool, sh_for_ffn[un], 48 * (FGROUPS // 2 * l + pair + 1))
            rows = y[:, bass.ts(n, GT), :]
            nc.gpsimd.tensor_tensor(rows, rows, b2[:, bass.ts(l, 1), :].broadcast_to([P, GT, DIM]),
                                    ALU.add).then_inc(bias_added, 1)

        def pool_ffn(pool, l, g, u, n, un, pair):
            if n is not None:
                pool_ffn_front(pool, l, n, un, pair)

        def shift_rows(sp, dst, tile, n, done):
            src = y[:, bass.ts(tile, n), :]
            H = DIM // 2
            sp.dma_start(dst[:, :, 0:H], src[:, :, 0:H]).then_inc(done, 16)
            sp.dma_start(dst[1:P, :, H:DIM], src[0:P - 1, :, H:DIM]).then_inc(done, 16)
            sp.dma_start(dst[0:1, 1::2, H:DIM], src[P - 1:P, 0::2, H:DIM]).then_inc(done, 16)

        with nc.Block() as block:
            @block.sync
            def _(sp):
                sp.wait_ge(edge_zero, 2)
                with sp.Fori(0, LAYERS) as l:
                    sp.wait_ge(attn_in_psum, START + SEQS * l)
                    sp.dma_start(wa[:], k.dram["loc_wa"][bass.ts(l, 1)].rearrange("a p n -> p (a n)"))\
                      .then_inc(wa_loaded, 16)
                    with sp.Fori(0, SEQS // 2) as i:
                        for u in range(2):
                            t = 2 * i + u
                            sp.wait_ge(hT_in_psum, seq(l, t) + 1)
                            sp.wait_ge(y_for_attn, seq(l, t) + 1)
                            shift_rows(sp, rows_a[:, u], t, T, sh_for_attn[u])
                    sp.wait_ge(ffn_in_psum, START + FGROUPS * l)
                    sp.dma_start(wf[:], k.dram["loc_wf"][bass.ts(l, 1)].rearrange("a p n -> p (a n)"))\
                      .then_inc(wf_loaded, 16)
                    with sp.Fori(0, FGROUPS // 2) as i:
                        for u in range(2):
                            g = 2 * i + u
                            sp.wait_ge(fh_ready, group(l, g) + 1)
                            sp.wait_ge(y_for_ffn, START + SEQS * l + GS * (g + 1))
                            shift_rows(sp, rows_f[:, u], g, GT, sh_for_ffn[u])

            @block.tensor
            def _(pe):
                pe.sem_inc(hT_in_psum, FREE)
                pe.sem_inc(attn_in_psum, START)
                pe.sem_inc(ffn_in_psum, START)
                with pe.Fori(0, LAYERS) as l:
                    pe.wait_ge(wa_loaded, 16 * (l + 1))
                    run_attention(pe, l, pe_attention, pe_first)
                    pe.wait_ge(y_for_ffn, START + SEQS * (l + 1))
                    settle(pe, wf_loaded, 16 * (l + 1))
                    run_ffn(pe, l, pe_ffn)

            @block.vector
            def _(dve):
                nc.vector.memset(rows_a[0:1, :, 0, DIM // 2:DIM], 0.0).then_inc(edge_zero, 1)
                nc.vector.memset(rows_f[0:1, :, 0::2, DIM // 2:DIM], 0.0).then_inc(edge_zero, 1)
                dve.sem_inc(fh_ready, FREE)
                dve.sem_inc(y_for_ffn, START)
                for l in range(LAYERS):
                    for tab, const, by in ((rot_cos, cos, scale), (rot_sin, sin, scale_swapped)):
                        nc.vector.tensor_tensor(tab[:, T * l:T * (l + 1)], const[:],
                                                by[:, l:l + 1].broadcast_to([P, T, 2, HEAD_DIM]),
                                                ALU.mult).then_inc(tables_steps, 1)
                dve.wait_ge(tables_steps, 2 * LAYERS)
                with dve.Fori(0, TILES // (4 * GT)) as i:
                    def tile(of, b):
                        return lambda j: of[:, bass.ts(2 * GT * (2 * i + b) + j, 1), :]
                    for b in range(2):
                        norm_statistics(k, dve, outer[b], i, tile(x, b))
                    for b in range(2):
                        norm_apply(k, dve, outer[b], i, tile(y, b), tile(x, b), (y_for_attn, 2 * GT // T))
                with dve.Fori(0, LAYERS) as l:
                    run_attention(dve, l, dve_attention, dve_first)
                    run_ffn(dve, l, dve_ffn)
                dve.wait_ge(y_for_attn, SEQS * (LAYERS + 1))
                with dve.Fori(0, TILES // (2 * GT)) as g:
                    rows = bass.ts(g, 2 * GT)
                    nc.vector.scalar_tensor_tensor(x[:, rows, :], y[:, rows, :], 0.5, x[:, rows, :],
                                                   ALU.mult, ALU.add)

            @block.scalar
            def _(act):
                for started in (raw_ready, qkT_ready, v_ready, oT_ready):
                    act.sem_inc(started, START)
                with act.Fori(0, LAYERS) as l:
                    run_attention(act, l, act_attention, act_first)
                    run_ffn(act, l, act_ffn)

            @block.gpsimd
            def _(pool):
                with pool.Fori(0, TILES // (4 * GT)) as i:
                    for b in range(2):
                        norm_rstd(k, pool, outer[b], i)
                pool.wait_ge(tables_steps, 2 * LAYERS)
                with pool.Fori(0, LAYERS) as l:
                    run_attention(pool, l, pool_attention, pool_first)
                    run_ffn(pool, l, pool_ffn)


def store_stage(k):
    nc = k.nc
    stored = k.sem("stored")
    with nc.Block() as block:
        @block.sync
        def _(sp):
            sp.dma_start(k.dram["out"], k.x[:]).then_inc(stored, 16)
            sp.wait_ge(stored, 16)


STAGES = {
    "moe1": (moe_stage, "moe", "moe1"),
    "l0": (linear_attention_stage, "lin", "lin"),
    "moe2": (moe_stage, "moe", "moe2"),
    "l1a": (local_attention_stage, "loc", "loc1"),
    "mamba": (state_space_stage, "ssm", "ssm"),
    "l1b": (local_attention_stage, "loc", "loc2"),
}


def build(nc, dram, stages):
    with ExitStack() as stack:
        k = Core(nc, dram, stack)
        load_rest = load_stage(k)
        if not stages[0].startswith("moe"):
            load_rest()
        done = set()
        for i, s in enumerate(stages):
            stage, kind, name = STAGES[s]
            if kind in done:
                k.clear(kind)
            done.add(kind)
            stage(k, name)
            if i == 0 and s.startswith("moe"):
                load_rest()
        store_stage(k)


def shape_constants():
    c = {"ident": np.eye(P, dtype=np.float32)}
    expert_of = 2 * np.arange(MOE_CHUNKS)[:, None] + np.arange(P)[None, :] // EXPERT_HID
    c["b_moe_sel"] = (np.arange(EXPERTS)[:, None, None] == expert_of[None]).astype(np.float32)
    c["c_moe_rank"] = np.broadcast_to(EXPERTS - np.arange(EXPERTS, dtype=np.float32), (P, 4, EXPERTS))
    pick = np.zeros((P, 2 * SSM_STATE, P), np.float32)
    for n in range(2 * SSM_STATE):
        pick[32 + n::32, n, :] = 1.0
    c["b_ssm_pick"] = pick.astype(np.float32)
    f = np.float32
    half = np.arange(0, HEAD_DIM, 2, dtype=f)
    inv_freq = f(1.0) / f(10000.0) ** (half / f(HEAD_DIM))
    pos = np.arange(SEQ_LEN, dtype=f)
    angle = pos[:, None] * inv_freq[None, :]
    base = (half + f(0.4 * HEAD_DIM)) / f(1.4 * HEAD_DIM)
    stretch = base[None, :] ** ((pos - SEQ_LEN // 2) / f(WINDOW // 2))[:, None]
    both = np.stack([8 * stretch, 1 / stretch], axis=1)
    cos, sin = np.cos(angle)[:, None] * both, np.sin(angle)[:, None] * both

    def by_tile(v):
        return v.reshape(SEQ_LEN // P, P, 2, HEAD_DIM).swapaxes(0, 1).astype(f)
    c["c_loc_cos"] = by_tile(np.concatenate([cos, cos], axis=-1))
    c["c_loc_sin"] = by_tile(np.concatenate([-sin, sin], axis=-1))
    i, j = np.arange(WINDOW)[:, None], np.arange(WINDOW)[None, :]
    own, before, never = j <= i, j >= i, np.zeros((WINDOW, WINDOW), bool)
    rows = [np.concatenate([own, never], 1), np.concatenate([before, own], 1),
            np.concatenate([own, before], 1), np.concatenate([before, own], 1)]
    pairs = np.concatenate([np.concatenate(rows[0:2]), np.concatenate(rows[2:4])], axis=1)
    c["b_loc_mask"] = np.where(np.tile(pairs, (1, 2)), 0, MASKED).astype(np.float32)
    c["b_loc_ident"] = np.eye(P).astype(np.float32)
    return c


def layouts(i):
    a = {}
    a["x"] = i["L0_attn_x"].reshape(TILES, P, DIM).transpose(1, 0, 2)
    a["c_moe_gate"] = i["L0_ffn_gate_w"].T
    a["c_moe_wg"] = i["L0_ffn_w_gate"].reshape(EXPERTS * EXPERT_HID, DIM).T
    a["c_moe_wu"] = i["L0_ffn_w_up"].reshape(EXPERTS * EXPERT_HID, DIM).T
    a["c_moe_wd"] = i["L0_ffn_w_down"].transpose(0, 2, 1).reshape(MOE_CHUNKS, P, DIM).transpose(1, 0, 2)
    qkv = i["L0_attn_w_qkv"]
    a["lin_w"] = np.concatenate([qkv[:, :, 0:DIM], qkv[:, :, DIM:2 * DIM],
                                 qkv[:, :, 2 * DIM:3 * DIM].transpose(0, 2, 1), i["L0_attn_w_out"]], axis=2)
    a["c_lin_gamma"] = i["L0_attn_gamma"].T
    a["c_lin_beta"] = i["L0_attn_beta"].T
    a["c_lin_bias"] = np.broadcast_to(i["L0_attn_b_out"], (P,) + i["L0_attn_b_out"].shape)
    chunks = SSM_INNER // P

    def by_chunk(v):
        return v.reshape((chunks, P) + v.shape[1:]).swapaxes(0, 1)
    a["c_ssm_win"] = i["L1_attn_W_in"]
    wx = i["L1_attn_W_xproj"]
    low, rows = wx[:, :SSM_RANK], wx[:, SSM_RANK:]
    a["c_ssm_wx"] = by_chunk(np.concatenate([low, np.zeros_like(low), rows, rows, rows], axis=1))
    a["c_ssm_wdt"] = i["L1_attn_W_dt"]
    a["c_ssm_wout"] = by_chunk(i["L1_attn_W_out"])
    a["c_ssm_taps"] = by_chunk(i["L1_attn_conv_k"][:, 0, :].T)
    a["c_ssm_convb"] = by_chunk(i["L1_attn_conv_b"])
    a["c_ssm_bdt"] = by_chunk(i["L1_attn_b_dt"])
    a["c_ssm_d"] = by_chunk(i["L1_attn_D"])
    a["c_ssm_alog"] = by_chunk(i["L1_attn_A_log"])
    layers = i["L1_ffn_wo"].shape[0]
    w_o = i["L1_ffn_wo"].reshape(layers, INNER // P, P, DIM).transpose(0, 2, 1, 3).reshape(layers, P, -1)
    a["loc_wa"] = np.concatenate([i["L1_ffn_wqkv"], w_o], axis=2)
    hid = i["L1_ffn_w2"].shape[1]

    def pad(v, axis):
        width = [(0, 0)] * v.ndim
        width[axis] = (0, HID_CHUNKS * P - hid)
        return np.pad(v, width)
    w1, b1 = i["L1_ffn_w1"], i["L1_ffn_b1"]
    w2 = pad(i["L1_ffn_w2"], 1).reshape(layers, HID_CHUNKS, P, DIM).transpose(0, 2, 1, 3).reshape(layers, P, -1)
    a["loc_wf"] = np.concatenate([pad(w1[..., :hid], 2), pad(w1[..., hid:], 2), w2], axis=2)
    b1 = np.stack([pad(b1[:, :hid], 1), pad(b1[:, hid:], 1)], axis=1)
    a["c_loc_b1"] = b1.reshape(layers * 2 * HID_CHUNKS, P).T
    a["c_loc_b2"] = np.broadcast_to(i["L1_ffn_b2"], (P,) + i["L1_ffn_b2"].shape)
    a["c_loc_lng"] = i["L1_ffn_ln_g"].T
    a["c_loc_lnb"] = i["L1_ffn_ln_b"].T
    scale = np.stack([i["L1_ffn_q_scale"], i["L1_ffn_k_scale"]], axis=1)
    a["c_loc_scale"] = np.broadcast_to(scale, (P,) + scale.shape)
    a["c_loc_scale_swapped"] = np.broadcast_to(np.roll(scale, HEAD_DIM // 2, axis=-1), (P,) + scale.shape)
    return a


ALL = ("moe1", "l0", "moe2", "l1a", "mamba", "l1b")


def program(nc, inputs, stages=ALL):
    arrays = {n: np.ascontiguousarray(a) for n, a in
              (layouts({n: np.asarray(v) for n, v in inputs.items()}) | shape_constants()).items()}
    dram = {n: nc.dram_tensor(n, a.shape, mybir.dt.from_np(a.dtype), kind="ExternalInput").ap()
            for n, a in arrays.items()}
    dram["out"] = nc.dram_tensor("out", (P, TILES, DIM), FP32, kind="ExternalOutput").ap()
    build(nc, dram, stages)
    return arrays


def kernel(**inputs):
    import concourse.bacc as _bacc
    from concourse.bass_utils import run_bass_kernel_spmd as _run

    nc = _bacc.Bacc("TRN2", target_bir_lowering=False, num_devices=1)
    arrays = program(nc, inputs)
    out = _run(nc, [arrays], core_ids=[0]).results[0]["out"]
    return out.transpose(1, 0, 2).reshape(SEQS, SEQ_LEN, DIM)
```
